# Optimizing a Trainium2 kernel written in Bass

```python
import numpy as np
import jax
import jax.numpy as jnp

def _softmax(x, axis=-1):
    return jax.nn.softmax(x, axis=axis)

def _gelu(x):
    return jax.nn.gelu(x, approximate=True)

def _silu(x):
    return jax.nn.silu(x)

def _sigmoid(x):
    return jax.nn.sigmoid(x)

def _layernorm(x, axis=-1, eps=1e-05):
    m = jnp.mean(x, axis=axis, keepdims=True)
    v = jnp.var(x, axis=axis, keepdims=True)
    return (x - m) / jnp.sqrt(v + eps)

def _scatter_add(tgt, idx, src, axis=0):
    return tgt.at[idx].add(src)

def _segment_sum(src, seg, n):
    return jax.ops.segment_sum(src, seg, n)
kernel_name = 'mk_prb_d2_jaxref_r8_30dc58'

def setup_inputs(seed: int=0):
    np.random.seed(seed)
    _w = jnp.asarray

    def _L0_attn_setup():
        import jax, jax.numpy as jnp
        import numpy as np

        def log_g(x):
            return jnp.where(x >= 0, jnp.log(jax.nn.relu(x) + 0.5), -jax.nn.softplus(-x))

        def parallel_scan_log(log_coeffs, log_values):
            a_star = jnp.pad(jnp.cumsum(log_coeffs, axis=1), ((0, 0), (1, 0), (0, 0)))
            log_h = a_star + jax.lax.cumlogsumexp(log_values - a_star, axis=1)
            return jnp.exp(log_h)[:, 1:]
        key = jax.random.key(seed)
        ks = jax.random.split(key, 7)
        B, T, Din, Dh = (4, 512, 128, 128)
        s = 1.0 / np.sqrt(Din)
        return {'x': jax.random.normal(ks[0], (B, T, Din), dtype=jnp.float32), 'W_f': jax.random.uniform(ks[1], (Dh, Din), jnp.float32, -s, s), 'b_f': jax.random.uniform(ks[2], (Dh,), jnp.float32, -s, s), 'W_i': jax.random.uniform(ks[3], (Dh, Din), jnp.float32, -s, s), 'b_i': jax.random.uniform(ks[4], (Dh,), jnp.float32, -s, s), 'W_h': jax.random.uniform(ks[5], (Dh, Din), jnp.float32, -s, s), 'b_h': jax.random.uniform(ks[6], (Dh,), jnp.float32, -s, s)}
    _L0_attn_in = _L0_attn_setup()

    def _L0_ffn_setup():
        import jax, jax.numpy as jnp
        import numpy as np
        FEATURES = 128
        D_IN = 128

        def fp8_gemm_optimized(x, input_scale, kernel, kernel_scale):
            s_in = input_scale[0]
            s_k = kernel_scale[0]
            x_q = (x.astype(jnp.float32) / s_in).astype(jnp.float8_e4m3fn)
            k_q = (kernel.astype(jnp.float32) / s_k).astype(jnp.float8_e4m3fn)
            y = jnp.dot(x_q.astype(jnp.float32), k_q.astype(jnp.float32), preferred_element_type=jnp.float32)
            return y * (s_in * s_k)
        key = jax.random.key(seed)
        kx, kk, kb = jax.random.split(key, 3)
        x = jax.random.normal(kx, (4, 1024, D_IN), dtype=jnp.float32)
        limit = np.sqrt(6.0 / (D_IN + FEATURES)).astype(np.float32)
        kernel = jax.random.uniform(kk, (D_IN, FEATURES), dtype=jnp.float32, minval=-limit, maxval=limit).astype(jnp.bfloat16)
        input_scale = jnp.ones((1,), dtype=jnp.float32)
        kernel_scale = jnp.ones((1,), dtype=jnp.float32)
        bias = jnp.zeros((FEATURES,), dtype=jnp.bfloat16)
        return {'x': x, 'kernel': kernel, 'input_scale': input_scale, 'kernel_scale': kernel_scale, 'bias': bias}
    _L0_ffn_in = _L0_ffn_setup()

    def _L1_attn_setup():
        import jax, jax.numpy as jnp
        import numpy as np
        import math
        D_MODEL = 128
        EXPAND = 2
        D_INNER = EXPAND * D_MODEL
        HEADDIM = 64
        NHEADS = D_INNER // HEADDIM
        D_STATE = 128
        D_CONV = 4
        CHUNK = 128
        SEQLEN = 512
        BATCH = 1
        CONV_DIM = D_INNER + 2 * (2 * D_STATE)
        D_IN_PROJ = 2 * D_INNER + 2 * (2 * D_STATE) + 2 * NHEADS
        EPS = 1e-05

        def silu(x):
            return x * jax.nn.sigmoid(x)

        def segsum_exp(a):
            T = a.shape[-1]
            m1 = jnp.tril(jnp.ones((T, T), bool), -1)
            s = jnp.cumsum(jnp.where(m1, a[..., :, None], 0.0), axis=-2)
            m0 = jnp.tril(jnp.ones((T, T), bool))
            return jnp.where(m0, jnp.exp(jnp.where(m0, s, 0.0)), 0.0)

        def ssd(x, A, B, C, chunk):
            b, L, h, p = x.shape
            c = L // chunk
            x = x.reshape(b, c, chunk, h, p)
            A = A.reshape(b, c, chunk, h).transpose(0, 3, 1, 2)
            B = B.reshape(b, c, chunk, -1)
            C = C.reshape(b, c, chunk, -1)
            A_cs = jnp.cumsum(A, axis=-1)
            Lmat = segsum_exp(A)
            Y_diag = jnp.einsum('bcln,bcsn,bhcls,bcshp->bclhp', C, B, Lmat, x)
            decay_states = jnp.exp(A_cs[..., -1:] - A_cs)
            states = jnp.einsum('bcln,bhcl,bclhp->bchpn', B, decay_states, x)
            states = jnp.concatenate([jnp.zeros_like(states[:, :1]), states], axis=1)
            decay_chunk = segsum_exp(jnp.pad(A_cs[..., -1], ((0, 0), (0, 0), (1, 0))))
            new_states = jnp.einsum('bhzc,bchpn->bzhpn', decay_chunk, states)
            states, final_state = (new_states[:, :-1], new_states[:, -1])
            Y_off = jnp.einsum('bcln,bchpn,bhcl->bclhp', C, states, jnp.exp(A_cs))
            Y = (Y_diag + Y_off).reshape(b, L, h, p)
            return (Y, final_state)
        key = jax.random.key(seed)
        ks = jax.random.split(key, 8)
        s = 0.02
        u = jax.random.normal(ks[0], (BATCH, SEQLEN, D_MODEL), jnp.float32)
        in_proj_w = jax.random.normal(ks[1], (D_IN_PROJ, D_MODEL), jnp.float32) * s
        conv_w = jax.random.normal(ks[2], (CONV_DIM, 1, D_CONV), jnp.float32) * (1.0 / math.sqrt(D_CONV))
        conv_b = jnp.zeros((CONV_DIM,), jnp.float32)
        dt = jnp.exp(jax.random.uniform(ks[3], (NHEADS,)) * (math.log(0.1) - math.log(0.001)) + math.log(0.001))
        dt = jnp.clip(dt, 0.0001)
        dt_bias = dt + jnp.log(-jnp.expm1(-dt))
        A_log = jnp.log(jax.random.uniform(ks[4], (NHEADS,), minval=1.0, maxval=16.0))
        D = jnp.ones((NHEADS,), jnp.float32)
        fc_D_w = jax.random.normal(ks[5], (NHEADS, D_INNER), jnp.float32) * s
        norm_w = jnp.ones((D_INNER,), jnp.float32)
        out_proj_w = jax.random.normal(ks[6], (D_MODEL, D_INNER), jnp.float32) * s
        return dict(u=u, in_proj_w=in_proj_w, conv_w=conv_w, conv_b=conv_b, dt_bias=dt_bias, A_log=A_log, D=D, fc_D_w=fc_D_w, norm_w=norm_w, out_proj_w=out_proj_w)
    _L1_attn_in = _L1_attn_setup()

    def _L1_ffn_setup():
        import jax, jax.numpy as jnp
        import numpy as np
        E = 8
        TOP_K = 2
        D = 128
        F = 256
        B, S = (2, 256)
        key = jax.random.key(seed)
        k0, k1, k2, k3, k4 = jax.random.split(key, 5)
        return {'hidden_states': jax.random.normal(k0, (B, S, D), dtype=jnp.float32), 'gate_w': jax.random.normal(k1, (D, E), dtype=jnp.float32) * 0.02, 'w1': jax.random.normal(k2, (E, D, F), dtype=jnp.float32) * 0.02, 'w2': jax.random.normal(k3, (E, F, D), dtype=jnp.float32) * 0.02, 'w3': jax.random.normal(k4, (E, D, F), dtype=jnp.float32) * 0.02}
    _L1_ffn_in = _L1_ffn_setup()
    _d = {'L0_attn_x': _L0_attn_in['x'], 'L0_attn_W_f': _L0_attn_in['W_f'], 'L0_attn_b_f': _L0_attn_in['b_f'], 'L0_attn_W_i': _L0_attn_in['W_i'], 'L0_attn_b_i': _L0_attn_in['b_i'], 'L0_attn_W_h': _L0_attn_in['W_h'], 'L0_attn_b_h': _L0_attn_in['b_h'], 'L0_ffn_kernel': _L0_ffn_in['kernel'], 'L0_ffn_input_scale': _L0_ffn_in['input_scale'], 'L0_ffn_kernel_scale': _L0_ffn_in['kernel_scale'], 'L0_ffn_bias': _L0_ffn_in['bias'], 'L1_attn_in_proj_w': _L1_attn_in['in_proj_w'], 'L1_attn_conv_w': _L1_attn_in['conv_w'], 'L1_attn_conv_b': _L1_attn_in['conv_b'], 'L1_attn_dt_bias': _L1_attn_in['dt_bias'], 'L1_attn_A_log': _L1_attn_in['A_log'], 'L1_attn_D': _L1_attn_in['D'], 'L1_attn_fc_D_w': _L1_attn_in['fc_D_w'], 'L1_attn_norm_w': _L1_attn_in['norm_w'], 'L1_attn_out_proj_w': _L1_attn_in['out_proj_w'], 'L1_ffn_gate_w': _L1_ffn_in['gate_w'], 'L1_ffn_w1': _L1_ffn_in['w1'], 'L1_ffn_w2': _L1_ffn_in['w2'], 'L1_ffn_w3': _L1_ffn_in['w3']}
    _x0 = _d['L0_attn_x']
    _d['L0_attn_x'] = jax.random.normal(jax.random.fold_in(jax.random.key(seed), 1), (8, 512, 128), dtype=_x0.dtype)
    del _x0
    return _d

def reference(L0_attn_x, L0_attn_W_f, L0_attn_b_f, L0_attn_W_i, L0_attn_b_i, L0_attn_W_h, L0_attn_b_h, L0_ffn_kernel, L0_ffn_input_scale, L0_ffn_kernel_scale, L0_ffn_bias, L1_attn_in_proj_w, L1_attn_conv_w, L1_attn_conv_b, L1_attn_dt_bias, L1_attn_A_log, L1_attn_D, L1_attn_fc_D_w, L1_attn_norm_w, L1_attn_out_proj_w, L1_ffn_gate_w, L1_ffn_w1, L1_ffn_w2, L1_ffn_w3):

    def _L0_attn_ref(x, W_f, b_f, W_i, b_i, W_h, b_h):
        import jax, jax.numpy as jnp
        import numpy as np

        def log_g(x):
            return jnp.where(x >= 0, jnp.log(jax.nn.relu(x) + 0.5), -jax.nn.softplus(-x))

        def parallel_scan_log(log_coeffs, log_values):
            a_star = jnp.pad(jnp.cumsum(log_coeffs, axis=1), ((0, 0), (1, 0), (0, 0)))
            log_h = a_star + jax.lax.cumlogsumexp(log_values - a_star, axis=1)
            return jnp.exp(log_h)[:, 1:]
        B = x.shape[0]
        Dh = W_f.shape[0]
        f_pre = jnp.einsum('btd,hd->bth', x, W_f) + b_f
        i_pre = jnp.einsum('btd,hd->bth', x, W_i) + b_i
        h_pre = jnp.einsum('btd,hd->bth', x, W_h) + b_h
        diff = jax.nn.softplus(-f_pre) - jax.nn.softplus(-i_pre)
        log_f = -jax.nn.softplus(diff)
        log_i = -jax.nn.softplus(-diff)
        log_h0 = jnp.zeros((B, 1, Dh), dtype=x.dtype)
        log_tilde_h = log_g(h_pre)
        log_values = jnp.concatenate([log_h0, log_i + log_tilde_h], axis=1)
        return parallel_scan_log(log_f, log_values)

    def _L0_ffn_ref(x, kernel, input_scale, kernel_scale, bias):
        import jax, jax.numpy as jnp
        import numpy as np
        FEATURES = 128
        D_IN = 128

        def fp8_gemm_optimized(x, input_scale, kernel, kernel_scale):
            s_in = input_scale[0]
            s_k = kernel_scale[0]
            x_q = (x.astype(jnp.float32) / s_in).astype(jnp.float8_e4m3fn)
            k_q = (kernel.astype(jnp.float32) / s_k).astype(jnp.float8_e4m3fn)
            y = jnp.dot(x_q.astype(jnp.float32), k_q.astype(jnp.float32), preferred_element_type=jnp.float32)
            return y * (s_in * s_k)
        dtype = jnp.bfloat16
        x = x.astype(dtype)
        orig_shape = x.shape
        x2 = x.reshape(-1, x.shape[-1])
        y = fp8_gemm_optimized(x2, input_scale, kernel, kernel_scale)
        y = y.astype(dtype) + bias
        return y.reshape(orig_shape[:-1] + (FEATURES,))

    def _L1_attn_ref(u, in_proj_w, conv_w, conv_b, dt_bias, A_log, D, fc_D_w, norm_w, out_proj_w):
        import jax, jax.numpy as jnp
        import numpy as np
        import math
        D_MODEL = 128
        EXPAND = 2
        D_INNER = EXPAND * D_MODEL
        HEADDIM = 64
        NHEADS = D_INNER // HEADDIM
        D_STATE = 128
        D_CONV = 4
        CHUNK = 128
        SEQLEN = 512
        BATCH = 1
        CONV_DIM = D_INNER + 2 * (2 * D_STATE)
        D_IN_PROJ = 2 * D_INNER + 2 * (2 * D_STATE) + 2 * NHEADS
        EPS = 1e-05

        def silu(x):
            return x * jax.nn.sigmoid(x)

        def segsum_exp(a):
            T = a.shape[-1]
            m1 = jnp.tril(jnp.ones((T, T), bool), -1)
            s = jnp.cumsum(jnp.where(m1, a[..., :, None], 0.0), axis=-2)
            m0 = jnp.tril(jnp.ones((T, T), bool))
            return jnp.where(m0, jnp.exp(jnp.where(m0, s, 0.0)), 0.0)

        def ssd(x, A, B, C, chunk):
            b, L, h, p = x.shape
            c = L // chunk
            x = x.reshape(b, c, chunk, h, p)
            A = A.reshape(b, c, chunk, h).transpose(0, 3, 1, 2)
            B = B.reshape(b, c, chunk, -1)
            C = C.reshape(b, c, chunk, -1)
            A_cs = jnp.cumsum(A, axis=-1)
            Lmat = segsum_exp(A)
            Y_diag = jnp.einsum('bcln,bcsn,bhcls,bcshp->bclhp', C, B, Lmat, x)
            decay_states = jnp.exp(A_cs[..., -1:] - A_cs)
            states = jnp.einsum('bcln,bhcl,bclhp->bchpn', B, decay_states, x)
            states = jnp.concatenate([jnp.zeros_like(states[:, :1]), states], axis=1)
            decay_chunk = segsum_exp(jnp.pad(A_cs[..., -1], ((0, 0), (0, 0), (1, 0))))
            new_states = jnp.einsum('bhzc,bchpn->bzhpn', decay_chunk, states)
            states, final_state = (new_states[:, :-1], new_states[:, -1])
            Y_off = jnp.einsum('bcln,bchpn,bhcl->bclhp', C, states, jnp.exp(A_cs))
            Y = (Y_diag + Y_off).reshape(b, L, h, p)
            return (Y, final_state)
        b, l, _ = u.shape
        zxbcdt = u @ in_proj_w.T
        z = zxbcdt[..., :D_INNER]
        xBC = zxbcdt[..., D_INNER:D_INNER + CONV_DIM]
        dt = zxbcdt[..., D_INNER + CONV_DIM:]
        dt = jnp.concatenate([dt[..., :NHEADS], jnp.flip(dt[..., NHEADS:], axis=1)], axis=0)
        dt = jax.nn.softplus(dt + dt_bias)
        xc = jnp.transpose(xBC, (0, 2, 1))
        xc = jax.lax.conv_general_dilated(xc, conv_w, (1,), [(D_CONV - 1, 0)], feature_group_count=CONV_DIM, dimension_numbers=('NCH', 'OIH', 'NCH'))
        xc = xc + conv_b[None, :, None]
        xBC = silu(jnp.transpose(xc, (0, 2, 1)))
        x = xBC[..., :D_INNER]
        BC = xBC[..., D_INNER:]
        x_og = x
        x2 = jnp.concatenate([x, jnp.flip(x, 1)], axis=0)
        BC = jnp.concatenate([BC[..., :2 * D_STATE], jnp.flip(BC[..., 2 * D_STATE:], 1)], axis=0)
        B = BC[..., :D_STATE]
        C = BC[..., D_STATE:]
        xh = x2.reshape(2 * b, l, NHEADS, HEADDIM)
        A = -jnp.exp(A_log)
        Y, final_state = ssd(xh * dt[..., None], A * dt, B, C, CHUNK)
        y = Y + xh * D[:, None]
        y = y.reshape(2 * b, l, D_INNER)
        y = jnp.concatenate([jnp.zeros_like(y[:, :1]), y[:, :-1]], axis=1)
        y_fw, y_bw = (y[:b], jnp.flip(y[b:], 1))
        fd = x_og @ fc_D_w.T + D
        y = y_fw + y_bw + x_og * jnp.repeat(fd, HEADDIM, axis=-1)
        yg = y * silu(z)
        yn = yg * jax.lax.rsqrt(jnp.mean(yg * yg, axis=-1, keepdims=True) + EPS) * norm_w
        return yn @ out_proj_w.T

    def _L1_ffn_ref(hidden_states, gate_w, w1, w2, w3):
        import jax, jax.numpy as jnp
        import numpy as np
        E = 8
        TOP_K = 2
        D = 128
        F = 256
        B, S = (2, 256)
        b, s, d = hidden_states.shape
        x = hidden_states.reshape(-1, d)
        router_logits = x @ gate_w
        probs = jax.nn.softmax(router_logits, axis=-1)
        top_w, top_i = jax.lax.top_k(probs, TOP_K)
        top_w = top_w / jnp.sum(top_w, axis=-1, keepdims=True)
        out = jnp.zeros_like(x)
        for e in range(E):
            w_e = jnp.sum(jnp.where(top_i == e, top_w, 0.0), axis=-1)
            act = jax.nn.silu(x @ w1[e]) * (x @ w3[e])
            out = out + act @ w2[e] * w_e[:, None]
        return out.reshape(b, s, d)
    x = L0_attn_x
    xn = _layernorm(x, axis=-1)
    x = x + _L0_attn_ref(xn, L0_attn_W_f, L0_attn_b_f, L0_attn_W_i, L0_attn_b_i, L0_attn_W_h, L0_attn_b_h) + _L0_ffn_ref(xn, L0_ffn_kernel, L0_ffn_input_scale, L0_ffn_kernel_scale, L0_ffn_bias)
    xn = _layernorm(x, axis=-1)
    x = x + _L1_attn_ref(xn, L1_attn_in_proj_w, L1_attn_conv_w, L1_attn_conv_b, L1_attn_dt_bias, L1_attn_A_log, L1_attn_D, L1_attn_fc_D_w, L1_attn_norm_w, L1_attn_out_proj_w) + _L1_ffn_ref(xn, L1_ffn_gate_w, L1_ffn_w1, L1_ffn_w2, L1_ffn_w3)
    return x

_drawn_inputs = setup_inputs


def setup_inputs(seed=0):
    import zlib

    import numpy as np

    out = dict(_drawn_inputs(seed))
    spreads = {'L0_ffn_bias': (0.0, 0.1),
     'L1_attn_conv_b': (0.0, 0.1),
     'L1_attn_D': (1.0, 0.6),
     'L1_attn_norm_w': (1.0, 0.6)}
    factors = {'L0_attn_b_f': 8.0,
     'L0_attn_b_i': 8.0,
     'L1_attn_dt_bias': 64.0,
     'L1_attn_A_log': 8.0,
     'L1_attn_fc_D_w': 45.499,
     'L1_ffn_gate_w': 8.0,
     'L1_ffn_w1': 8.0,
     'L1_ffn_w2': 8.0,
     'L1_ffn_w3': 8.0}
    for name, (base, spread) in spreads.items():
        noise = np.random.default_rng([zlib.crc32(name.encode()), seed]).standard_normal(out[name].shape)
        drawn = base * np.exp(spread * noise) if base else spread * noise
        out[name] = jnp.asarray(drawn.astype(out[name].dtype))
    for name, factor in factors.items():
        out[name] = (out[name] * factor).astype(out[name].dtype)
    return out
```

```python
from contextlib import ExitStack

import numpy as np
import concourse.bass as bass
from concourse import mybir

P = 128
B, S, D = 8, 512, 128
NT = S // P
TILES = B * NT
HEADS, HDIM = 4, 64
INNER = HEADS * HDIM
CT = INNER // P
TAPS = 4
E, F = 8, 256
TOP = 2
SLOT_TILES = (B * S * TOP + E * (P - 1)) // P + 1
EPS = 1e-5
CLAMP = 40.0
FP8_MIN = 2.0 ** -6
FP8_MAGIC = 1.5 * 2.0 ** 20
STEPS = 2 * NT
PAY = D + 4
DEEP = 4

F32, BF16, U32, I32 = mybir.dt.float32, mybir.dt.bfloat16, mybir.dt.uint32, mybir.dt.int32
ALU, ACT, AX = mybir.AluOpType, mybir.ActivationFunctionType, mybir.AxisListType

XA, XB, BF_, CF_, BB_, CB_ = range(6)
CONV_ORDER = [XA, XB, BF_, BB_, CF_, CB_]
IDENT, AFTER, BEFORE, UPTO, FROM, ONES = range(6)


def shape_constants():
    k = np.arange(P)[:, None]
    j = np.arange(P)[None, :]
    return np.stack([k == j, k > j, k < j, k <= j, k >= j, k + j >= 0], 1).astype(np.float32)


ROUTE_GAP, ROUTE_BOTH, ROUTE_ALL = 14, 15, 43
EX_LAST = (SLOT_TILES - 1) // DEEP * DEEP


def unit(u):
    d, k = u % 2, u // 2
    return d, (k if d == 0 else NT - 1 - k), k


def build(nc, x, w_gates, b_gates, w_fp8, s_in, s_w, b_fp8, w_inT, conv_w, conv_b, dt_bias, a_log, d_skip,
          w_fd, norm_w, w_outT, gate_w, w13, w2, consts, iotas, row_ids, spare_ids, slots_d, pairs_d, rows_d, out, stop=0):
    with ExitStack() as ctx:
        def sb(name, shape, dt=F32):
            return ctx.enter_context(nc.sbuf_tensor(name, shape, dt))

        def sem(name):
            return ctx.enter_context(nc.semaphore(name))

        bank = [ctx.enter_context(nc.psum_tensor(f"bank{i}", [P, 512], F32)) for i in range(8)]
        conv_ps = bank[0:2]
        seg_ps = bank[2]
        gram_ps = bank[3]
        y_ps = bank[4]
        state_ps = bank[5]
        tm_ps = [bank[5], bank[2], bank[3], bank[4]]
        l0a_ps, l0b_ps = bank[6], bank[7]

        x_all = sb("x_all", [P, TILES, D])
        logits = sb("logits", [P, TILES, E])
        cst = sb("cst", [P, 6, P])
        ident, ones = cst[:, IDENT, :], cst[:, ONES, :]
        wg = sb("wg", [P, 3, P])
        bg = sb("bg", [P, 3])
        kq = sb("kq", [P, P], BF16)
        kraw = sb("kraw", [P, P], BF16)
        b8 = sb("b8", [P, 1], BF16)
        scales = sb("scales", [P, 2])
        iscale = sb("iscale", [P, 2])
        sprod = sb("sprod", [P, 1])
        w_in = sb("w_in", [P, 1032])
        taps = sb("taps", [P, TAPS, 768])
        cb = sb("cb", [P, 6])
        dtb = sb("dtb", [P, 2 * HEADS])
        a_neg = sb("a_neg", [P, 2 * HEADS])
        dcol = sb("dcol", [P, CT])
        wfd = sb("wfd", [P, CT, INNER])
        nw = sb("nw", [P, CT])
        wout = sb("wout", [P, CT, D])
        gate = sb("gate", [P, E])
        zero16 = sb("zero16", [P, 512], BF16)
        half_neg = sb("half_neg", [P, NT])
        eps = sb("eps", [P, NT])
        carrier = sb("carrier", [P, 1])
        carrier_p = sb("carrier_p", [P, 1])
        st = sb("st", [P, NT, 6])
        mv = sb("mv", [P, NT, 2])
        vpe = sb("vpe", [P, NT])
        rstd = sb("rstd", [P, NT])
        xn = sb("xn", [P, NT, D])
        xnT = sb("xnT", [P, S])
        work = sb("work", [P, 12 * S])
        pre, cl, ex, lgt = (work[:, n * 3 * S:(n + 1) * 3 * S].rearrange("p (g s) -> p g s", g=3) for n in range(4))
        diff = sb("diff", [P, S])
        cld = sb("cld", [P, S])
        val = sb("val", [P, S])
        hT = sb("hT", [P, S])
        xq16 = sb("xq16", [P, S], BF16)
        xqs = sb("xqs", [P, S])
        magic = sb("magic", [P, S])
        xqr = sb("xqr", [P, S])
        xq = sb("xq", [P, S], BF16)
        y16 = sb("y16", [P, S], BF16)
        y16b = sb("y16b", [P, S], BF16)
        uT = sb("uT", [P, TAPS - 1 + S])
        xs = sb("xs", [P, CT, S + 2])
        bc = sb("bc", [P, 4, S])
        zs = sb("zs", [P, CT, S])
        xtm = sb("xtm", [P, NT, INNER])
        btm = sb("btm", [P, 2, NT, P])
        dtr = sb("dtr", [P, NT, 2 * HEADS])
        dtc = sb("dtc", [P, NT, 2 * HEADS])
        dt = sb("dt", [P, NT, 2 * HEADS])
        adt = sb("adt", [P, NT, 2 * HEADS])
        ea = sb("ea", [P, 4, NT, HEADS])
        xdt = sb("xdt", [P, 2, NT, INNER])
        gm = sb("gm", [P, 2, NT, P])
        seg = sb("seg", [P, 2, HEADS, P])
        dec = sb("dec", [P, 2, HEADS, P])
        mm_ = sb("mm_", [P, 2, HEADS, P])
        xdd = sb("xdd", [P, 2, INNER])
        state = sb("state", [P, 2, INNER])
        stt_ = sb("stt_", [P, INNER])
        yo = sb("yo", [P, INNER])
        yt = sb("yt", [P, 2, INNER])
        nb = sb("nb", [P, CT, S])
        skip = sb("skip", [P, CT, S])
        yg = sb("yg", [P, CT, S])
        ysum = sb("ysum", [P, CT, S])
        sq = sb("sq", [P, CT, S])
        ms = sb("ms", [P, NT])
        rms = sb("rms", [P, NT])

        ws1 = sb("ws1", [P, E, 2 * F])
        ws2 = sb("ws2", [P, E, CT, D])
        iota = sb("iota", [P, SLOT_TILES])
        rev = sb("rev", [P, E])
        taken = [0]

        def reuse(n):
            taken[0] += n
            return work[:, taken[0] - n:taken[0]]

        def te(x):
            return x.rearrange("p (t e) -> p t e", e=E)

        stage = reuse(2 * TOP * NT * PAY).rearrange("p (q k t w) -> p q k t w", q=2, k=TOP, t=NT)
        oh, score, both, pos = (te(reuse(TILES * E)) for _ in range(4))
        picks = [te(reuse(TILES * E)) for _ in range(TOP)]
        totals, running = (reuse(TILES * E).rearrange("p (e t) -> p e t", e=E) for _ in range(2))
        begun = te(reuse(SLOT_TILES * E))
        best = sb("best", [P, TOP, TILES])
        low = sb("low", [P, TILES])
        weight = sb("weight", [P, TOP, TILES])
        count_i = sb("count_i", [P, E], I32)
        need = sb("need", [P, E])
        upto_e = sb("upto_e", [P, E])
        base = sb("base", [P, E])
        posf = sb("posf", [P, TOP, TILES])
        slot = sb("slot", [P, TOP, TILES], U32)
        tile_ef = sb("tile_ef", [P, SLOT_TILES])
        tile_e = sb("tile_e", [P, SLOT_TILES], I32)
        ids = sb("ids", [P, TOP, TILES, 1], I32)
        spare = sb("spare", [P, PAY])
        xe = sb("xe", [P, DEEP, PAY])
        xeT = sb("xeT", [P, 2, P])
        to_row = sb("to_row", [P, DEEP, 1], U32)
        sg = sb("sg", [P, 2, F])
        hid = sb("hid", [P, 2, F])
        hidT = sb("hidT", [P, 2, F])
        ye = sb("ye", [P, DEEP, D])
        pair = xdt[:].rearrange("p d c (a w) -> p (d c a) w", w=D).rearrange("p (q t k) w -> p q t k w", q=2, k=TOP)

        ld_x, ld_a, ld_b, out_st = sem("ld_x"), sem("ld_a"), sem("ld_b"), sem("out_st")
        prep_v, prep_p, prep_s = sem("prep_v"), sem("prep_p"), sem("prep_s")
        bst, bag, var_e, rs = sem("bst"), sem("bag"), sem("var_e"), sem("rs")
        xn_r, tr1, xnT_r, pre_mm, pre_r = sem("xn_r"), sem("tr1"), sem("xnT_r"), sem("pre_mm"), sem("pre_r")
        cl_r, ex_r, ln_r, sp_r, df_r = sem("cl_r"), sem("ex_r"), sem("ln_r"), sem("sp_r"), sem("df_r")
        lh_r, cd_r, ed_r, ld_r, spd_r, li_r, gt_r = (sem(n) for n in ("lh_r", "cd_r", "ed_r", "ld_r", "spd_r", "li_r", "gt_r"))
        g_r, v_r, h_r = sem("g_r"), sem("v_r"), sem("h_r")
        q_v, q_p, ffn_mm, y_r, yb_r, hs_r = (sem(n) for n in ("q_v", "q_p", "ffn_mm", "y_r", "yb_r", "hs_r"))
        trh, x1_r, xn2_r, tr2, uT_r, lg_mm, lg_r = (sem(n) for n in ("trh", "x1_r", "xn2_r", "tr2", "uT_r", "lg_mm", "lg_r"))
        dt_mm, dt_v, dt_s, ea_mm, ea_r = (sem(n) for n in ("dt_mm", "dt_v", "dt_s", "ea_mm", "ea_r"))
        cv_mm, cv_r, tm_mm, tm_r, g_mm, gm_r, fd_mm, sk_r, nb_r, xdt_r = (
            sem(n) for n in ("cv_mm", "cv_r", "tm_mm", "tm_r", "g_mm", "gm_r", "fd_mm", "sk_r", "nb_r", "xdt_r"))
        seg_r, seg_mm, dec_r, m_r, xdd_r, yd_mm, st_mm, stp_r, st_r, yo_r, yt_r, sh_mm = (
            sem(n) for n in ("seg_r", "seg_mm", "dec_r", "m_r", "xdd_r", "yd_mm", "st_mm", "stp_r", "st_r", "yo_r", "yt_r", "sh_mm"))
        nbs_r, ya_r, yg_r, sq_r, ms_mm, ms_r, rms_r, pj_mm, acc_r = (
            sem(n) for n in ("nbs_r", "ya_r", "yg_r", "sq_r", "ms_mm", "ms_r", "rms_r", "pj_mm", "acc_r"))

        ld_w, ld_t, slots_zero, rows_st, ids_in = (
            sem(n) for n in ("ld_w", "ld_t", "slots_zero", "rows_st", "ids_in"))
        ld_stage, scattered, pair_in = ([sem(f"{n}{q}") for q in range(2)] for n in ("ld_stage", "scattered", "pair_in"))
        xe_in, y_out = ([sem(f"{n}{q}") for q in range(DEEP)] for n in ("xe_in", "y_out"))
        route, gap_exp, rank_mm = sem("route"), sem("gap_exp"), sem("rank_mm")
        xeT_mm, xeT_r, row_r, h_mm, sg_r, hid_r, hidT_mm, hidT_r, y_mm, ye_r = (
            sem(n) for n in ("xeT_mm", "xeT_r", "row_r", "h_mm", "sg_r", "hid_r", "hidT_mm", "hidT_r", "y_mm",
                             "ye_r"))
        carried = sem("carried")
        sum1, sum2, spare_r = sem("sum1"), sem("sum2"), sem("spare_r")

        per_batch = {1: [dt_mm, pj_mm, ea_mm, ea_r, ms_mm, ms_r, rms_r],
                     2: [dt_s, g_mm, gm_r, fd_mm, sk_r, nb_r, xdt_r, nbs_r, ya_r, yg_r, sq_r],
                     4: [tm_mm, tm_r, stp_r, acc_r],
                     5: [dt_v],
                     6: [xdd_r, st_mm, st_r, yo_r],
                     8: [cv_mm, cv_r, seg_r, seg_mm, dec_r, m_r, yd_mm, yt_r, sh_mm]}

        block = ctx.enter_context(nc.Block())

        loads_a = [(cst[:], consts), (wg[:], w_gates), (bg[:], b_gates), (kraw[:], w_fp8), (b8[:], b_fp8),
                   (scales[:, 0:1], s_in.partition_broadcast(P)), (scales[:, 1:2], s_w.partition_broadcast(P))]
        loads_b = [(w_in[:], w_inT), (taps[:], conv_w.partition_broadcast(P)), (cb[:], conv_b),
                   (dtb[:, 0:HEADS], dt_bias.partition_broadcast(P)), (dtb[:, HEADS:], dt_bias.partition_broadcast(P)),
                   (a_neg[:, 0:HEADS], a_log.partition_broadcast(P)), (a_neg[:, HEADS:], a_log.partition_broadcast(P)),
                   (dcol[:], d_skip), (wfd[:], w_fd), (nw[:], norm_w), (wout[:], w_outT), (gate[:], gate_w)]
        wc = taps

        @block.sync
        def _(sp):
            def store(b):
                sp.wait_ge(sum2, NT * (b + 1))
                sp.dma_start(out[b].rearrange("(t p) d -> p t d", p=P),
                             x_all[:, NT * b:NT * b + NT, :]).then_inc(out_st, 16)

            for t, (dst, src) in enumerate(loads_a):
                sp.dma_start(dst, src).then_inc(ld_a, 16)
            for b in range(B):
                sp.dma_start(x_all[:, NT * b:NT * b + NT, :], x[b].rearrange("(t p) d -> p t d", p=P)).then_inc(ld_x, 16)
                if b == 0:
                    for dst, src in loads_b:
                        sp.dma_start(dst, src).then_inc(ld_b, 16)
            sp.dma_start(ws1[:], w13).then_inc(ld_w, 16)
            sp.dma_start(ws2[:], w2).then_inc(ld_w, 16)
            sp.wait_ge(spare_r, 1)
            sp.dma_start(spare[:, D:D + 1].bitcast(I32), spare_ids).then_inc(ld_t, 16)
            sp.dma_start(ids[:, :, :, 0], row_ids).then_inc(ld_t, 16)
            sp.dma_start(iota[:], iotas).then_inc(ld_t, 16)
            sp.wait_ge(ld_t, 48)
            sp.dma_start(slots_d.rearrange("(t p) w -> p t w", p=P),
                         spare[:].unsqueeze(1).to_broadcast([P, SLOT_TILES, PAY])).then_inc(slots_zero, 16)
            with sp.Fori(0, B) as b:
                sp.wait_ge(xn2_r, 4 * b + 4)
                sp.dma_start(rows_d[bass.ds(b * NT, NT), :, :].rearrange("t p d -> p t d"), xn[:]).then_inc(rows_st, 16)
            sp.wait_ge(rows_st, 16 * B)
            for b in range(B):
                if b >= 2:
                    sp.wait_ge(scattered[b % 2], 16 * NT * TOP * (b // 2))
                for k in range(TOP):
                    sp.dma_start(stage[:, b % 2, k, :, 0:D],
                                 rows_d[b * NT:(b + 1) * NT].rearrange("t p d -> p t d")).then_inc(ld_stage[b % 2], 16)
            for one in scattered:
                sp.wait_ge(one, 16 * NT * TOP * B // 2)
            slot_tiles = slots_d.rearrange("(t p) w -> t p w", p=P)

            def load_tile(i, n, free):
                if free:
                    sp.wait_ge(xeT_mm, i - DEEP + 1)
                    sp.wait_ge(row_r, i - DEEP + 1)
                sp.dma_start(xe[:, n, :], slot_tiles[bass.ds(i, 1)].rearrange("a p w -> p (a w)")).then_inc(xe_in[n], 16)

            for n in range(DEEP):
                load_tile(n, n, False)
            with sp.Fori(1, SLOT_TILES // DEEP) as group:
                for n in range(DEEP):
                    load_tile(group * DEEP + n, n, True)
            for one in y_out:
                sp.wait_ge(one, 16 * SLOT_TILES // DEEP)
            by_token = pairs_d[0:B * S * TOP].rearrange("(g t p k) d -> g p t k d", p=P, k=TOP, t=NT)
            for b in range(B):
                if b >= 2:
                    sp.wait_ge(sum2, NT * (b - 1))
                sp.dma_start(pair[:, b % 2], by_token[b]).then_inc(pair_in[b % 2], 16)
                if b >= 1:
                    store(b - 1)
            store(B - 1)
            sp.wait_ge(out_st, 16 * B)

        @block.tensor
        def _(pe):
            def l0_transpose(b):
                pe.wait_ge(xn_r, 4 * b + 4)
                if not (isinstance(b, int) and b == 0):
                    pe.wait_ge(uT_r, b)
                for j in range(NT):
                    mm = nc.tensor.transpose(l0a_ps[:, j * P:(j + 1) * P], xn[:, j, :], ident)
                mm.then_inc(tr1, 1)

            def l0_gates(b, g):
                pe.wait_ge(xnT_r, b + 1)
                ps = (l0b_ps, l0a_ps, l0b_ps)[g]
                if g == 0 and not (isinstance(b, int) and b == 0):
                    pe.wait_ge(lg_r, b)
                if g == 2:
                    pe.wait_ge(pre_r, 3 * b + 1)
                nc.tensor.matmul(ps[:], wg[:, g, :], xnT[:], start=True, stop=True).then_inc(pre_mm, 1)

            def l0_ffn(b):
                pe.wait_ge(pre_r, 3 * b + 2)
                pe.wait_ge(q_p, 2 * b + 2)
                nc.tensor.matmul(l0a_ps[:], kq[:], xq[:], start=True, stop=True).then_inc(ffn_mm, 1)

            def l0_back(b):
                pe.wait_ge(pre_r, 3 * b + 3)
                pe.wait_ge(hs_r, b + 1)
                for j in range(NT):
                    mm = nc.tensor.transpose(l0b_ps[:, j * P:(j + 1) * P], hT[:, j * P:(j + 1) * P], ident)
                mm.then_inc(trh, 1)

            def l0_u(b):
                pe.wait_ge(y_r, b + 1)
                pe.wait_ge(xn2_r, 4 * b + 4)
                for j in range(NT):
                    mm = nc.tensor.transpose(l0a_ps[:, j * P:(j + 1) * P], xn[:, j, :], ident)
                mm.then_inc(tr2, 1)

            def l0_logits(b):
                pe.wait_ge(uT_r, b + 1)
                pe.wait_ge(x1_r, b + 1)
                for j in range(NT):
                    mm = nc.tensor.matmul(l0b_ps[:, j * E:(j + 1) * E], uT[:, 3 + j * P:3 + (j + 1) * P], gate[:],
                                          start=True, stop=True)
                mm.then_inc(lg_mm, 1)

            def mx_dt(b):
                pe.wait_ge(uT_r, b)
                pe.wait_ge(gm_r, 2 * b)
                for j in range(NT):
                    mm = nc.tensor.matmul(gram_ps[:, j * 8:(j + 1) * 8], uT[:, 3 + j * P:3 + (j + 1) * P],
                                          w_in[:, 1024:1032], start=True, stop=True)
                mm.then_inc(dt_mm, 1)

            def mx_conv(b, n):
                if n >= 2:
                    pe.wait_ge(cv_r, 8 * b + n - 1)
                else:
                    pe.wait_ge(ya_r, 2 * b - 1 + n)
                ps = conv_ps[n % 2]
                if n < 6:
                    q = CONV_ORDER[n]
                    for k in range(TAPS):
                        mm = nc.tensor.matmul(ps[:], wc[:, k, q * P:(q + 1) * P], uT[:, k:k + S],
                                              start=(k == 0), stop=(k == TAPS - 1))
                else:
                    mm = nc.tensor.matmul(ps[:], w_in[:, (n - 6) * P:(n - 5) * P], uT[:, 3:3 + S], start=True, stop=True)
                mm.then_inc(cv_mm, 1)

            def mx_timemajor(b, n):
                pe.wait_ge(cv_r, 8 * b + 4)
                pe.wait_ge(*((ms_r, b), (acc_r, 4 * b), (sk_r, 2 * b + 1), (sk_r, 2 * b + 2))[n])
                for q in range(4):
                    if n < 2:
                        c = 2 * n + q // 2
                        src = xs[:, q % 2, 1 + c * P:1 + (c + 1) * P]
                    else:
                        src = bc[:, 2 * (n - 2), q * P:(q + 1) * P]
                    mm = nc.tensor.transpose(tm_ps[n][:, q * P:(q + 1) * P], src, ident)
                mm.then_inc(tm_mm, 1)

            def mx_gram(b, d):
                pe.wait_ge(cv_r, 8 * b + 6)
                pe.wait_ge(tm_r, 4 * b + 3 + d)
                ps = (bank[3], bank[4])[d]
                for c in range(NT):
                    mm = nc.tensor.matmul(ps[:, c * P:(c + 1) * P], bc[:, 2 * d, c * P:(c + 1) * P],
                                          bc[:, 2 * d + 1, c * P:(c + 1) * P], start=True, stop=True)
                mm.then_inc(g_mm, 1)

            def mx_sums(b):
                pe.wait_ge(dt_v, 5 * b + 5)
                pe.wait_ge(tm_r, 4 * b + 1)
                nc.tensor.matmul(state_ps[:, 0:16], cst[:, UPTO, :], adt[:, :, 0:HEADS], start=True, stop=True)
                nc.tensor.matmul(state_ps[:, 16:32], cst[:, FROM, :], adt[:, :, HEADS:], start=True, stop=True)
                nc.tensor.matmul(state_ps[:, 32:48], ones, adt[:, :, 0:HEADS], start=True, stop=True)
                nc.tensor.matmul(state_ps[:, 48:64], ones, adt[:, :, HEADS:], start=True, stop=True).then_inc(ea_mm, 1)

            def mx_skip(b, ct):
                pe.wait_ge(*((dt_v, 5 * b + 1), (yt_r, 8 * b))[ct])
                if ct == 0:
                    pe.wait_ge(cv_r, 8 * b + 2)
                for k in range(CT):
                    mm = nc.tensor.matmul((bank[3], bank[4])[ct][:], wfd[:, k, ct * P:(ct + 1) * P], xs[:, k, 1:S + 1],
                                          start=(k == 0), stop=(k == CT - 1))
                mm.then_inc(fd_mm, 1)

            def mx_clear(b, ct):
                pe.wait_ge(cv_r, 8 * b + 7 + ct)
                nc.tensor.matmul(conv_ps[ct][:], zero16[:, 0:P], zero16[:], start=True, stop=False, skip_group_check=True)

            def mx_segments(b, u):
                d = unit(u)[0]
                pe.wait_ge(seg_r, 8 * b + u + 1)
                if u == 0:
                    pe.wait_ge(tm_r, 4 * b + 2)
                else:
                    pe.wait_ge(dec_r, 8 * b + u)
                nc.tensor.matmul(seg_ps[:], cst[:, (AFTER, BEFORE)[d], :], seg[:, u % 2, :, :],
                                 start=True, stop=True).then_inc(seg_mm, 1)

            def mx_output(b, u):
                d, c, k = unit(u)
                if u == 0:
                    pe.wait_ge(gm_r, 2 * b + 2)
                    pe.wait_ge(ea_r, b + 1)
                else:
                    pe.wait_ge(yt_r, 8 * b + u)
                if k > 0:
                    pe.wait_ge(st_r, 6 * b + 2 * (k - 1) + d + 1)
                    nc.tensor.matmul(y_ps[:, 0:INNER], bc[:, 2 * d + 1, c * P:(c + 1) * P], state[:, d, :],
                                     start=True, stop=True)
                pe.wait_ge(m_r, 8 * b + u + 1)
                for h in range(HEADS):
                    mm = nc.tensor.matmul(y_ps[:, INNER + h * HDIM:INNER + (h + 1) * HDIM], mm_[:, u % 2, h, :],
                                          xdt[:, d, c, h * HDIM:(h + 1) * HDIM], start=True, stop=True)
                mm.then_inc(yd_mm, 1)

            def mx_state(b, u):
                d, c, k = unit(u)
                pe.wait_ge(xdd_r, 6 * b + u + 1)
                if u >= 1:
                    pe.wait_ge(st_r, 6 * b + u)
                nc.tensor.matmul(state_ps[:, (u % 2) * INNER:(u % 2 + 1) * INNER],
                                 btm[:, d, c, :], xdd[:, u % 2, :],
                                 start=True, stop=True).then_inc(st_mm, 1)

            def mx_shift(b, u):
                d, c, _ = unit(u)
                pe.wait_ge(yt_r, 8 * b + u + 1)
                lo = c * P + (1 if d == 0 else -1)
                first, last = max(lo, 0), min(lo + P, S)
                for ct in range(CT):
                    mm = nc.tensor.matmul(conv_ps[ct][:, first:last], yt[:, u % 2, ct * P:(ct + 1) * P],
                                          cst[:, IDENT, first - lo:last - lo], start=False, stop=(u == STEPS - 1),
                                          skip_group_check=True)
                mm.then_inc(sh_mm, 1)

            def mx_project(b):
                pe.wait_ge(sq_r, 2 * b + 2)
                pe.wait_ge(st_r, 6 * b + 6)
                for j in range(NT):
                    for ct in range(CT):
                        mm = nc.tensor.matmul(state_ps[:, j:j + 1], sq[:, ct, j * P:(j + 1) * P], cst[:, ONES, 0:1],
                                              start=(ct == 0), stop=(ct == CT - 1))
                mm.then_inc(ms_mm, 1)
                pe.wait_ge(dec_r, 8 * b + 8)
                for j in range(NT):
                    for ct in range(CT):
                        mm = nc.tensor.matmul(seg_ps[:, j * P:(j + 1) * P], yg[:, ct, j * P:(j + 1) * P], wout[:, ct, :],
                                              start=(ct == 0), stop=(ct == CT - 1))
                mm.then_inc(pj_mm, 1)

            def mixer(b, nxt):
                def l0(f, *a):
                    if nxt is not None:
                        f(nxt, *a)
                for n in range(2, 8):
                    mx_conv(b, n)
                    if n == 2:
                        mx_skip(b, 0)
                    if n == 3:
                        l0(l0_transpose)
                        mx_skip(b, 1)
                    if n in (4, 5, 6):
                        l0(l0_gates, n - 4)
                    if n == 4:
                        mx_timemajor(b, 0)
                        mx_timemajor(b, 1)
                    if n == 4 and nxt is None:
                        ranks()
                    if n == 6:
                        mx_timemajor(b, 2)
                        mx_timemajor(b, 3)
                mx_sums(b)
                mx_gram(b, 0)
                mx_gram(b, 1)
                mx_clear(b, 0)
                mx_clear(b, 1)
                mx_segments(b, 0)
                for u in range(STEPS):
                    if u + 1 < STEPS:
                        mx_segments(b, u + 1)
                    if u >= 1:
                        mx_shift(b, u - 1)
                    if u == 4:
                        l0(l0_back)
                    if u == 7:
                        l0(l0_u)
                    mx_output(b, u)
                    if u < STEPS - 2:
                        mx_state(b, u)
                    if u == 0:
                        l0(l0_ffn)
                mx_shift(b, STEPS - 1)
                if nxt is not None:
                    l0_logits(nxt)
                    mx_head(b + 1)
                mx_project(b)

            def mx_head(b):
                mx_dt(b)
                mx_conv(b, 0)
                mx_conv(b, 1)

            def layer0(b):
                l0_transpose(b)
                for g in range(3):
                    l0_gates(b, g)
                l0_ffn(b)
                l0_back(b)
                l0_u(b)
                l0_logits(b)

            def ranks():
                pe.wait_ge(route, ROUTE_BOTH)
                pe.wait_ge(lg_r, B)
                nc.tensor.matmul(l0a_ps[:, 0:TILES * E], cst[:, BEFORE, :], both.rearrange("p t e -> p (t e)"),
                                 start=True, stop=True)
                nc.tensor.matmul(l0b_ps[:, 0:TILES * E], ones, both.rearrange("p t e -> p (t e)"),
                                 start=True, stop=True).then_inc(rank_mm, 1)

            def ex_transpose(i, n, first):
                pe.wait_ge(xe_in[n], (i - n) * (16 // DEEP) + 16)
                if not first:
                    pe.wait_ge(xeT_r, i - 1)
                nc.tensor.transpose(bank[n % 2][:, 0:P], xe[:, n, 0:D], ident).then_inc(xeT_mm, 1)

            def ex_hidden(i, n, first):
                e = pe.value_load(tile_e[0:1, bass.ds(i, 1)], min_val=0, max_val=E - 1)
                pe.wait_ge(xeT_r, i + 1)
                if not first:
                    pe.wait_ge(hid_r, i - 1)
                nc.tensor.matmul(bank[2 + n % 2][:], xeT[:, n % 2, :],
                                 ws1[:, bass.ds(e, 1), :].rearrange("p a f -> p (a f)"),
                                 start=True, stop=True).then_inc(h_mm, 1)

            def ex_hiddenT(i, n, first):
                pe.wait_ge(hid_r, i + 1)
                if not first:
                    pe.wait_ge(hidT_r, i - 1)
                for f in range(CT):
                    mm = nc.tensor.transpose(bank[4 + n % 2][:, f * P:(f + 1) * P], hid[:, n % 2, f * P:(f + 1) * P], ident)
                mm.then_inc(hidT_mm, 1)

            def ex_out(i, n, first):
                e = pe.value_load(tile_e[0:1, bass.ds(i, 1)], min_val=0, max_val=E - 1)
                pe.wait_ge(hidT_r, i + 1)
                if not first:
                    pe.wait_ge(ye_r, i - 1)
                for f in range(CT):
                    mm = nc.tensor.matmul(bank[6 + n % 2][:, 0:D], hidT[:, n % 2, f * P:(f + 1) * P],
                                          ws2[:, bass.ds(e, 1), f, :].rearrange("p a d -> p (a d)"),
                                          start=(f == 0), stop=(f == CT - 1))
                mm.then_inc(y_mm, 1)

            def ex_step(i, n):
                known = isinstance(i, int)
                if not known or i + 1 < SLOT_TILES:
                    ex_transpose(i + 1, (n + 1) % DEEP, known and i < 1)
                if not known or i < SLOT_TILES:
                    ex_hidden(i, n, known and i < 2)
                if not known or 0 <= i - 1 < SLOT_TILES:
                    ex_hiddenT(i - 1, (n - 1) % DEEP, known and i - 1 < 2)
                if not known or i - 2 >= 0:
                    ex_out(i - 2, (n - 2) % DEEP, known and i - 2 < 2)

            def experts():
                pe.wait_ge(acc_r, NT * (B + 1))
                pe.wait_ge(yg_r, 2 * (B + 1))
                pe.wait_ge(ms_r, B + 1)
                pe.wait_ge(ld_w, 32)
                pe.wait_ge(route, ROUTE_ALL)
                ex_transpose(0, 0, True)
                for i in range(DEEP):
                    ex_step(i, i % DEEP)
                with pe.Fori(1, EX_LAST // DEEP) as group:
                    for n in range(DEEP):
                        ex_step(group * DEEP + n, n)
                for i in range(EX_LAST, SLOT_TILES + 2):
                    ex_step(i, i % DEEP)

            pe.wait_ge(ld_a, 16 * len(loads_a))
            pe.wait_ge(prep_v, 10)
            pe.wait_ge(prep_p, 5)
            pe.wait_ge(ld_b, 16 * len(loads_b))
            layer0(0)
            if stop == 1:
                with pe.Fori(1, B) as b:
                    layer0(b)
                return
            mx_head(1)
            with pe.Fori(1, B) as b:
                mixer(b, b)
            mixer(B, None)
            experts()

        @block.vector
        def _(v):
            def norm_stats(b, half):
                if half == 1:
                    v.wait_ge(x1_r, b + 1)
                    v.memset(carrier[:], 0.0)
                for j in range(NT):
                    v.bn_stats(st[:, j, :], x_all[:, bass.ds(b * NT + j, 1), :]).then_inc(bst, 1)
                if half == 1 or not (isinstance(b, int) and b == 0):
                    v.wait_ge(rs, 2 * b + half)
                v.wait_ge(bst, 8 * b + 4 * half + 4)
                v.memset(carrier[:], 0.0)
                for j in range(NT):
                    v.bn_aggr(mv[:, j, :], st[:, j, :]).then_inc(bag, 1)

            def norm_apply(b, half):
                v.wait_ge(rs, 2 * b + half + 1)
                if half == 1:
                    v.wait_ge(tr1, b + 1)
                elif not (isinstance(b, int) and b == 0):
                    v.wait_ge(tr2, b)
                    v.wait_ge(rows_st, 16 * b)
                for j in range(NT):
                    v.tensor_scalar(xn[:, j, :], x_all[:, bass.ds(b * NT + j, 1), :].rearrange("p a d -> p (a d)"),
                                    mv[:, j, 0:1], rstd[:, j:j + 1],
                                    ALU.subtract, ALU.mult).then_inc((xn_r, xn2_r)[half], 1)

            def l0_clamps(b):
                v.wait_ge(pre_r, 3 * b + 2)
                v.tensor_scalar(cl[:, 0:2, :], pre[:, 0:2, :], CLAMP, None, ALU.min).then_inc(cl_r, 1)
                v.wait_ge(pre_r, 3 * b + 3)
                v.tensor_scalar(cl[:, 2, :], pre[:, 2, :], 0.0, None, ALU.min).then_inc(cl_r, 1)

            def l0_quantise(b):
                v.wait_ge(xnT_r, b + 1)
                if not (isinstance(b, int) and b == 0):
                    v.wait_ge(q_p, 2 * b)
                v.tensor_copy(xq16[:], xnT[:]).then_inc(q_v, 1)
                v.wait_ge(q_v, 4 * b + 1)
                v.tensor_scalar(xqs[:], xq16[:], iscale[:, 0:1], None, ALU.mult).then_inc(q_v, 1)
                v.wait_ge(q_v, 4 * b + 2)
                v.tensor_scalar(magic[:].bitcast(U32), xqs[:].bitcast(U32), 0x7F800000, None,
                                ALU.bitwise_and).then_inc(q_v, 1)
                v.wait_ge(q_v, 4 * b + 3)
                v.tensor_scalar(magic[:], magic[:], FP8_MIN, FP8_MAGIC, ALU.max, ALU.mult).then_inc(q_v, 1)

            def l0_softplus(b):
                v.wait_ge(ln_r, b + 1)
                v.tensor_tensor(ex[:, 0:2, :], pre[:, 0:2, :], ex[:, 0:2, :], ALU.max).then_inc(sp_r, 1)
                v.wait_ge(sp_r, b + 1)
                v.tensor_tensor(diff[:], ex[:, 0, :], ex[:, 1, :], ALU.subtract).then_inc(df_r, 1)
                v.wait_ge(df_r, b + 1)
                v.tensor_scalar(cld[:], diff[:], CLAMP, None, ALU.min).then_inc(cd_r, 1)

            def l0_gatelogs(b):
                v.wait_ge(ld_r, b + 1)
                v.tensor_tensor(lgt[:, 0, :], diff[:], cld[:], ALU.max).then_inc(spd_r, 1)
                v.wait_ge(spd_r, b + 1)
                v.tensor_tensor(lgt[:, 1, :], lgt[:, 0, :], diff[:], ALU.subtract).then_inc(li_r, 1)

            def l0_recur(b):
                v.wait_ge(gt_r, b + 1)
                v.scalar_tensor_tensor(val[:], pre[:, 2, :], 0.0, lgt[:, 2, :], ALU.max, ALU.add).then_inc(g_r, 1)
                v.wait_ge(g_r, b + 1)
                v.tensor_tensor(val[:], val[:], lgt[:, 1, :], ALU.mult).then_inc(v_r, 1)
                v.wait_ge(v_r, b + 1)
                v.tensor_tensor_scan(hT[:], lgt[:, 0, :], val[:], 1.0, ALU.mult, ALU.add).then_inc(h_r, 1)
                v.wait_ge(y_r, b + 1)
                v.tensor_scalar(y16b[:], y16[:], b8[:, 0:1], None, ALU.add).then_inc(yb_r, 1)

            def l0_residual(b):
                v.wait_ge(trh, b + 1)
                rows = x_all[:, bass.ds(b * NT, NT), :]
                v.tensor_tensor(rows, rows, l0b_ps[:].rearrange("p (t d) -> p t d", t=NT), ALU.add).then_inc(x1_r, 1)

            def l0_logits(b):
                v.wait_ge(lg_mm, b + 1)
                v.tensor_copy(logits[:, bass.ds(b * NT, NT), :],
                              l0b_ps[:, 0:NT * E].rearrange("p (t e) -> p t e", t=NT)).then_inc(lg_r, 1)

            def mx_dt(b):
                v.wait_ge(dt_mm, b + 1)
                v.tensor_tensor(dtr[:], gram_ps[:, 0:NT * 8].rearrange("p (t e) -> p t e", t=NT),
                                dtb[:].unsqueeze(1).to_broadcast([P, NT, 8]), ALU.add).then_inc(dt_v, 1)
                v.wait_ge(dt_v, 5 * b + 1)
                v.tensor_scalar(dtc[:], dtr[:], CLAMP, None, ALU.min).then_inc(dt_v, 1)
                v.wait_ge(dt_s, 2 * b + 2)
                v.tensor_tensor(dt[:], dtr[:], dtc[:], ALU.max).then_inc(dt_v, 2)
                v.wait_ge(dt_v, 5 * b + 4)
                v.tensor_tensor(adt[:], dt[:], a_neg[:].unsqueeze(1).to_broadcast([P, NT, 8]), ALU.mult).then_inc(dt_v, 1)

            def mx_inputs(b, d):
                v.wait_ge(tm_r, 4 * b + 2)
                v.wait_ge(dt_v, 5 * b + 5)
                v.tensor_tensor(xdt[:, d, :, :].rearrange("p c (h q) -> p c h q", h=HEADS),
                                xtm[:].rearrange("p c (h q) -> p c h q", h=HEADS),
                                dt[:, :, d * HEADS:(d + 1) * HEADS].unsqueeze(3).to_broadcast([P, NT, HEADS, HDIM]),
                                ALU.mult).then_inc(xdt_r, 1)

            def mx_mask(b, d):
                v.wait_ge(g_mm, 2 * b + d + 1)
                v.tensor_tensor(gm[:, d, :, :], (bank[3], bank[4])[d][:].rearrange("p (c l) -> p c l", c=NT),
                                cst[:, (UPTO, FROM)[d], :].unsqueeze(1).to_broadcast([P, NT, P]),
                                ALU.mult).then_inc(gm_r, 1)

            def mx_skip(b, ct):
                v.wait_ge(fd_mm, 2 * b + ct + 1)
                v.scalar_tensor_tensor(skip[:, ct, :], (bank[3], bank[4])[ct][:], dcol[:, ct:ct + 1],
                                       xs[:, ct, 1:S + 1], ALU.add, ALU.mult).then_inc(sk_r, 1)

            def mx_decay(b, u):
                d, c, k = unit(u)
                v.wait_ge(dec_r, 8 * b + u + 1)
                v.wait_ge(gm_r, 2 * b + 2)
                v.tensor_tensor(mm_[:, u % 2, :, :], dec[:, u % 2, :, :],
                                gm[:, d, c, :].unsqueeze(1).to_broadcast([P, HEADS, P]), ALU.mult).then_inc(m_r, 1)
                if k < NT - 1:
                    v.wait_ge(xdt_r, 2 * b + d + 1)
                    if u >= 2:
                        v.wait_ge(st_mm, 6 * b + u - 1)
                    edge = P - 1 if d == 0 else 0
                    v.tensor_tensor(xdd[:, u % 2, :].rearrange("p (h q) -> p h q", h=HEADS),
                                    xdt[:, d, c, :].rearrange("p (h q) -> p h q", h=HEADS),
                                    dec[:, u % 2, :, edge:edge + 1].to_broadcast([P, HEADS, HDIM]),
                                    ALU.mult).then_inc(xdd_r, 1)

            def mx_output(b, u):
                d, c, k = unit(u)
                v.wait_ge(yd_mm, 8 * b + u + 1)
                if u >= 2:
                    v.wait_ge(sh_mm, 8 * b + u - 1)
                if k == 0:
                    v.tensor_copy(yt[:, u % 2, :], y_ps[:, INNER:]).then_inc(yt_r, 1)
                    return
                v.tensor_tensor(yo[:].rearrange("p (h q) -> p h q", h=HEADS),
                                y_ps[:, 0:INNER].rearrange("p (h q) -> p h q", h=HEADS),
                                ea[:, d, c, :].unsqueeze(2).to_broadcast([P, HEADS, HDIM]), ALU.mult).then_inc(yo_r, 1)
                v.wait_ge(yo_r, 6 * b + u - 1)
                v.tensor_tensor(yt[:, u % 2, :], yo[:], y_ps[:, INNER:], ALU.add).then_inc(yt_r, 1)

            def mx_state(b, u):
                d, c, k = unit(u)
                half = state_ps[:, (u % 2) * INNER:(u % 2 + 1) * INNER]
                if k == 0:
                    v.wait_ge(st_mm, 6 * b + u + 1)
                    v.tensor_copy(state[:, d, :], half).then_inc(st_r, 1)
                    return
                v.wait_ge(st_mm, 6 * b + u + 1)
                v.tensor_tensor(stt_[:].rearrange("p (h q) -> p h q", h=HEADS),
                                state[:, d, :].rearrange("p (h q) -> p h q", h=HEADS),
                                ea[:, 2 + d, c, :].unsqueeze(2).to_broadcast([P, HEADS, HDIM]), ALU.mult).then_inc(stp_r, 1)
                v.wait_ge(stp_r, 4 * b + u - 1)
                v.tensor_tensor(state[:, d, :], stt_[:], half, ALU.add).then_inc(st_r, 1)

            def mx_neighbours(b, ct):
                v.wait_ge(nb_r, 2 * b + ct + 1)
                v.wait_ge(sk_r, 2 * b + ct + 1)
                v.scalar_tensor_tensor(skip[:, ct, :], nb[:, ct, :], dcol[:, ct:ct + 1], skip[:, ct, :],
                                       ALU.mult, ALU.add).then_inc(nbs_r, 1)

            def mx_gate(b):
                v.wait_ge(nbs_r, 2 * b + 2)
                v.wait_ge(sh_mm, 8 * b + 8)
                for ct in range(CT):
                    v.tensor_tensor(ysum[:, ct, :], skip[:, ct, :], conv_ps[ct][:], ALU.add).then_inc(ya_r, 1)
                for ct in range(CT):
                    v.wait_ge(ya_r, 2 * b + ct + 1)
                    v.tensor_tensor(yg[:, ct, :], ysum[:, ct, :], zs[:, ct, :], ALU.mult).then_inc(yg_r, 1)

            def mx_finish(b):
                v.wait_ge(ms_mm, b + 1)
                v.tensor_scalar(ms[:], state_ps[:, 0:NT], 1.0 / INNER, EPS, ALU.mult, ALU.add).then_inc(ms_r, 1)
                v.wait_ge(rms_r, b + 1)
                v.wait_ge(pj_mm, b + 1)
                for j in range(NT):
                    row = x_all[:, bass.ds((b - 1) * NT + j, 1), :].rearrange("p a d -> p (a d)")
                    v.scalar_tensor_tensor(row, seg_ps[:, j * P:(j + 1) * P], rms[:, j:j + 1], row,
                                           ALU.mult, ALU.add).then_inc(acc_r, 1)

            def mixer(b, nxt):
                def l0(f, *a):
                    if nxt is not None:
                        f(nxt, *a)
                l0(norm_stats, 0)
                l0(norm_apply, 0)
                mx_skip(b, 0)
                mx_skip(b, 1)
                l0(l0_quantise)
                mx_inputs(b, 0)
                mx_inputs(b, 1)
                mx_neighbours(b, 0)
                mx_neighbours(b, 1)
                l0(l0_clamps)
                mx_mask(b, 0)
                mx_mask(b, 1)
                for u in range(STEPS):
                    if u == 0:
                        mx_decay(b, 0)
                    if u + 1 < STEPS:
                        mx_decay(b, u + 1)
                    mx_output(b, u)
                    if u < STEPS - 2:
                        mx_state(b, u)
                    if u == 0:
                        l0(l0_softplus)
                    if u == 1:
                        l0(l0_gatelogs)
                    if u == 2:
                        l0(l0_recur)
                    if u == 4:
                        l0(l0_residual)
                        l0(norm_stats, 1)
                    if u == 5:
                        l0(norm_apply, 1)
                mx_gate(b)
                if nxt is not None:
                    mx_dt(b + 1)
                    l0_logits(nxt)
                mx_finish(b)

            def layer0(b):
                norm_stats(b, 0)
                norm_apply(b, 0)
                l0_quantise(b)
                l0_clamps(b)
                l0_softplus(b)
                l0_gatelogs(b)
                l0_recur(b)
                l0_residual(b)
                norm_stats(b, 1)
                norm_apply(b, 1)
                l0_logits(b)

            def routing():
                steps = [0]

                def then(ins, at=None):
                    steps[0] += 1
                    assert at is None or steps[0] == at, steps
                    ins.then_inc(route, 1)
                    v.wait_ge(route, steps[0])

                def over_e(x):
                    return x.unsqueeze(2).to_broadcast([P, TILES, E])

                def over_t(x):
                    return x.unsqueeze(1).to_broadcast([P, TILES, E])

                v.wait_ge(ld_t, 48)
                v.wait_ge(lg_r, B)
                then(v.tensor_scalar(rev[:], iota[:, 0:E], -1.0, float(E), ALU.mult, ALU.add))
                for k in range(TOP):
                    src = logits[:] if k == 0 else pos
                    then(v.tensor_reduce(best[:, k, :], src, AX.X, ALU.max))
                    then(v.tensor_tensor(oh, src, over_e(best[:, k, :]), ALU.is_equal))
                    then(v.tensor_tensor(score, oh, over_t(rev[:]), ALU.mult))
                    then(v.tensor_reduce(low[:], score, AX.X, ALU.max))
                    then(v.tensor_tensor(picks[k], over_t(rev[:]), over_e(low[:]), ALU.is_equal))
                    if k == 0:
                        then(v.tensor_scalar(score, picks[0], -3.0e38, None, ALU.mult))
                        then(v.tensor_tensor(pos, score, logits[:], ALU.add))
                then(v.tensor_tensor(weight[:, 1, :], best[:, 1, :], best[:, 0, :], ALU.subtract), ROUTE_GAP)
                then(v.tensor_tensor(both, picks[0], picks[1], ALU.add), ROUTE_BOTH)
                v.wait_ge(gap_exp, 1)
                then(v.tensor_scalar(low[:], weight[:, 1, :], 1.0, None, ALU.add))
                then(v.reciprocal(weight[:, 0, :], low[:]))
                then(v.tensor_tensor(weight[:, 1, :], weight[:, 1, :], weight[:, 0, :], ALU.mult))
                v.wait_ge(rank_mm, 1)
                then(v.tensor_copy(totals.rearrange("p e t -> p t e"),
                                   l0b_ps[:, 0:TILES * E].rearrange("p (t e) -> p t e", e=E)))
                for e in range(E):
                    v.tensor_tensor_scan(running[:, e, :], cst[:, ONES, 0:TILES], totals[:, e, :], 0.0,
                                         ALU.mult, ALU.add).then_inc(route, 1)
                steps[0] += E
                v.wait_ge(route, steps[0])
                then(v.tensor_scalar(count_i[:], running[:, :, TILES - 1], float(P - 1), None, ALU.add))
                then(v.tensor_scalar(count_i[:], count_i[:], 7, None, ALU.arith_shift_right))
                then(v.tensor_copy(need[:], count_i[:]))
                then(v.tensor_tensor_scan(upto_e[:], cst[:, ONES, 0:E], need[:], 0.0, ALU.mult, ALU.add))
                then(v.tensor_tensor(base[:], upto_e[:], need[:], ALU.subtract))
                then(v.tensor_tensor(running, running, totals, ALU.subtract))
                then(v.scalar_tensor_tensor(running, base[:].unsqueeze(2).to_broadcast([P, E, TILES]), float(P),
                                            running, ALU.mult, ALU.add))
                then(v.tensor_tensor(pos, running.rearrange("p e t -> p t e"),
                                     l0a_ps[:, 0:TILES * E].rearrange("p (t e) -> p t e", e=E), ALU.add))
                for k in range(TOP):
                    then(v.tensor_tensor(score, picks[k], pos, ALU.mult))
                    then(v.tensor_reduce(posf[:, k, :], score, AX.X, ALU.add))
                then(v.tensor_copy(slot[:], posf[:]))
                then(v.tensor_tensor(begun, base[:].unsqueeze(1).to_broadcast([P, SLOT_TILES, E]),
                                     iota[:].unsqueeze(2).to_broadcast([P, SLOT_TILES, E]), ALU.is_le))
                then(v.tensor_reduce(tile_ef[:], begun, AX.X, ALU.add))
                then(v.tensor_scalar(tile_e[:], tile_ef[:], -1.0, None, ALU.add), ROUTE_ALL)

            def ex_product(i, n, first):
                v.wait_ge(sg_r, i + 1)
                if not first:
                    v.wait_ge(hidT_mm, i - 1)
                v.tensor_tensor(hid[:, n % 2, :], sg[:, n % 2, :], bank[2 + n % 2][:, F:], ALU.mult).then_inc(hid_r, 1)

            def ex_rows(i, n, first):
                v.wait_ge(xe_in[n], (i - n) * (16 // DEEP) + 16)
                if not first:
                    v.wait_ge(y_out[n], (i - n) * (16 // DEEP))
                v.tensor_copy(to_row[:, n, :], xe[:, n, D:D + 1].bitcast(U32)).then_inc(row_r, 1)

            def ex_result(i, n, first):
                v.wait_ge(y_mm, i + 1)
                if not first:
                    v.wait_ge(y_out[n], (i - n) * (16 // DEEP))
                v.tensor_copy(ye[:, n, :], bank[6 + n % 2][:, 0:D]).then_inc(ye_r, 1)

            def ex_step(i, n):
                known = isinstance(i, int)
                if not known or i < SLOT_TILES:
                    ex_rows(i, n, known and i < DEEP)
                    ex_product(i, n, known and i < 2)
                if not known or i >= 2:
                    ex_result(i - 2, (n - 2) % DEEP, known and i - 2 < DEEP)

            def experts():
                for i in range(DEEP + 2):
                    ex_step(i, i % DEEP)
                with v.Fori(1, EX_LAST // DEEP) as group:
                    for n in range(2, DEEP + 2):
                        ex_step(group * DEEP + n, n % DEEP)
                for i in range(EX_LAST + 2, SLOT_TILES + 2):
                    ex_step(i, i % DEEP)

            def combine():
                for b in range(B):
                    v.wait_ge(pair_in[b % 2], 16 * (b // 2 + 1))
                    for k, done in enumerate((sum1, sum2)):
                        if k == 1:
                            v.wait_ge(sum1, NT * (b + 1))
                        for j in range(NT):
                            t = b * NT + j
                            v.scalar_tensor_tensor(x_all[:, t, :], pair[:, b % 2, j, k, :], weight[:, k, t:t + 1],
                                                   x_all[:, t, :], ALU.mult, ALU.add).then_inc(done, 1)

            v.wait_ge(ld_a, 16 * len(loads_a))
            v.reciprocal(iscale[:], scales[:]).then_inc(prep_v, 1)
            v.tensor_tensor(sprod[:], scales[:, 0:1], scales[:, 1:2], ALU.mult).then_inc(prep_v, 1)
            v.tensor_scalar(bg[:, 0:2], bg[:, 0:2], -1.0, None, ALU.mult).then_inc(prep_v, 1)
            v.wait_ge(prep_v, 3)
            v.tensor_scalar(xqs[:, 0:P], kraw[:], iscale[:, 1:2], None, ALU.mult).then_inc(prep_v, 1)
            v.wait_ge(prep_v, 4)
            v.tensor_scalar(magic[:, 0:P].bitcast(U32), xqs[:, 0:P].bitcast(U32), 0x7F800000, None,
                            ALU.bitwise_and).then_inc(prep_v, 1)
            v.wait_ge(prep_v, 5)
            v.tensor_scalar(magic[:, 0:P], magic[:, 0:P], FP8_MIN, FP8_MAGIC, ALU.max, ALU.mult).then_inc(prep_v, 1)
            v.wait_ge(prep_p, 5)
            v.wait_ge(ld_b, 16 * len(loads_b))
            for k in range(TAPS):
                last = v.tensor_tensor(taps[:, k, :], taps[:, k, :], w_in[:, INNER:INNER + 768], ALU.mult)
            last.then_inc(prep_v, 1)
            for ct in range(CT):
                v.tensor_scalar(wout[:, ct, :], wout[:, ct, :], nw[:, ct:ct + 1], None, ALU.mult).then_inc(prep_v, 1)
            v.wait_ge(prep_s, 1)
            v.tensor_scalar(a_neg[:], a_neg[:], -1.0, None, ALU.mult).then_inc(prep_v, 1)
            v.wait_ge(ld_x, 16 * B)
            layer0(0)
            if stop == 1:
                with v.Fori(1, B) as b:
                    layer0(b)
                return
            mx_dt(1)
            with v.Fori(1, B) as b:
                mixer(b, b)
            routing()
            mixer(B, None)
            experts()
            combine()

        @block.scalar
        def _(s):
            act = nc.scalar.activation

            def l0_xnT(b):
                s.wait_ge(tr1, b + 1)
                if not (isinstance(b, int) and b == 0):
                    s.wait_ge(pre_mm, 3 * b)
                    s.wait_ge(q_v, 4 * b)
                act(xnT[:], l0a_ps[:], ACT.Copy).then_inc(xnT_r, 1)

            def l0_pre(b, g):
                s.wait_ge(pre_mm, 3 * b + g + 1)
                if g == 0 and not (isinstance(b, int) and b == 0):
                    s.wait_ge(g_r, b)
                act(pre[:, g, :], (l0b_ps, l0a_ps, l0b_ps)[g][:], ACT.Identity, bias=bg[:, g:g + 1],
                    scale=(1.0 if g == 2 else -1.0)).then_inc(pre_r, 1)

            def l0_exp1(b):
                s.wait_ge(cl_r, 2 * b + 2)
                act(ex, cl, ACT.Exp).then_inc(ex_r, 1)
                s.wait_ge(ex_r, b + 1)
                act(ex, ex, ACT.Ln, bias=1.0).then_inc(ln_r, 1)

            def l0_exp2(b):
                s.wait_ge(cd_r, b + 1)
                act(cld[:], cld[:], ACT.Exp).then_inc(ed_r, 1)
                s.wait_ge(ed_r, b + 1)
                act(cld[:], cld[:], ACT.Ln, bias=1.0).then_inc(ld_r, 1)

            def l0_exp3(b):
                s.wait_ge(li_r, b + 1)
                s.wait_ge(lh_r, b + 1)
                act(lgt, lgt, ACT.Exp, scale=-1.0).then_inc(gt_r, 1)

            def l0_y(b):
                s.wait_ge(ffn_mm, b + 1)
                if not (isinstance(b, int) and b == 0):
                    s.wait_ge(yb_r, b)
                act(y16[:], l0a_ps[:], ACT.Identity, bias=0.0, scale=sprod[:, 0:1]).then_inc(y_r, 1)

            def l0_uT(b):
                s.wait_ge(tr2, b + 1)
                if not (isinstance(b, int) and b == 0) and stop != 1:
                    s.wait_ge(cv_mm, 8 * b + 8)
                    s.wait_ge(lg_mm, b)
                act(uT[:, TAPS - 1:], l0a_ps[:], ACT.Copy).then_inc(uT_r, 1)

            def mx_dt(b):
                s.wait_ge(dt_v, 5 * b + 2)
                act(dtc[:], dtc[:], ACT.Exp).then_inc(dt_s, 1)
                s.wait_ge(dt_s, 2 * b + 1)
                act(dtc[:], dtc[:], ACT.Ln, bias=1.0).then_inc(dt_s, 1)

            def mx_conv(b, n):
                s.wait_ge(cv_mm, 8 * b + n + 1)
                if n == 0:
                    s.wait_ge(sk_r, 2 * b)
                    s.wait_ge(nb_r, 2 * b)
                if n == 2:
                    s.wait_ge(yd_mm, 8 * b)
                if n == 6:
                    s.wait_ge(yg_r, 2 * b)
                ps = conv_ps[n % 2]
                if n >= 6:
                    act(zs[:, n - 6, :], ps[:], ACT.Silu).then_inc(cv_r, 1)
                    return
                q = CONV_ORDER[n]
                dst = xs[:, q, 1:S + 1] if q < CT else bc[:, q - CT, :]
                act(dst, ps[:], ACT.Silu, bias=cb[:, q:q + 1]).then_inc(cv_r, 1)

            def mx_timemajor(b, n):
                s.wait_ge(tm_mm, 4 * b + n + 1)
                if n == 0:
                    s.wait_ge(xdt_r, 2 * b)
                dst = xtm[:, 2 * n:2 * n + 2, :] if n < 2 else btm[:, n - 2, :, :]
                act(dst.rearrange("p c n -> p (c n)"), tm_ps[n][:], ACT.Copy).then_inc(tm_r, 1)

            def mx_sums(b):
                s.wait_ge(ea_mm, b + 1)
                act(ea[:].rearrange("p a c h -> p (a c h)"), state_ps[:, 0:64], ACT.Exp).then_inc(ea_r, 1)

            def mx_decay(b, u):
                s.wait_ge(seg_mm, 8 * b + u + 1)
                if u >= 2:
                    s.wait_ge(m_r, 8 * b + u - 1)
                    s.wait_ge(xdd_r, 6 * b + u - 1) if u < STEPS - 0 and u - 1 <= 6 else None
                act(dec[:, u % 2, :, :].rearrange("p h l -> p (h l)"), seg_ps[:], ACT.Exp).then_inc(dec_r, 1)

            def mx_squares(b, ct):
                s.wait_ge(yg_r, 2 * b + ct + 1)
                act(sq[:, ct, :], yg[:, ct, :], ACT.Square).then_inc(sq_r, 1)

            def mixer(b, nxt):
                def l0(f, *a):
                    if nxt is not None:
                        f(nxt, *a)
                for n in range(2, 8):
                    mx_conv(b, n)
                    if n == 3:
                        l0(l0_xnT)
                    if n in (4, 5, 6):
                        l0(l0_pre, n - 4)
                    if n == 4:
                        mx_timemajor(b, 0)
                        mx_timemajor(b, 1)
                    if n == 6:
                        mx_timemajor(b, 2)
                        mx_timemajor(b, 3)
                nc.scalar.preload_act_table_set("natural_log_exp_and_others")
                mx_sums(b)
                for u in range(STEPS):
                    mx_decay(b, u)
                    if u == 0:
                        l0(l0_exp1)
                    if u == 2:
                        l0(l0_exp2)
                        l0(l0_y)
                    if u == 3:
                        l0(l0_exp3)
                l0(l0_uT)
                mx_squares(b, 0)
                mx_squares(b, 1)
                if nxt is not None:
                    mx_head(b + 1)

            def mx_head(b):
                mx_dt(b)
                mx_conv(b, 0)
                mx_conv(b, 1)

            def layer0(b):
                l0_xnT(b)
                for g in range(3):
                    l0_pre(b, g)
                l0_exp1(b)
                l0_exp2(b)
                l0_exp3(b)
                l0_y(b)
                l0_uT(b)

            def ex_step(i, n):
                known = isinstance(i, int)
                if not known or i + 1 < SLOT_TILES:
                    ex_xT(i + 1, (n + 1) % DEEP, known and i + 1 < 2)
                if not known or i < SLOT_TILES:
                    s.wait_ge(h_mm, i + 1)
                    if not known or i >= 2:
                        s.wait_ge(hid_r, i - 1)
                    act(sg[:, n % 2, :], bank[2 + n % 2][:, 0:F], ACT.Silu).then_inc(sg_r, 1)
                if not known or i >= 1:
                    s.wait_ge(hidT_mm, i)
                    if not known or i >= 3:
                        s.wait_ge(y_mm, i - 2)
                    act(hidT[:, (n - 1) % 2, :], bank[4 + (n - 1) % 2][:, 0:F], ACT.Copy).then_inc(hidT_r, 1)

            def ex_xT(i, n, first):
                s.wait_ge(xeT_mm, i + 1)
                if not first:
                    s.wait_ge(h_mm, i - 1)
                act(xeT[:, n % 2, :], bank[n % 2][:, 0:P], ACT.Copy).then_inc(xeT_r, 1)

            def experts():
                ex_xT(0, 0, True)
                for i in range(DEEP):
                    ex_step(i, i % DEEP)
                with s.Fori(1, EX_LAST // DEEP) as group:
                    for n in range(DEEP):
                        ex_step(group * DEEP + n, n)
                for i in range(EX_LAST, SLOT_TILES + 1):
                    ex_step(i, i % DEEP)

            nc.scalar.preload_act_table_set("natural_log_exp_and_others")
            s.wait_ge(ld_b, 16 * len(loads_b))
            act(a_neg[:], a_neg[:], ACT.Exp).then_inc(prep_s, 1)
            s.wait_ge(prep_v, 3)
            s.wait_ge(prep_p, 5)
            layer0(0)
            if stop == 1:
                with s.Fori(1, B) as b:
                    layer0(b)
                return
            mx_head(1)
            with s.Fori(1, B) as b:
                mixer(b, b)
            s.wait_ge(route, ROUTE_GAP)
            act(weight[:, 1, :], weight[:, 1, :], ACT.Exp).then_inc(gap_exp, 1)
            mixer(B, None)
            experts()

        @block.gpsimd
        def _(g):
            def norm_rstd(b, half):
                g.wait_ge(bag, 8 * b + 4 * half + 4)
                g.tensor_tensor(vpe[:], mv[:, :, 1], eps[:], ALU.add).then_inc(var_e, 1)
                g.wait_ge(var_e, 2 * b + half + 1)
                g.tensor_tensor(rstd[:], vpe[:], half_neg[:], ALU.pow).then_inc(rs, 1)

            def l0_round(b):
                g.wait_ge(q_v, 4 * b + 4)
                g.tensor_tensor(xqr[:], xqs[:], magic[:], ALU.add).then_inc(q_p, 1)
                g.wait_ge(q_p, 2 * b + 1)
                if not (isinstance(b, int) and b == 0):
                    g.wait_ge(ffn_mm, b)
                g.tensor_tensor(xq[:], xqr[:], magic[:], ALU.subtract).then_inc(q_p, 1)

            def l0_candidate(b):
                g.wait_ge(ln_r, b + 1)
                if not (isinstance(b, int) and b == 0):
                    g.wait_ge(h_r, b)
                g.tensor_tensor(lgt[:, 2, :], ex[:, 2, :], cl[:, 2, :], ALU.subtract).then_inc(lh_r, 1)

            def l0_sum(b):
                g.wait_ge(h_r, b + 1)
                g.wait_ge(yb_r, b + 1)
                g.tensor_tensor(hT[:], hT[:], y16b[:], ALU.add).then_inc(hs_r, 1)

            def mx_segments(b, u):
                d, c, _ = unit(u)
                if u == 0:
                    g.wait_ge(dt_v, 5 * b + 5)
                if u >= 2:
                    g.wait_ge(seg_mm, 8 * b + u - 1)
                g.tensor_tensor(seg[:, u % 2, :, :],
                                adt[:, c, d * HEADS:(d + 1) * HEADS].unsqueeze(2).to_broadcast([P, HEADS, P]),
                                cst[:, (UPTO, FROM)[d], :].unsqueeze(1).to_broadcast([P, HEADS, P]),
                                ALU.mult).then_inc(seg_r, 1)

            def mx_neighbours(b, ct):
                g.wait_ge(cv_r, 8 * b + ct + 1)
                g.wait_ge(nbs_r, 2 * b)
                g.tensor_tensor(nb[:, ct, :], xs[:, ct, 0:S], xs[:, ct, 2:S + 2], ALU.add).then_inc(nb_r, 1)

            def mx_rms(b):
                g.wait_ge(ms_r, b + 1)
                g.tensor_tensor(rms[:], ms[:], half_neg[:], ALU.pow).then_inc(rms_r, 1)

            def mixer(b, nxt):
                def l0(f, *a):
                    if nxt is not None:
                        f(nxt, *a)
                l0(norm_rstd, 0)
                mx_neighbours(b, 0)
                mx_neighbours(b, 1)
                mx_segments(b, 0)
                mx_segments(b, 1)
                l0(l0_round)
                if nxt is None:
                    scatter(0)
                for u in range(2, STEPS):
                    if nxt is None:
                        scatter(u - 1)
                    if u == 3:
                        l0(l0_candidate)
                    if u == 6:
                        l0(l0_sum)
                    mx_segments(b, u)
                l0(norm_rstd, 1)
                mx_rms(b)
                if nxt is None:
                    scatter(STEPS - 1)

            def scatter(b):
                if b == 0:
                    g.wait_ge(route, ROUTE_ALL)
                    g.wait_ge(slots_zero, 16)
                if b >= 2:
                    g.wait_ge(scattered[b % 2], 16 * NT * TOP * (b // 2))
                g.tensor_copy(stage[:, b % 2, :, :, D:D + 1].bitcast(I32),
                              ids[:, :, b * NT:(b + 1) * NT, :]).then_inc(ids_in, 1)
                g.wait_ge(ids_in, b + 1)
                g.wait_ge(ld_stage[b % 2], 16 * TOP * (b // 2 + 1))
                for k in range(TOP):
                    for j in range(NT):
                        t = b * NT + j
                        g.indirect_dma_start(slots_d, bass.IndirectOffsetOnAxis(ap=slot[:, k, t:t + 1], axis=0),
                                             stage[:, b % 2, k, j, :], None).then_inc(scattered[b % 2], 16)

            def ex_scatter(i, n):
                g.wait_ge(ye_r, i + 1)
                g.wait_ge(carried, i + 1)
                g.tensor_tensor(carrier_p[:], eps[:, 0:1], eps[:, 0:1], ALU.mult).then_inc(carried, 1)
                g.indirect_dma_start(pairs_d, bass.IndirectOffsetOnAxis(ap=to_row[:, n, :], axis=0),
                                     ye[:, n, :], None, bounds_check=B * S * TOP - 1,
                                     oob_is_err=False).then_inc(y_out[n], 16)

            def experts():
                with g.Fori(0, SLOT_TILES // DEEP) as group:
                    for n in range(DEEP):
                        ex_scatter(group * DEEP + n, n)

            def layer0(b):
                norm_rstd(b, 0)
                l0_round(b)
                l0_candidate(b)
                l0_sum(b)
                norm_rstd(b, 1)

            g.sem_inc(carried, 1)
            for per, sems in per_batch.items():
                for one in sems:
                    g.sem_inc(one, per)
            g.memset(spare[:], 0.0).then_inc(spare_r, 1)
            g.memset(eps[:], EPS)
            g.memset(half_neg[:], -0.5).then_inc(prep_p, 1)
            g.memset(zero16[:], 0.0).then_inc(prep_p, 1)
            g.memset(uT[:, 0:TAPS - 1], 0.0)
            g.memset(xs[:, :, 0:1], 0.0)
            g.memset(xs[:, :, S + 1:S + 2], 0.0).then_inc(prep_p, 1)
            g.wait_ge(prep_v, 6)
            g.tensor_tensor(xqr[:, 0:P], xqs[:, 0:P], magic[:, 0:P], ALU.add).then_inc(prep_p, 1)
            g.wait_ge(prep_p, 4)
            g.tensor_tensor(kq[:], xqr[:, 0:P], magic[:, 0:P], ALU.subtract).then_inc(prep_p, 1)
            layer0(0)
            if stop == 1:
                with g.Fori(1, B) as b:
                    layer0(b)
                return
            with g.Fori(1, B) as b:
                mixer(b, b)
            mixer(B, None)
            experts()


STOP = 0


def kernel(L0_attn_x, L0_attn_W_f, L0_attn_b_f, L0_attn_W_i, L0_attn_b_i, L0_attn_W_h, L0_attn_b_h, L0_ffn_kernel,
           L0_ffn_input_scale, L0_ffn_kernel_scale, L0_ffn_bias, L1_attn_in_proj_w, L1_attn_conv_w, L1_attn_conv_b,
           L1_attn_dt_bias, L1_attn_A_log, L1_attn_D, L1_attn_fc_D_w, L1_attn_norm_w, L1_attn_out_proj_w,
           L1_ffn_gate_w, L1_ffn_w1, L1_ffn_w2, L1_ffn_w3):
    import concourse.bacc as bacc
    from concourse.bass_utils import run_bass_kernel_spmd as run

    a = np.asarray

    def columns(w):
        return a(w).reshape(-1, P).T

    def rows(w):
        return a(w).reshape(-1, P, a(w).shape[-1]).transpose(1, 0, 2)

    ins = {
        "x": a(L0_attn_x),
        "w_gates": np.stack([a(L0_attn_W_f).T, a(L0_attn_W_i).T, a(L0_attn_W_h).T], 1),
        "b_gates": np.stack([a(L0_attn_b_f), a(L0_attn_b_i), a(L0_attn_b_h)], 1),
        "w_fp8": a(L0_ffn_kernel), "s_in": a(L0_ffn_input_scale), "s_w": a(L0_ffn_kernel_scale),
        "b_fp8": a(L0_ffn_bias).reshape(P, 1),
        "w_inT": a(L1_attn_in_proj_w).T,
        "conv_w": a(L1_attn_conv_w).reshape(-1, TAPS).T,
        "conv_b": columns(L1_attn_conv_b),
        "dt_bias": a(L1_attn_dt_bias), "a_log": a(L1_attn_A_log),
        "d_skip": columns(np.repeat(a(L1_attn_D), HDIM)),
        "w_fd": rows(np.repeat(a(L1_attn_fc_D_w), HDIM, axis=0).T),
        "norm_w": columns(L1_attn_norm_w),
        "w_outT": rows(a(L1_attn_out_proj_w).T),
        "gate_w": a(L1_ffn_gate_w),
        "w13": np.concatenate([a(L1_ffn_w1), a(L1_ffn_w3)], 2).transpose(1, 0, 2),
        "w2": a(L1_ffn_w2).reshape(E, CT, P, D).transpose(2, 0, 1, 3),
        "consts": shape_constants(),
        "row_ids": ((np.arange(TILES)[None, None, :] * P + np.arange(P)[:, None, None]) * TOP
                    + np.arange(TOP)[None, :, None]).astype(np.int32),
        "spare_ids": (B * S * TOP + np.arange(P, dtype=np.int32)).reshape(P, 1),
        "iotas": np.broadcast_to(np.arange(SLOT_TILES, dtype=np.float32), (P, SLOT_TILES)),
    }
    ins = {k: np.ascontiguousarray(v) for k, v in ins.items()}
    nc = bacc.Bacc("TRN2", target_bir_lowering=False, num_devices=1)
    aps = {k: nc.dram_tensor(f"in_{k}", v.shape, mybir.dt.from_np(v.dtype), kind="ExternalInput").ap()
           for k, v in ins.items()}
    out = nc.dram_tensor("out", (B, S, D), F32, kind="ExternalOutput").ap()
    slots_d = nc.dram_tensor("slots", (SLOT_TILES * P, PAY), F32, kind="Internal").ap()
    pairs_d = nc.dram_tensor("pairs", (B * S * TOP + P, D), F32, kind="Internal").ap()
    rows_d = nc.dram_tensor("rows", (TILES, P, D), F32, kind="Internal").ap()
    build(nc, **aps, slots_d=slots_d, pairs_d=pairs_d, rows_d=rows_d, out=out, stop=STOP)
    r = run(nc, [{f"in_{k}": v for k, v in ins.items()}], core_ids=[0])
    return r.results[0]["out"]
```

```python
from contextlib import ExitStack

import numpy as np
import concourse.bass as bass
from concourse import mybir

P = 128
B, S, D = 8, 512, 128
NT = S // P
TILES = B * NT
HEADS, HDIM = 4, 64
INNER = HEADS * HDIM
CT = INNER // P
CONV = INNER + 4 * P
TAPS = 4
E, F = 8, 256
TOP = 2
SLOT_TILES = (B * S * TOP + E * (P - 1)) // P + 1
EPS = 1e-5
CLAMP = 40.0
FP8_MIN = 2.0 ** -6
FP8_MAGIC = 1.5 * 2.0 ** 20
STEPS = 2 * NT
PAY = D + 4
DEEP = 8

F32, F32R = mybir.dt.float32, mybir.dt.float32r
BF16, U32, I32 = mybir.dt.bfloat16, mybir.dt.uint32, mybir.dt.int32
ALU, ACT, AX = mybir.AluOpType, mybir.ActivationFunctionType, mybir.AxisListType

XA, XB, BF_, CF_, BB_, CB_ = range(6)
CONV_ORDER = [XA, XB, BF_, BB_, CF_, CB_]
IDENT, AFTER, BEFORE, UPTO, FROM, ONES = range(6)


def shape_constants():
    k = np.arange(P)[:, None]
    j = np.arange(P)[None, :]
    return np.stack([k == j, k > j, k < j, k <= j, k >= j, k + j >= 0], 1).astype(np.float32)


ROUTE_GAP, ROUTE_BOTH, ROUTE_ALL = 14, 15, 43
EX_LAST = (SLOT_TILES - 1) // DEEP * DEEP


def unit(u):
    d, k = u % 2, u // 2
    return d, (k if d == 0 else NT - 1 - k), k


def build(nc, x, w_gates, b_gates, w_fp8, s_in, s_w, b_fp8, w_inT, conv_w, conv_b, dt_bias, a_log, d_skip,
          w_fd, norm_w, w_outT, gate_w, w13, w2, consts, iotas, row_ids, spare_ids, slots_d, pairs_d, rows_d, out):
    with ExitStack() as ctx:
        def sb(name, shape, dt=F32):
            return ctx.enter_context(nc.sbuf_tensor(name, shape, dt))

        def sem(name):
            return ctx.enter_context(nc.semaphore(name))

        bank = [ctx.enter_context(nc.psum_tensor(f"bank{i}", [P, 512], F32)) for i in range(8)]
        conv_ps = bank[0:2]
        seg_ps = bank[2]
        gram_ps = bank[3]
        y_ps = bank[3:5]
        state_ps = bank[5]
        tm_ps = [bank[5], bank[2], bank[3], bank[4]]
        l0a_ps, l0b_ps = bank[6], bank[7]

        x_all = sb("x_all", [P, TILES, D])
        logits = sb("logits", [P, TILES, E])
        cst = sb("cst", [P, 6, P])
        ident, ones = cst[:, IDENT, :], cst[:, ONES, :]
        wg = sb("wg", [P, 3, P])
        bg = sb("bg", [P, 3])
        kq = sb("kq", [P, P], BF16)
        kraw = sb("kraw", [P, P], BF16)
        b8 = sb("b8", [P, 1], BF16)
        scales = sb("scales", [P, 2])
        iscale = sb("iscale", [P, 2])
        sprod = sb("sprod", [P, 1])
        w_in = sb("w_in", [P, INNER + CONV + 2 * HEADS])
        wc_hi = sb("wc_hi", [P, TAPS, CONV], F32R)
        wc_lo = sb("wc_lo", [P, TAPS, CONV], F32R)
        wz_hi = sb("wz_hi", [P, INNER], F32R)
        wz_lo = sb("wz_lo", [P, INNER], F32R)
        cb = sb("cb", [P, 6])
        dtb = sb("dtb", [P, 2 * HEADS])
        a_neg = sb("a_neg", [P, 2 * HEADS])
        dcol = sb("dcol", [P, CT])
        wfd = sb("wfd", [P, CT, INNER])
        nw = sb("nw", [P, CT])
        wout = sb("wout", [P, CT, D])
        gate = sb("gate", [P, E])
        zero16 = sb("zero16", [P, 512], BF16)
        half_neg = sb("half_neg", [P, NT])
        eps = sb("eps", [P, NT])
        carrier = sb("carrier", [P, 1])
        carrier_p = sb("carrier_p", [P, 1])
        st = sb("st", [P, NT, 6])
        mv = sb("mv", [P, NT, 2])
        vpe = sb("vpe", [P, NT])
        rstd = sb("rstd", [P, NT])
        xn = sb("xn", [P, NT, D])
        xnT = sb("xnT", [P, S])
        work = sb("work", [P, 12 * S])
        pre, cl, ex, lgt = (work[:, n * 3 * S:(n + 1) * 3 * S].rearrange("p (g s) -> p g s", g=3) for n in range(4))
        diff = sb("diff", [P, S])
        cld = sb("cld", [P, S])
        val = sb("val", [P, S])
        hT = sb("hT", [P, S])
        xq16 = sb("xq16", [P, S], BF16)
        xqs = sb("xqs", [P, S])
        magic = sb("magic", [P, S])
        xqr = sb("xqr", [P, S])
        xq = sb("xq", [P, S], BF16)
        y16 = sb("y16", [P, S], BF16)
        y16b = sb("y16b", [P, S], BF16)
        uT = sb("uT", [P, TAPS - 1 + S])
        uT_hi = sb("uT_hi", [P, TAPS - 1 + S + 1], F32R)
        uT_lo = sb("uT_lo", [P, TAPS - 1 + S + 1], F32R)
        xs = sb("xs", [P, CT, S + 2])
        bc = sb("bc", [P, 4, S])
        zs = sb("zs", [P, CT, S])
        xtm = sb("xtm", [P, NT, INNER])
        btm = sb("btm", [P, 2, NT, P])
        dtr = sb("dtr", [P, NT, 2 * HEADS])
        dtc = sb("dtc", [P, NT, 2 * HEADS])
        dt = sb("dt", [P, NT, 2 * HEADS])
        adt = sb("adt", [P, NT, 2 * HEADS])
        ea = sb("ea", [P, 4, NT, HEADS])
        xdt = sb("xdt", [P, 2, NT, INNER])
        gm = sb("gm", [P, 2, NT, P])
        seg = sb("seg", [P, 2, HEADS, P])
        dec = sb("dec", [P, 2, HEADS, P])
        mm_ = sb("mm_", [P, 2, HEADS, P])
        xdd = sb("xdd", [P, 2, INNER])
        state = sb("state", [P, 2, INNER])
        stt_ = sb("stt_", [P, INNER])
        yo = sb("yo", [P, INNER])
        yt = sb("yt", [P, 2, INNER])
        nb = sb("nb", [P, CT, S])
        skip = sb("skip", [P, CT, S])
        yg = sb("yg", [P, CT, S])
        ms = sb("ms", [P, NT])
        rms = sb("rms", [P, NT])

        ws1 = sb("ws1", [P, E, 2 * F])
        ws2 = sb("ws2", [P, E, CT, D])
        taps = ws1[:].rearrange("p e f -> p (e f)")[:, 0:TAPS * CONV].rearrange("p (k n) -> p k n", k=TAPS)
        iota = sb("iota", [P, SLOT_TILES])
        rev = sb("rev", [P, E])
        taken = [0]

        def reuse(n):
            taken[0] += n
            return work[:, taken[0] - n:taken[0]]

        def te(x):
            return x.rearrange("p (t e) -> p t e", e=E)

        stage = reuse(2 * TOP * NT * PAY).rearrange("p (q k t w) -> p q k t w", q=2, k=TOP, t=NT)
        oh, score, both, pos = (te(reuse(TILES * E)) for _ in range(4))
        picks = [te(reuse(TILES * E)) for _ in range(TOP)]
        totals, running = (reuse(TILES * E).rearrange("p (e t) -> p e t", e=E) for _ in range(2))
        begun = te(reuse(SLOT_TILES * E))
        best = sb("best", [P, TOP, TILES])
        low = sb("low", [P, TILES])
        weight = sb("weight", [P, TOP, TILES])
        count_i = sb("count_i", [P, E], I32)
        need = sb("need", [P, E])
        upto_e = sb("upto_e", [P, E])
        base = sb("base", [P, E])
        posf = sb("posf", [P, TOP, TILES])
        slot = sb("slot", [P, TOP, TILES], U32)
        tile_ef = sb("tile_ef", [P, SLOT_TILES])
        tile_e = sb("tile_e", [P, SLOT_TILES], I32)
        ids = sb("ids", [P, TOP, TILES, 1], I32)
        spare = sb("spare", [P, PAY])
        xe = bc[:].rearrange("p g s -> p (g s)")[:, 0:DEEP * PAY].rearrange("p (n w) -> p n w", n=DEEP)
        xeT = sb("xeT", [P, 2, P])
        to_row = sb("to_row", [P, DEEP, 1], U32)
        sg = seg[:].rearrange("p a h l -> p (a h l)")[:, 0:2 * F].rearrange("p (q f) -> p q f", q=2)
        hid = dec[:].rearrange("p a h l -> p (a h l)")[:, 0:2 * F].rearrange("p (q f) -> p q f", q=2)
        hidT = mm_[:].rearrange("p a h l -> p (a h l)")[:, 0:2 * F].rearrange("p (q f) -> p q f", q=2)
        ye = zs[:].rearrange("p a (c d) -> p (a c) d", d=D)
        pair = xdt[:].rearrange("p d c (a w) -> p (d c a) w", w=D).rearrange("p (q t k) w -> p q t k w", q=2, k=TOP)

        ld_x0, ld_x, ld_a, ld_b, out_st = sem("ld_x0"), sem("ld_x"), sem("ld_a"), sem("ld_b"), sem("out_st")
        prep_v, prep_p, prep_s, prep_m, uh_r, ul_r = (
            sem(n) for n in ("prep_v", "prep_p", "prep_s", "prep_m", "uh_r", "ul_r"))
        bst, bag, var_e, rs = sem("bst"), sem("bag"), sem("var_e"), sem("rs")
        xn_r, tr1, xnT_r, pre_mm, pre_r = sem("xn_r"), sem("tr1"), sem("xnT_r"), sem("pre_mm"), sem("pre_r")
        cl_r, ex_r, ln_r, sp_r, df_r = sem("cl_r"), sem("ex_r"), sem("ln_r"), sem("sp_r"), sem("df_r")
        lh_r, cd_r, ed_r, ld_r, spd_r, li_r, gt_r = (sem(n) for n in ("lh_r", "cd_r", "ed_r", "ld_r", "spd_r", "li_r", "gt_r"))
        g_r, v_r, h_r = sem("g_r"), sem("v_r"), sem("h_r")
        q_v, q_p, ffn_mm, y_r, yb_r, hs_r = (sem(n) for n in ("q_v", "q_p", "ffn_mm", "y_r", "yb_r", "hs_r"))
        trh, x1_r, xn2_r, tr2, uT_r, lg_mm, lg_r = (sem(n) for n in ("trh", "x1_r", "xn2_r", "tr2", "uT_r", "lg_mm", "lg_r"))
        dt_mm, dt_v, dt_s, ea_mm, ea_r = (sem(n) for n in ("dt_mm", "dt_v", "dt_s", "ea_mm", "ea_r"))
        cv_mm, cv_r, tm_mm, tm_r, g_mm, gm_r, fd_mm, sk_r, nb_r, xdt_r = (
            sem(n) for n in ("cv_mm", "cv_r", "tm_mm", "tm_r", "g_mm", "gm_r", "fd_mm", "sk_r", "nb_r", "xdt_r"))
        seg_r, seg_mm, dec_r, m_r, xdd_r, yd_mm, st_mm, stp_r, st_r, yo_r, yt_r, sh_mm = (
            sem(n) for n in ("seg_r", "seg_mm", "dec_r", "m_r", "xdd_r", "yd_mm", "st_mm", "stp_r", "st_r", "yo_r", "yt_r", "sh_mm"))
        nbs_r, ya_r, yg_r, sq_r, ms_mm, ms_r, rms_r, pj_mm, acc_r = (
            sem(n) for n in ("nbs_r", "ya_r", "yg_r", "sq_r", "ms_mm", "ms_r", "rms_r", "pj_mm", "acc_r"))

        ld_w, ld_t, slots_zero, rows_st, ids_in = (
            sem(n) for n in ("ld_w", "ld_t", "slots_zero", "rows_st", "ids_in"))
        ld_stage, scattered, pair_in = ([sem(f"{n}{q}") for q in range(2)] for n in ("ld_stage", "scattered", "pair_in"))
        xe_in, y_out = ([sem(f"{n}{q}") for q in range(DEEP)] for n in ("xe_in", "y_out"))
        route, gap_exp, rank_mm = sem("route"), sem("gap_exp"), sem("rank_mm")
        xeT_mm, xeT_r, row_r, h_mm, sg_r, hid_r, hidT_mm, hidT_r, y_mm, ye_r = (
            sem(n) for n in ("xeT_mm", "xeT_r", "row_r", "h_mm", "sg_r", "hid_r", "hidT_mm", "hidT_r", "y_mm",
                             "ye_r"))
        carried = sem("carried")
        sum1, sum2, spare_r = sem("sum1"), sem("sum2"), sem("spare_r")

        per_batch = {1: [dt_mm, pj_mm, ea_mm, ea_r, ms_mm, ms_r, rms_r],
                     2: [dt_s, g_mm, gm_r, fd_mm, sk_r, nb_r, xdt_r, nbs_r, ya_r, yg_r, sq_r],
                     4: [tm_mm, tm_r, stp_r, acc_r],
                     5: [dt_v],
                     6: [xdd_r, st_mm, st_r, yo_r],
                     8: [cv_mm, cv_r, seg_r, seg_mm, dec_r, m_r, yd_mm, yt_r, sh_mm]}

        block = ctx.enter_context(nc.Block())

        loads_a = [(cst[:], consts), (wg[:], w_gates), (bg[:], b_gates), (kraw[:], w_fp8), (b8[:], b_fp8),
                   (scales[:, 0:1], s_in.partition_broadcast(P)), (scales[:, 1:2], s_w.partition_broadcast(P))]
        loads_b = [(w_in[:], w_inT), (taps, conv_w.partition_broadcast(P)), (cb[:], conv_b),
                   (dtb[:, 0:HEADS], dt_bias.partition_broadcast(P)), (dtb[:, HEADS:], dt_bias.partition_broadcast(P)),
                   (a_neg[:, 0:HEADS], a_log.partition_broadcast(P)), (a_neg[:, HEADS:], a_log.partition_broadcast(P)),
                   (dcol[:], d_skip), (wfd[:], w_fd), (nw[:], norm_w), (wout[:], w_outT), (gate[:], gate_w)]

        @block.sync
        def _(sp):
            def store(b):
                sp.wait_ge(sum2, NT * (b + 1))
                sp.dma_start(out[b].rearrange("(t p) d -> p t d", p=P),
                             x_all[:, NT * b:NT * b + NT, :]).then_inc(out_st, 16)

            def load_x(b, done):
                sp.dma_start(x_all[:, NT * b:NT * b + NT, :], x[b].rearrange("(t p) d -> p t d", p=P)).then_inc(done, 16)

            load_x(0, ld_x0)
            for dst, src in loads_a:
                sp.dma_start(dst, src).then_inc(ld_a, 16)
            for dst, src in loads_b:
                sp.dma_start(dst, src).then_inc(ld_b, 16)
            for b in range(1, B):
                load_x(b, ld_x)
            sp.wait_ge(prep_m, 5)
            sp.dma_start(ws1[:], w13).then_inc(ld_w, 16)
            sp.dma_start(ws2[:], w2).then_inc(ld_w, 16)
            sp.wait_ge(spare_r, 1)
            sp.dma_start(spare[:, D:D + 1].bitcast(I32), spare_ids).then_inc(ld_t, 16)
            sp.dma_start(ids[:, :, :, 0], row_ids).then_inc(ld_t, 16)
            sp.dma_start(iota[:], iotas).then_inc(ld_t, 16)
            sp.wait_ge(ld_t, 48)
            sp.dma_start(slots_d.rearrange("(t p) w -> p t w", p=P),
                         spare[:].unsqueeze(1).to_broadcast([P, SLOT_TILES, PAY])).then_inc(slots_zero, 16)
            with sp.Fori(0, B) as b:
                sp.wait_ge(xn2_r, 4 * b + 4)
                sp.dma_start(rows_d[bass.ds(b * NT, NT), :, :].rearrange("t p d -> p t d"), xn[:]).then_inc(rows_st, 16)
            sp.wait_ge(rows_st, 16 * B)
            for b in range(B):
                if b >= 2:
                    sp.wait_ge(scattered[b % 2], 16 * NT * TOP * (b // 2))
                for k in range(TOP):
                    sp.dma_start(stage[:, b % 2, k, :, 0:D],
                                 rows_d[b * NT:(b + 1) * NT].rearrange("t p d -> p t d")).then_inc(ld_stage[b % 2], 16)
            sp.wait_ge(yd_mm, 8 * (B + 1))
            for one in scattered:
                sp.wait_ge(one, 16 * NT * TOP * B // 2)
            slot_tiles = slots_d.rearrange("(t p) w -> t p w", p=P)

            def load_tile(i, n, free):
                if free:
                    sp.wait_ge(xeT_mm, i - DEEP + 1)
                    sp.wait_ge(row_r, i - DEEP + 1)
                sp.dma_start(xe[:, n, :], slot_tiles[bass.ds(i, 1)].rearrange("a p w -> p (a w)")).then_inc(xe_in[n], 16)

            for n in range(DEEP):
                load_tile(n, n, False)
            with sp.Fori(1, SLOT_TILES // DEEP) as group:
                for n in range(DEEP):
                    load_tile(group * DEEP + n, n, True)
            for one in y_out:
                sp.wait_ge(one, 16 * (SLOT_TILES // DEEP))
            by_token = pairs_d[0:B * S * TOP].rearrange("(g t p k) d -> g p t k d", p=P, k=TOP, t=NT)
            for b in range(B):
                if b >= 2:
                    sp.wait_ge(sum2, NT * (b - 1))
                sp.dma_start(pair[:, b % 2], by_token[b]).then_inc(pair_in[b % 2], 16)
                if b >= 1:
                    store(b - 1)
            store(B - 1)
            sp.wait_ge(out_st, 16 * B)

        @block.tensor
        def _(pe):
            def l0_transpose(b):
                pe.wait_ge(xn_r, 4 * b + 4)
                if not (isinstance(b, int) and b == 0):
                    pe.wait_ge(uh_r, b)
                for j in range(NT):
                    mm = nc.tensor.transpose(l0a_ps[:, j * P:(j + 1) * P], xn[:, j, :], ident)
                mm.then_inc(tr1, 1)

            def l0_gates(b, g):
                pe.wait_ge(xnT_r, b + 1)
                ps = (l0b_ps, l0a_ps, l0b_ps)[g]
                if g == 0 and not (isinstance(b, int) and b == 0):
                    pe.wait_ge(lg_r, b)
                if g == 2:
                    pe.wait_ge(pre_r, 3 * b + 1)
                nc.tensor.matmul(ps[:], wg[:, g, :], xnT[:], start=True, stop=True).then_inc(pre_mm, 1)

            def l0_ffn(b):
                pe.wait_ge(pre_r, 3 * b + 2)
                pe.wait_ge(q_p, 2 * b + 2)
                nc.tensor.matmul(l0a_ps[:], kq[:], xq[:], start=True, stop=True).then_inc(ffn_mm, 1)

            def l0_back(b):
                pe.wait_ge(pre_r, 3 * b + 3)
                pe.wait_ge(hs_r, b + 1)
                for j in range(NT):
                    mm = nc.tensor.transpose(l0b_ps[:, j * P:(j + 1) * P], hT[:, j * P:(j + 1) * P], ident)
                mm.then_inc(trh, 1)

            def l0_u(b):
                pe.wait_ge(y_r, b + 1)
                pe.wait_ge(xn2_r, 4 * b + 4)
                for j in range(NT):
                    mm = nc.tensor.transpose(l0a_ps[:, j * P:(j + 1) * P], xn[:, j, :], ident)
                mm.then_inc(tr2, 1)

            def l0_logits(b):
                if isinstance(b, int) and b == 0:
                    pe.wait_ge(ld_b, 16 * len(loads_b))
                pe.wait_ge(uT_r, b + 1)
                pe.wait_ge(x1_r, b + 1)
                for j in range(NT):
                    mm = nc.tensor.matmul(l0b_ps[:, j * E:(j + 1) * E], uT[:, 3 + j * P:3 + (j + 1) * P], gate[:],
                                          start=True, stop=True)
                mm.then_inc(lg_mm, 1)

            def mx_dt(b):
                pe.wait_ge(uT_r, b)
                pe.wait_ge(yt_r, 8 * b - 1)
                for j in range(NT):
                    mm = nc.tensor.matmul(gram_ps[:, j * 8:(j + 1) * 8], uT[:, 3 + j * P:3 + (j + 1) * P],
                                          w_in[:, INNER + CONV:], start=True, stop=True)
                mm.then_inc(dt_mm, 1)

            def mx_conv(b, n):
                if n >= 2:
                    pe.wait_ge(cv_r, 8 * b + n - 1)
                else:
                    pe.wait_ge(ya_r, 2 * b - 1 + n)
                ps = conv_ps[n % 2]
                if n == 0:
                    pe.wait_ge(uh_r, b)
                if n < 6:
                    cols = slice(CONV_ORDER[n] * P, (CONV_ORDER[n] + 1) * P)
                    hi, lo = ([w[:, k, cols] for k in range(TAPS)] for w in (wc_hi, wc_lo))
                    first = 0
                else:
                    cols = slice((n - 6) * P, (n - 5) * P)
                    hi, lo = [wz_hi[:, cols]], [wz_lo[:, cols]]
                    first = TAPS - 1
                for part, (w, u) in enumerate(((hi, uT_hi), (lo, uT_hi), (hi, uT_lo))):
                    if part == 2 and n == 0:
                        pe.wait_ge(ul_r, b)
                    for k, one in enumerate(w):
                        mm = nc.tensor.matmul(ps[:], one, u[:, first + k:first + k + S],
                                              start=(part == 0 and k == 0), stop=(part == 2 and k == len(w) - 1))
                mm.then_inc(cv_mm, 1)

            def mx_timemajor(b, n):
                pe.wait_ge(cv_r, 8 * b + 4)
                pe.wait_ge(*((ms_r, b), (acc_r, 4 * b), (sk_r, 2 * b + 1), (sk_r, 2 * b + 2))[n])
                for q in range(4):
                    if n < 2:
                        c = 2 * n + q // 2
                        src = xs[:, q % 2, 1 + c * P:1 + (c + 1) * P]
                    else:
                        src = bc[:, 2 * (n - 2), q * P:(q + 1) * P]
                    mm = nc.tensor.transpose(tm_ps[n][:, q * P:(q + 1) * P], src, ident)
                mm.then_inc(tm_mm, 1)

            def mx_gram(b, d):
                pe.wait_ge(cv_r, 8 * b + 6)
                pe.wait_ge(tm_r, 4 * b + 3 + d)
                ps = (bank[3], bank[4])[d]
                for c in range(NT):
                    mm = nc.tensor.matmul(ps[:, c * P:(c + 1) * P], bc[:, 2 * d, c * P:(c + 1) * P],
                                          bc[:, 2 * d + 1, c * P:(c + 1) * P], start=True, stop=True)
                mm.then_inc(g_mm, 1)

            def mx_sums(b):
                pe.wait_ge(dt_v, 5 * b + 5)
                pe.wait_ge(tm_r, 4 * b + 1)
                nc.tensor.matmul(state_ps[:, 0:16], cst[:, UPTO, :], adt[:, :, 0:HEADS], start=True, stop=True)
                nc.tensor.matmul(state_ps[:, 16:32], cst[:, FROM, :], adt[:, :, HEADS:], start=True, stop=True)
                nc.tensor.matmul(state_ps[:, 32:48], ones, adt[:, :, 0:HEADS], start=True, stop=True)
                nc.tensor.matmul(state_ps[:, 48:64], ones, adt[:, :, HEADS:], start=True, stop=True).then_inc(ea_mm, 1)

            def mx_skip(b, ct):
                pe.wait_ge(*((dt_v, 5 * b + 1), (yt_r, 8 * b))[ct])
                if ct == 0:
                    pe.wait_ge(cv_r, 8 * b + 2)
                for k in range(CT):
                    mm = nc.tensor.matmul((bank[3], bank[4])[ct][:], wfd[:, k, ct * P:(ct + 1) * P], xs[:, k, 1:S + 1],
                                          start=(k == 0), stop=(k == CT - 1))
                mm.then_inc(fd_mm, 1)

            def mx_clear(b, ct):
                pe.wait_ge(cv_r, 8 * b + 7 + ct)
                nc.tensor.matmul(conv_ps[ct][:], zero16[:, 0:P], zero16[:], start=True, stop=False, skip_group_check=True)

            def mx_segments(b, u):
                d = unit(u)[0]
                pe.wait_ge(seg_r, 8 * b + u + 1)
                if u == 0:
                    pe.wait_ge(tm_r, 4 * b + 2)
                else:
                    pe.wait_ge(dec_r, 8 * b + u)
                nc.tensor.matmul(seg_ps[:], cst[:, (AFTER, BEFORE)[d], :], seg[:, u % 2, :, :],
                                 start=True, stop=True).then_inc(seg_mm, 1)

            def mx_output(b, u):
                d, c, k = unit(u)
                ps = y_ps[u % 2]
                if u == 0:
                    pe.wait_ge(gm_r, 2 * b + 2)
                    pe.wait_ge(ea_r, b + 1)
                if u >= 2:
                    pe.wait_ge(yt_r, 8 * b + u - 1)
                if k > 0:
                    pe.wait_ge(st_r, 6 * b + 2 * (k - 1) + d + 1)
                    nc.tensor.matmul(ps[:, 0:INNER], bc[:, 2 * d + 1, c * P:(c + 1) * P], state[:, d, :],
                                     start=True, stop=True)
                pe.wait_ge(m_r, 8 * b + u + 1)
                for h in range(HEADS):
                    mm = nc.tensor.matmul(ps[:, INNER + h * HDIM:INNER + (h + 1) * HDIM], mm_[:, u % 2, h, :],
                                          xdt[:, d, c, h * HDIM:(h + 1) * HDIM], start=True, stop=True)
                mm.then_inc(yd_mm, 1)

            def mx_state(b, u):
                d, c, k = unit(u)
                pe.wait_ge(xdd_r, 6 * b + u + 1)
                if u >= 1:
                    pe.wait_ge(st_r, 6 * b + u)
                nc.tensor.matmul(state_ps[:, (u % 2) * INNER:(u % 2 + 1) * INNER],
                                 btm[:, d, c, :], xdd[:, u % 2, :],
                                 start=True, stop=True).then_inc(st_mm, 1)

            def mx_shift(b, u):
                d, c, _ = unit(u)
                pe.wait_ge(yt_r, 8 * b + u + 1)
                lo = c * P + (1 if d == 0 else -1)
                first, last = max(lo, 0), min(lo + P, S)
                for ct in range(CT):
                    mm = nc.tensor.matmul(conv_ps[ct][:, first:last], yt[:, u % 2, ct * P:(ct + 1) * P],
                                          cst[:, IDENT, first - lo:last - lo], start=False, stop=(u == STEPS - 1),
                                          skip_group_check=True)
                mm.then_inc(sh_mm, 1)

            def mx_project(b):
                pe.wait_ge(sq_r, 2 * b + 2)
                pe.wait_ge(st_r, 6 * b + 6)
                for j in range(NT):
                    for ct in range(CT):
                        mm = nc.tensor.matmul(state_ps[:, j:j + 1], skip[:, ct, j * P:(j + 1) * P], cst[:, ONES, 0:1],
                                              start=(ct == 0), stop=(ct == CT - 1))
                mm.then_inc(ms_mm, 1)
                pe.wait_ge(dec_r, 8 * b + 8)
                for j in range(NT):
                    for ct in range(CT):
                        mm = nc.tensor.matmul(seg_ps[:, j * P:(j + 1) * P], yg[:, ct, j * P:(j + 1) * P], wout[:, ct, :],
                                              start=(ct == 0), stop=(ct == CT - 1))
                mm.then_inc(pj_mm, 1)

            def mixer(b, nxt):
                def l0(f, *a):
                    if nxt is not None:
                        f(nxt, *a)
                for n in range(2, 8):
                    mx_conv(b, n)
                    if n == 2:
                        mx_skip(b, 0)
                    if n == 3:
                        l0(l0_transpose)
                        mx_skip(b, 1)
                    if n in (4, 5, 6):
                        l0(l0_gates, n - 4)
                    if n == 4:
                        mx_timemajor(b, 0)
                        mx_timemajor(b, 1)
                    if n == 4 and nxt is None:
                        ranks()
                    if n == 6:
                        mx_timemajor(b, 2)
                        mx_timemajor(b, 3)
                mx_sums(b)
                mx_segments(b, 0)
                mx_gram(b, 0)
                mx_gram(b, 1)
                mx_clear(b, 0)
                mx_clear(b, 1)
                for u in range(STEPS):
                    if u + 1 < STEPS:
                        mx_segments(b, u + 1)
                    if u == 4:
                        l0(l0_back)
                    if u == 7:
                        l0(l0_u)
                    mx_output(b, u)
                    if u < STEPS - 2:
                        mx_state(b, u)
                    if u >= 1:
                        mx_shift(b, u - 1)
                    if u == 0:
                        l0(l0_ffn)
                mx_shift(b, STEPS - 1)
                if nxt is not None:
                    l0_logits(nxt)
                    mx_head(b + 1)
                mx_project(b)

            def mx_head(b):
                mx_dt(b)
                mx_conv(b, 0)
                mx_conv(b, 1)

            def layer0(b):
                l0_transpose(b)
                for g in range(3):
                    l0_gates(b, g)
                l0_ffn(b)
                l0_back(b)
                l0_u(b)
                l0_logits(b)

            def ranks():
                pe.wait_ge(route, ROUTE_BOTH)
                pe.wait_ge(lg_r, B)
                nc.tensor.matmul(l0a_ps[:, 0:TILES * E], cst[:, BEFORE, :], both.rearrange("p t e -> p (t e)"),
                                 start=True, stop=True)
                nc.tensor.matmul(l0b_ps[:, 0:TILES * E], ones, both.rearrange("p t e -> p (t e)"),
                                 start=True, stop=True).then_inc(rank_mm, 1)

            def ex_transpose(i, n, first):
                pe.wait_ge(xe_in[n], (i - n) // DEEP * 16 + 16)
                if not first:
                    pe.wait_ge(xeT_r, i - 1)
                nc.tensor.transpose(bank[n % 2][:, 0:P], xe[:, n, 0:D], ident).then_inc(xeT_mm, 1)

            def tile_experts(first, count=DEEP + 8):
                return nc.values_load_multi_w_load_instructions(
                    tile_e[0:1, bass.ds(first, count)], engines=[mybir.EngineType.PE], min_val=0, max_val=E - 1,
                    skip_runtime_bounds_check_because="it counts the experts that have begun, of E, less one; 0 has")[1]

            def ex_hidden(i, n, first, e):
                pe.wait_ge(xeT_r, i + 1)
                if not first:
                    pe.wait_ge(hid_r, i - 1)
                nc.tensor.matmul(bank[2 + n % 2][:], xeT[:, n % 2, :],
                                 ws1[:, bass.ds(e, 1), :].rearrange("p a f -> p (a f)"),
                                 start=True, stop=True).then_inc(h_mm, 1)

            def ex_hiddenT(i, n, first):
                pe.wait_ge(hid_r, i + 1)
                if not first:
                    pe.wait_ge(hidT_r, i - 1)
                for f in range(CT):
                    mm = nc.tensor.transpose(bank[4 + n % 2][:, f * P:(f + 1) * P], hid[:, n % 2, f * P:(f + 1) * P], ident)
                mm.then_inc(hidT_mm, 1)

            def ex_out(i, n, first, e):
                pe.wait_ge(hidT_r, i + 1)
                if not first:
                    pe.wait_ge(ye_r, i - 1)
                for f in range(CT):
                    mm = nc.tensor.matmul(bank[6 + n % 2][:, 0:D], hidT[:, n % 2, f * P:(f + 1) * P],
                                          ws2[:, bass.ds(e, 1), f, :].rearrange("p a d -> p (a d)"),
                                          start=(f == 0), stop=(f == CT - 1))
                mm.then_inc(y_mm, 1)

            def ex_step(i, n, e_hidden, e_out):
                known = isinstance(i, int)
                if not known or i + 1 < SLOT_TILES:
                    ex_transpose(i + 1, (n + 1) % DEEP, known and i < 1)
                if not known or 0 <= i - 2 < SLOT_TILES:
                    ex_hiddenT(i - 2, (n - 2) % DEEP, known and i - 2 < 2)
                if not known or i - 3 >= 0:
                    ex_out(i - 3, (n - 3) % DEEP, known and i - 3 < 2, e_out)
                if not known or i < SLOT_TILES:
                    ex_hidden(i, n, known and i < 2, e_hidden)

            def experts():
                pe.wait_ge(acc_r, NT * (B + 1))
                pe.wait_ge(yg_r, 2 * (B + 1))
                pe.wait_ge(ms_r, B + 1)
                pe.wait_ge(ld_w, 32)
                pe.wait_ge(route, ROUTE_ALL)
                ex_transpose(0, 0, True)
                e = tile_experts(0)
                for i in range(DEEP + 1):
                    ex_step(i, i % DEEP, e[i], e[i - 3] if i >= 3 else None)
                with pe.Fori(1, EX_LAST // DEEP) as group:
                    e = tile_experts(group * DEEP - 4)
                    for n in range(1, DEEP + 1):
                        ex_step(group * DEEP + n, n % DEEP, e[4 + n], e[4 + n - 3])
                e = tile_experts(EX_LAST - 4, SLOT_TILES - EX_LAST + 4)
                for i in range(EX_LAST + 1, SLOT_TILES + 3):
                    at = i - EX_LAST + 4
                    ex_step(i, i % DEEP, e[at] if i < SLOT_TILES else None, e[at - 3])

            pe.wait_ge(ld_a, 16 * len(loads_a))
            pe.wait_ge(prep_v, 3)
            pe.wait_ge(prep_p, 5)
            layer0(0)
            pe.wait_ge(prep_m, 8)
            mx_head(1)
            with pe.Fori(1, B) as b:
                mixer(b, b)
            mixer(B, None)
            experts()

        @block.vector
        def _(v):
            def norm_stats(b, half):
                if half == 1:
                    v.wait_ge(x1_r, b + 1)
                    v.memset(carrier[:], 0.0)
                for j in range(NT):
                    v.bn_stats(st[:, j, :], x_all[:, bass.ds(b * NT + j, 1), :]).then_inc(bst, 1)
                if half == 1 or not (isinstance(b, int) and b == 0):
                    v.wait_ge(rs, 2 * b + half)
                v.wait_ge(bst, 8 * b + 4 * half + 4)
                v.memset(carrier[:], 0.0)
                for j in range(NT):
                    v.bn_aggr(mv[:, j, :], st[:, j, :]).then_inc(bag, 1)

            def norm_apply(b, half):
                v.wait_ge(rs, 2 * b + half + 1)
                if half == 1:
                    v.wait_ge(tr1, b + 1)
                elif not (isinstance(b, int) and b == 0):
                    v.wait_ge(tr2, b)
                    v.wait_ge(rows_st, 16 * b)
                for j in range(NT):
                    v.tensor_scalar(xn[:, j, :], x_all[:, bass.ds(b * NT + j, 1), :].rearrange("p a d -> p (a d)"),
                                    mv[:, j, 0:1], rstd[:, j:j + 1],
                                    ALU.subtract, ALU.mult).then_inc((xn_r, xn2_r)[half], 1)

            def l0_clamps(b):
                v.wait_ge(pre_r, 3 * b + 2)
                v.tensor_scalar(cl[:, 0:2, :], pre[:, 0:2, :], CLAMP, None, ALU.min).then_inc(cl_r, 1)
                v.wait_ge(pre_r, 3 * b + 3)
                v.tensor_scalar(cl[:, 2, :], pre[:, 2, :], 0.0, None, ALU.min).then_inc(cl_r, 1)

            def l0_quantise(b):
                v.wait_ge(xnT_r, b + 1)
                if not (isinstance(b, int) and b == 0):
                    v.wait_ge(q_p, 2 * b)
                v.tensor_copy(xq16[:], xnT[:]).then_inc(q_v, 1)
                v.wait_ge(q_v, 4 * b + 1)
                v.tensor_scalar(xqs[:], xq16[:], iscale[:, 0:1], None, ALU.mult).then_inc(q_v, 1)
                v.wait_ge(q_v, 4 * b + 2)
                v.tensor_scalar(magic[:].bitcast(U32), xqs[:].bitcast(U32), 0x7F800000, None,
                                ALU.bitwise_and).then_inc(q_v, 1)
                v.wait_ge(q_v, 4 * b + 3)
                v.tensor_scalar(magic[:], magic[:], FP8_MIN, FP8_MAGIC, ALU.max, ALU.mult).then_inc(q_v, 1)

            def l0_softplus(b):
                v.wait_ge(ln_r, b + 1)
                v.tensor_tensor(ex[:, 0:2, :], pre[:, 0:2, :], ex[:, 0:2, :], ALU.max).then_inc(sp_r, 1)
                v.wait_ge(sp_r, b + 1)
                v.tensor_tensor(diff[:], ex[:, 0, :], ex[:, 1, :], ALU.subtract).then_inc(df_r, 1)
                v.wait_ge(df_r, b + 1)
                v.tensor_scalar(cld[:], diff[:], CLAMP, None, ALU.min).then_inc(cd_r, 1)

            def l0_gatelogs(b):
                v.wait_ge(ld_r, b + 1)
                v.tensor_tensor(lgt[:, 0, :], diff[:], cld[:], ALU.max).then_inc(spd_r, 1)
                v.wait_ge(spd_r, b + 1)
                v.tensor_tensor(lgt[:, 1, :], lgt[:, 0, :], diff[:], ALU.subtract).then_inc(li_r, 1)

            def l0_recur(b):
                v.wait_ge(gt_r, b + 1)
                v.scalar_tensor_tensor(val[:], pre[:, 2, :], 0.0, lgt[:, 2, :], ALU.max, ALU.add).then_inc(g_r, 1)
                v.wait_ge(g_r, b + 1)
                v.tensor_tensor(val[:], val[:], lgt[:, 1, :], ALU.mult).then_inc(v_r, 1)
                v.wait_ge(v_r, b + 1)
                v.tensor_tensor_scan(hT[:], lgt[:, 0, :], val[:], 1.0, ALU.mult, ALU.add).then_inc(h_r, 1)
                v.wait_ge(y_r, b + 1)
                v.tensor_scalar(y16b[:], y16[:], b8[:, 0:1], None, ALU.add).then_inc(yb_r, 1)

            def l0_residual(b):
                v.wait_ge(trh, b + 1)
                rows = x_all[:, bass.ds(b * NT, NT), :]
                v.tensor_tensor(rows, rows, l0b_ps[:].rearrange("p (t d) -> p t d", t=NT), ALU.add).then_inc(x1_r, 1)

            def l0_rest(b):
                v.wait_ge(uT_r, b + 1)
                v.wait_ge(uh_r, b + 1)
                if not (isinstance(b, int) and b == 0):
                    v.wait_ge(cv_mm, 8 * b + 8)
                v.tensor_tensor(uT_lo[:, TAPS - 1:TAPS - 1 + S], uT[:, TAPS - 1:],
                                uT_hi[:, TAPS - 1:TAPS - 1 + S].bitcast(F32), ALU.subtract).then_inc(ul_r, 1)

            def l0_logits(b):
                v.wait_ge(lg_mm, b + 1)
                v.tensor_copy(logits[:, bass.ds(b * NT, NT), :],
                              l0b_ps[:, 0:NT * E].rearrange("p (t e) -> p t e", t=NT)).then_inc(lg_r, 1)

            def mx_dt(b):
                v.wait_ge(dt_mm, b + 1)
                v.tensor_tensor(dtr[:], gram_ps[:, 0:NT * 8].rearrange("p (t e) -> p t e", t=NT),
                                dtb[:].unsqueeze(1).to_broadcast([P, NT, 8]), ALU.add).then_inc(dt_v, 1)
                v.wait_ge(dt_v, 5 * b + 1)
                v.tensor_scalar(dtc[:], dtr[:], CLAMP, None, ALU.min).then_inc(dt_v, 1)
                v.wait_ge(dt_s, 2 * b + 2)
                v.tensor_tensor(dt[:], dtr[:], dtc[:], ALU.max).then_inc(dt_v, 2)
                v.wait_ge(dt_v, 5 * b + 4)
                v.tensor_tensor(adt[:], dt[:], a_neg[:].unsqueeze(1).to_broadcast([P, NT, 8]), ALU.mult).then_inc(dt_v, 1)

            def mx_inputs(b, d):
                v.wait_ge(tm_r, 4 * b + 2)
                v.wait_ge(dt_v, 5 * b + 5)
                v.tensor_tensor(xdt[:, d, :, :].rearrange("p c (h q) -> p c h q", h=HEADS),
                                xtm[:].rearrange("p c (h q) -> p c h q", h=HEADS),
                                dt[:, :, d * HEADS:(d + 1) * HEADS].unsqueeze(3).to_broadcast([P, NT, HEADS, HDIM]),
                                ALU.mult).then_inc(xdt_r, 1)

            def mx_mask(b, d):
                v.wait_ge(g_mm, 2 * b + d + 1)
                v.tensor_tensor(gm[:, d, :, :], (bank[3], bank[4])[d][:].rearrange("p (c l) -> p c l", c=NT),
                                cst[:, (UPTO, FROM)[d], :].unsqueeze(1).to_broadcast([P, NT, P]),
                                ALU.mult).then_inc(gm_r, 1)

            def mx_skip(b, ct):
                v.wait_ge(fd_mm, 2 * b + ct + 1)
                v.scalar_tensor_tensor(skip[:, ct, :], (bank[3], bank[4])[ct][:], dcol[:, ct:ct + 1],
                                       xs[:, ct, 1:S + 1], ALU.add, ALU.mult).then_inc(sk_r, 1)

            def mx_segments(b, u):
                d, c, _ = unit(u)
                if u == 0:
                    v.wait_ge(dt_v, 5 * b + 5)
                if u >= 2:
                    v.wait_ge(seg_mm, 8 * b + u - 1)
                v.tensor_tensor(seg[:, u % 2, :, :],
                                adt[:, c, d * HEADS:(d + 1) * HEADS].unsqueeze(2).to_broadcast([P, HEADS, P]),
                                cst[:, (UPTO, FROM)[d], :].unsqueeze(1).to_broadcast([P, HEADS, P]),
                                ALU.mult).then_inc(seg_r, 1)

            def mx_decay(b, u):
                d, c, k = unit(u)
                v.wait_ge(dec_r, 8 * b + u + 1)
                v.wait_ge(gm_r, 2 * b + 2)
                v.tensor_tensor(mm_[:, u % 2, :, :], dec[:, u % 2, :, :],
                                gm[:, d, c, :].unsqueeze(1).to_broadcast([P, HEADS, P]), ALU.mult).then_inc(m_r, 1)
                if k < NT - 1:
                    v.wait_ge(xdt_r, 2 * b + d + 1)
                    if u >= 2:
                        v.wait_ge(st_mm, 6 * b + u - 1)
                    edge = P - 1 if d == 0 else 0
                    v.tensor_tensor(xdd[:, u % 2, :].rearrange("p (h q) -> p h q", h=HEADS),
                                    xdt[:, d, c, :].rearrange("p (h q) -> p h q", h=HEADS),
                                    dec[:, u % 2, :, edge:edge + 1].to_broadcast([P, HEADS, HDIM]),
                                    ALU.mult).then_inc(xdd_r, 1)

            def mx_output(b, u):
                d, c, k = unit(u)
                ps = y_ps[u % 2]
                v.wait_ge(yd_mm, 8 * b + u + 1)
                if u >= 2:
                    v.wait_ge(sh_mm, 8 * b + u - 1)
                if k == 0:
                    v.tensor_copy(yt[:, u % 2, :], ps[:, INNER:]).then_inc(yt_r, 1)
                    return
                v.wait_ge(yt_r, 8 * b + u)
                v.tensor_tensor(yo[:].rearrange("p (h q) -> p h q", h=HEADS),
                                ps[:, 0:INNER].rearrange("p (h q) -> p h q", h=HEADS),
                                ea[:, d, c, :].unsqueeze(2).to_broadcast([P, HEADS, HDIM]), ALU.mult).then_inc(yo_r, 1)
                v.wait_ge(yo_r, 6 * b + u - 1)
                v.tensor_tensor(yt[:, u % 2, :], yo[:], ps[:, INNER:], ALU.add).then_inc(yt_r, 1)

            def mx_state(b, u):
                d, c, k = unit(u)
                half = state_ps[:, (u % 2) * INNER:(u % 2 + 1) * INNER]
                if k == 0:
                    v.wait_ge(st_mm, 6 * b + u + 1)
                    v.tensor_copy(state[:, d, :], half).then_inc(st_r, 1)
                    return
                v.wait_ge(st_mm, 6 * b + u + 1)
                v.tensor_tensor(stt_[:].rearrange("p (h q) -> p h q", h=HEADS),
                                state[:, d, :].rearrange("p (h q) -> p h q", h=HEADS),
                                ea[:, 2 + d, c, :].unsqueeze(2).to_broadcast([P, HEADS, HDIM]), ALU.mult).then_inc(stp_r, 1)
                v.wait_ge(stp_r, 4 * b + u - 1)
                v.tensor_tensor(state[:, d, :], stt_[:], half, ALU.add).then_inc(st_r, 1)

            def mx_neighbours(b, ct):
                v.wait_ge(nb_r, 2 * b + ct + 1)
                v.wait_ge(sk_r, 2 * b + ct + 1)
                v.scalar_tensor_tensor(skip[:, ct, :], nb[:, ct, :], dcol[:, ct:ct + 1], skip[:, ct, :],
                                       ALU.mult, ALU.add).then_inc(nbs_r, 1)

            def mx_gate(b):
                v.wait_ge(nbs_r, 2 * b + 2)
                v.wait_ge(sh_mm, 8 * b + 8)
                for ct in range(CT):
                    v.tensor_tensor(skip[:, ct, :], skip[:, ct, :], conv_ps[ct][:], ALU.add).then_inc(ya_r, 1)
                for ct in range(CT):
                    v.wait_ge(ya_r, 2 * b + ct + 1)
                    v.tensor_tensor(yg[:, ct, :], skip[:, ct, :], zs[:, ct, :], ALU.mult).then_inc(yg_r, 1)

            def mx_finish(b):
                v.wait_ge(ms_mm, b + 1)
                v.tensor_scalar(ms[:], state_ps[:, 0:NT], 1.0 / INNER, EPS, ALU.mult, ALU.add).then_inc(ms_r, 1)
                v.wait_ge(rms_r, b + 1)
                v.wait_ge(pj_mm, b + 1)
                for j in range(NT):
                    row = x_all[:, bass.ds((b - 1) * NT + j, 1), :].rearrange("p a d -> p (a d)")
                    v.scalar_tensor_tensor(row, seg_ps[:, j * P:(j + 1) * P], rms[:, j:j + 1], row,
                                           ALU.mult, ALU.add).then_inc(acc_r, 1)

            def mixer(b, nxt):
                def l0(f, *a):
                    if nxt is not None:
                        f(nxt, *a)
                l0(norm_stats, 0)
                l0(norm_apply, 0)
                mx_skip(b, 0)
                mx_skip(b, 1)
                l0(l0_quantise)
                mx_inputs(b, 0)
                mx_inputs(b, 1)
                mx_neighbours(b, 0)
                mx_neighbours(b, 1)
                l0(l0_clamps)
                if nxt is None:
                    mx_segments(b, 0)
                    mx_segments(b, 1)
                mx_mask(b, 0)
                mx_mask(b, 1)
                for u in range(STEPS):
                    if u == 0:
                        mx_decay(b, 0)
                    if u + 1 < STEPS:
                        mx_decay(b, u + 1)
                    if nxt is None and u + 2 < STEPS:
                        mx_segments(b, u + 2)
                    mx_output(b, u)
                    if u < STEPS - 2:
                        mx_state(b, u)
                    if u == 0:
                        l0(l0_softplus)
                    if u == 1:
                        l0(l0_gatelogs)
                    if u == 2:
                        l0(l0_recur)
                    if u == 4:
                        l0(l0_residual)
                        l0(norm_stats, 1)
                    if u == 5:
                        l0(norm_apply, 1)
                l0(l0_rest)
                mx_gate(b)
                if nxt is not None:
                    mx_dt(b + 1)
                    l0_logits(nxt)
                mx_finish(b)

            def routing():
                steps = [0]

                def then(ins, at=None):
                    steps[0] += 1
                    assert at is None or steps[0] == at, steps
                    ins.then_inc(route, 1)
                    v.wait_ge(route, steps[0])

                def over_e(x):
                    return x.unsqueeze(2).to_broadcast([P, TILES, E])

                def over_t(x):
                    return x.unsqueeze(1).to_broadcast([P, TILES, E])

                v.wait_ge(ld_t, 48)
                v.wait_ge(lg_r, B)
                then(v.tensor_scalar(rev[:], iota[:, 0:E], -1.0, float(E), ALU.mult, ALU.add))
                for k in range(TOP):
                    src = logits[:] if k == 0 else pos
                    then(v.tensor_reduce(best[:, k, :], src, AX.X, ALU.max))
                    then(v.tensor_tensor(oh, src, over_e(best[:, k, :]), ALU.is_equal))
                    then(v.tensor_tensor(score, oh, over_t(rev[:]), ALU.mult))
                    then(v.tensor_reduce(low[:], score, AX.X, ALU.max))
                    then(v.tensor_tensor(picks[k], over_t(rev[:]), over_e(low[:]), ALU.is_equal))
                    if k == 0:
                        then(v.tensor_scalar(score, picks[0], -3.0e38, None, ALU.mult))
                        then(v.tensor_tensor(pos, score, logits[:], ALU.add))
                then(v.tensor_tensor(weight[:, 1, :], best[:, 1, :], best[:, 0, :], ALU.subtract), ROUTE_GAP)
                then(v.tensor_tensor(both, picks[0], picks[1], ALU.add), ROUTE_BOTH)
                v.wait_ge(gap_exp, 1)
                then(v.tensor_scalar(low[:], weight[:, 1, :], 1.0, None, ALU.add))
                then(v.reciprocal(weight[:, 0, :], low[:]))
                then(v.tensor_tensor(weight[:, 1, :], weight[:, 1, :], weight[:, 0, :], ALU.mult))
                v.wait_ge(rank_mm, 1)
                then(v.tensor_copy(totals.rearrange("p e t -> p t e"),
                                   l0b_ps[:, 0:TILES * E].rearrange("p (t e) -> p t e", e=E)))
                for e in range(E):
                    v.tensor_tensor_scan(running[:, e, :], cst[:, ONES, 0:TILES], totals[:, e, :], 0.0,
                                         ALU.mult, ALU.add).then_inc(route, 1)
                steps[0] += E
                v.wait_ge(route, steps[0])
                then(v.tensor_scalar(count_i[:], running[:, :, TILES - 1], float(P - 1), None, ALU.add))
                then(v.tensor_scalar(count_i[:], count_i[:], 7, None, ALU.arith_shift_right))
                then(v.tensor_copy(need[:], count_i[:]))
                then(v.tensor_tensor_scan(upto_e[:], cst[:, ONES, 0:E], need[:], 0.0, ALU.mult, ALU.add))
                then(v.tensor_tensor(base[:], upto_e[:], need[:], ALU.subtract))
                then(v.tensor_tensor(running, running, totals, ALU.subtract))
                then(v.scalar_tensor_tensor(running, base[:].unsqueeze(2).to_broadcast([P, E, TILES]), float(P),
                                            running, ALU.mult, ALU.add))
                then(v.tensor_tensor(pos, running.rearrange("p e t -> p t e"),
                                     l0a_ps[:, 0:TILES * E].rearrange("p (t e) -> p t e", e=E), ALU.add))
                for k in range(TOP):
                    then(v.tensor_tensor(score, picks[k], pos, ALU.mult))
                    then(v.tensor_reduce(posf[:, k, :], score, AX.X, ALU.add))
                then(v.tensor_copy(slot[:], posf[:]))
                then(v.tensor_tensor(begun, base[:].unsqueeze(1).to_broadcast([P, SLOT_TILES, E]),
                                     iota[:].unsqueeze(2).to_broadcast([P, SLOT_TILES, E]), ALU.is_le))
                then(v.tensor_reduce(tile_ef[:], begun, AX.X, ALU.add))
                then(v.tensor_scalar(tile_e[:], tile_ef[:], -1.0, None, ALU.add), ROUTE_ALL)

            def ex_product(i, n, first):
                v.wait_ge(sg_r, i + 1)
                if not first:
                    v.wait_ge(hidT_mm, i - 1)
                v.tensor_tensor(hid[:, n % 2, :], sg[:, n % 2, :], bank[2 + n % 2][:, F:], ALU.mult).then_inc(hid_r, 1)

            def ex_rows(i, n, first):
                v.wait_ge(xe_in[n], (i - n) // DEEP * 16 + 16)
                if not first:
                    v.wait_ge(y_out[n], (i - n) // DEEP * 16)
                v.tensor_copy(to_row[:, n, :], xe[:, n, D:D + 1].bitcast(U32)).then_inc(row_r, 1)

            def ex_result(i, n, first):
                v.wait_ge(y_mm, i + 1)
                if not first:
                    v.wait_ge(y_out[n], (i - n) // DEEP * 16)
                v.tensor_copy(ye[:, n, :], bank[6 + n % 2][:, 0:D]).then_inc(ye_r, 1)

            def ex_step(i, n):
                known = isinstance(i, int)
                if not known or i < SLOT_TILES:
                    ex_rows(i, n, known and i < DEEP)
                if not known or i >= 3:
                    ex_result(i - 3, (n - 3) % DEEP, known and i - 3 < DEEP)
                if not known or i < SLOT_TILES:
                    ex_product(i, n, known and i < 2)

            def experts():
                for i in range(DEEP + 3):
                    ex_step(i, i % DEEP)
                with v.Fori(1, EX_LAST // DEEP) as group:
                    for n in range(3, DEEP + 3):
                        ex_step(group * DEEP + n, n % DEEP)
                for i in range(EX_LAST + 3, SLOT_TILES + 3):
                    ex_step(i, i % DEEP)

            def combine():
                for b in range(B):
                    v.wait_ge(pair_in[b % 2], 16 * (b // 2 + 1))
                    for k, done in enumerate((sum1, sum2)):
                        if k == 1:
                            v.wait_ge(sum1, NT * (b + 1))
                        for j in range(NT):
                            t = b * NT + j
                            v.scalar_tensor_tensor(x_all[:, t, :], pair[:, b % 2, j, k, :], weight[:, k, t:t + 1],
                                                   x_all[:, t, :], ALU.mult, ALU.add).then_inc(done, 1)

            def prep_fp8():
                v.wait_ge(ld_a, 16 * len(loads_a))
                v.reciprocal(iscale[:], scales[:]).then_inc(prep_v, 1)
                v.tensor_tensor(sprod[:], scales[:, 0:1], scales[:, 1:2], ALU.mult).then_inc(prep_v, 1)
                v.tensor_scalar(bg[:, 0:2], bg[:, 0:2], -1.0, None, ALU.mult).then_inc(prep_v, 1)
                v.wait_ge(prep_v, 3)
                v.tensor_scalar(xqs[:, 0:P], kraw[:], iscale[:, 1:2], None, ALU.mult).then_inc(prep_v, 1)
                v.wait_ge(prep_v, 4)
                v.tensor_scalar(magic[:, 0:P].bitcast(U32), xqs[:, 0:P].bitcast(U32), 0x7F800000, None,
                                ALU.bitwise_and).then_inc(prep_v, 1)
                v.wait_ge(prep_v, 5)
                v.tensor_scalar(magic[:, 0:P], magic[:, 0:P], FP8_MIN, FP8_MAGIC, ALU.max, ALU.mult).then_inc(prep_v, 1)

            def prep_mixer_a():
                v.wait_ge(ld_b, 16 * len(loads_b))
                v.tensor_tensor(taps, taps, w_in[:, INNER:INNER + CONV].unsqueeze(1).to_broadcast([P, TAPS, CONV]),
                                ALU.mult).then_inc(prep_m, 1)
                v.tensor_copy(wz_hi[:], w_in[:, 0:INNER]).then_inc(prep_m, 1)

            def prep_mixer_b():
                v.wait_ge(prep_m, 3)
                v.tensor_tensor(wc_lo[:], taps, wc_hi[:].bitcast(F32), ALU.subtract).then_inc(prep_m, 1)
                v.tensor_tensor(wz_lo[:], w_in[:, 0:INNER], wz_hi[:].bitcast(F32), ALU.subtract).then_inc(prep_m, 1)
                for ct in range(CT):
                    v.tensor_scalar(wout[:, ct, :], wout[:, ct, :], nw[:, ct:ct + 1], None, ALU.mult).then_inc(prep_m, 1)
                v.wait_ge(prep_s, 1)
                v.tensor_scalar(a_neg[:], a_neg[:], -1.0, None, ALU.mult).then_inc(prep_m, 1)

            v.wait_ge(ld_x0, 16)
            v.wait_ge(prep_p, 1)
            norm_stats(0, 0)
            prep_fp8()
            norm_apply(0, 0)
            v.wait_ge(prep_p, 5)
            l0_quantise(0)
            l0_clamps(0)
            prep_mixer_a()
            l0_softplus(0)
            l0_gatelogs(0)
            prep_mixer_b()
            l0_recur(0)
            l0_residual(0)
            norm_stats(0, 1)
            norm_apply(0, 1)
            l0_rest(0)
            l0_logits(0)
            v.wait_ge(ld_x, 16 * (B - 1))
            v.wait_ge(prep_m, 8)
            mx_dt(1)
            with v.Fori(1, B) as b:
                mixer(b, b)
            routing()
            mixer(B, None)
            experts()
            combine()

        @block.scalar
        def _(s):
            act = nc.scalar.activation

            def l0_xnT(b):
                s.wait_ge(tr1, b + 1)
                if not (isinstance(b, int) and b == 0):
                    s.wait_ge(pre_mm, 3 * b)
                    s.wait_ge(q_v, 4 * b)
                act(xnT[:], l0a_ps[:], ACT.Copy).then_inc(xnT_r, 1)

            def l0_pre(b, g):
                s.wait_ge(pre_mm, 3 * b + g + 1)
                if g == 0 and not (isinstance(b, int) and b == 0):
                    s.wait_ge(g_r, b)
                act(pre[:, g, :], (l0b_ps, l0a_ps, l0b_ps)[g][:], ACT.Identity, bias=bg[:, g:g + 1],
                    scale=(1.0 if g == 2 else -1.0)).then_inc(pre_r, 1)

            def l0_exp1(b):
                s.wait_ge(cl_r, 2 * b + 2)
                act(ex, cl, ACT.Exp).then_inc(ex_r, 1)
                s.wait_ge(ex_r, b + 1)
                act(ex, ex, ACT.Ln, bias=1.0).then_inc(ln_r, 1)

            def l0_exp2(b):
                s.wait_ge(cd_r, b + 1)
                act(cld[:], cld[:], ACT.Exp).then_inc(ed_r, 1)
                s.wait_ge(ed_r, b + 1)
                act(cld[:], cld[:], ACT.Ln, bias=1.0).then_inc(ld_r, 1)

            def l0_exp3(b):
                s.wait_ge(li_r, b + 1)
                s.wait_ge(lh_r, b + 1)
                act(lgt, lgt, ACT.Exp, scale=-1.0).then_inc(gt_r, 1)

            def l0_y(b):
                s.wait_ge(ffn_mm, b + 1)
                if not (isinstance(b, int) and b == 0):
                    s.wait_ge(yb_r, b)
                act(y16[:], l0a_ps[:], ACT.Identity, bias=0.0, scale=sprod[:, 0:1]).then_inc(y_r, 1)

            def l0_uT(b):
                s.wait_ge(tr2, b + 1)
                if not (isinstance(b, int) and b == 0):
                    s.wait_ge(cv_mm, 8 * b + 8)
                    s.wait_ge(lg_mm, b)
                act(uT[:, TAPS - 1:], l0a_ps[:], ACT.Copy).then_inc(uT_r, 1)
                if not (isinstance(b, int) and b == 0):
                    s.wait_ge(ul_r, b)
                act(uT_hi[:, TAPS - 1:TAPS - 1 + S], l0a_ps[:], ACT.Copy).then_inc(uh_r, 1)

            def mx_dt(b):
                s.wait_ge(dt_v, 5 * b + 2)
                act(dtc[:], dtc[:], ACT.Exp).then_inc(dt_s, 1)
                s.wait_ge(dt_s, 2 * b + 1)
                act(dtc[:], dtc[:], ACT.Ln, bias=1.0).then_inc(dt_s, 1)

            def mx_conv(b, n):
                s.wait_ge(cv_mm, 8 * b + n + 1)
                if n == 0:
                    s.wait_ge(sk_r, 2 * b)
                    s.wait_ge(nb_r, 2 * b)
                if n == 2:
                    s.wait_ge(yd_mm, 8 * b)
                if n == 6:
                    s.wait_ge(yg_r, 2 * b)
                ps = conv_ps[n % 2]
                if n >= 6:
                    act(zs[:, n - 6, :], ps[:], ACT.Silu).then_inc(cv_r, 1)
                    return
                q = CONV_ORDER[n]
                dst = xs[:, q, 1:S + 1] if q < CT else bc[:, q - CT, :]
                act(dst, ps[:], ACT.Silu, bias=cb[:, q:q + 1]).then_inc(cv_r, 1)

            def mx_timemajor(b, n):
                s.wait_ge(tm_mm, 4 * b + n + 1)
                if n == 0:
                    s.wait_ge(xdt_r, 2 * b)
                dst = xtm[:, 2 * n:2 * n + 2, :] if n < 2 else btm[:, n - 2, :, :]
                act(dst.rearrange("p c n -> p (c n)"), tm_ps[n][:], ACT.Copy).then_inc(tm_r, 1)

            def mx_sums(b):
                s.wait_ge(ea_mm, b + 1)
                act(ea[:].rearrange("p a c h -> p (a c h)"), state_ps[:, 0:64], ACT.Exp).then_inc(ea_r, 1)

            def mx_decay(b, u):
                s.wait_ge(seg_mm, 8 * b + u + 1)
                if u >= 2:
                    s.wait_ge(m_r, 8 * b + u - 1)
                    s.wait_ge(xdd_r, 6 * b + u - 1) if u < STEPS - 0 and u - 1 <= 6 else None
                act(dec[:, u % 2, :, :].rearrange("p h l -> p (h l)"), seg_ps[:], ACT.Exp).then_inc(dec_r, 1)

            def mx_squares(b, ct):
                s.wait_ge(yg_r, 2 * b + ct + 1)
                act(skip[:, ct, :], yg[:, ct, :], ACT.Square).then_inc(sq_r, 1)

            def mixer(b, nxt):
                def l0(f, *a):
                    if nxt is not None:
                        f(nxt, *a)
                for n in range(2, 8):
                    mx_conv(b, n)
                    if n == 3:
                        l0(l0_xnT)
                    if n in (4, 5, 6):
                        l0(l0_pre, n - 4)
                    if n == 4:
                        mx_timemajor(b, 0)
                        mx_timemajor(b, 1)
                    if n == 6:
                        mx_timemajor(b, 2)
                        mx_timemajor(b, 3)
                nc.scalar.preload_act_table_set("natural_log_exp_and_others")
                mx_sums(b)
                for u in range(STEPS):
                    mx_decay(b, u)
                    if u == 0:
                        l0(l0_exp1)
                    if u == 2:
                        l0(l0_exp2)
                        l0(l0_y)
                    if u == 3:
                        l0(l0_exp3)
                l0(l0_uT)
                mx_squares(b, 0)
                mx_squares(b, 1)
                if nxt is not None:
                    mx_head(b + 1)

            def mx_head(b):
                mx_dt(b)
                mx_conv(b, 0)
                mx_conv(b, 1)

            def ex_step(i, n):
                known = isinstance(i, int)
                if not known or i + 1 < SLOT_TILES:
                    ex_xT(i + 1, (n + 1) % DEEP, known and i + 1 < 2)
                if not known or i >= 2:
                    s.wait_ge(hidT_mm, i - 1)
                    if not known or i >= 4:
                        s.wait_ge(y_mm, i - 3)
                    act(hidT[:, n % 2, :], bank[4 + n % 2][:, 0:F], ACT.Copy).then_inc(hidT_r, 1)
                if not known or i < SLOT_TILES:
                    s.wait_ge(h_mm, i + 1)
                    if not known or i >= 2:
                        s.wait_ge(hid_r, i - 1)
                    act(sg[:, n % 2, :], bank[2 + n % 2][:, 0:F], ACT.Silu).then_inc(sg_r, 1)

            def ex_xT(i, n, first):
                s.wait_ge(xeT_mm, i + 1)
                if not first:
                    s.wait_ge(h_mm, i - 1)
                act(xeT[:, n % 2, :], bank[n % 2][:, 0:P], ACT.Copy).then_inc(xeT_r, 1)

            def experts():
                ex_xT(0, 0, True)
                for i in range(DEEP):
                    ex_step(i, i % DEEP)
                with s.Fori(1, EX_LAST // DEEP) as group:
                    for n in range(DEEP):
                        ex_step(group * DEEP + n, n)
                for i in range(EX_LAST, SLOT_TILES + 2):
                    ex_step(i, i % DEEP)

            nc.scalar.preload_act_table_set("natural_log_exp_and_others")
            s.wait_ge(prep_v, 3)
            l0_xnT(0)
            for g in range(3):
                l0_pre(0, g)
            l0_exp1(0)
            s.wait_ge(ld_b, 16 * len(loads_b))
            act(a_neg[:], a_neg[:], ACT.Exp).then_inc(prep_s, 1)
            s.wait_ge(prep_m, 2)
            l0_exp2(0)
            act(wc_hi[:], taps, ACT.Copy).then_inc(prep_m, 1)
            l0_exp3(0)
            l0_y(0)
            l0_uT(0)
            mx_head(1)
            with s.Fori(1, B) as b:
                mixer(b, b)
            s.wait_ge(route, ROUTE_GAP)
            act(weight[:, 1, :], weight[:, 1, :], ACT.Exp).then_inc(gap_exp, 1)
            mixer(B, None)
            experts()

        @block.gpsimd
        def _(g):
            def norm_rstd(b, half):
                g.wait_ge(bag, 8 * b + 4 * half + 4)
                g.tensor_tensor(vpe[:], mv[:, :, 1], eps[:], ALU.add).then_inc(var_e, 1)
                g.wait_ge(var_e, 2 * b + half + 1)
                g.tensor_tensor(rstd[:], vpe[:], half_neg[:], ALU.pow).then_inc(rs, 1)

            def l0_round(b):
                g.wait_ge(q_v, 4 * b + 4)
                g.tensor_tensor(xqr[:], xqs[:], magic[:], ALU.add).then_inc(q_p, 1)
                g.wait_ge(q_p, 2 * b + 1)
                if not (isinstance(b, int) and b == 0):
                    g.wait_ge(ffn_mm, b)
                g.tensor_tensor(xq[:], xqr[:], magic[:], ALU.subtract).then_inc(q_p, 1)

            def l0_candidate(b):
                g.wait_ge(ln_r, b + 1)
                if not (isinstance(b, int) and b == 0):
                    g.wait_ge(h_r, b)
                g.tensor_tensor(lgt[:, 2, :], ex[:, 2, :], cl[:, 2, :], ALU.subtract).then_inc(lh_r, 1)

            def l0_sum(b):
                g.wait_ge(h_r, b + 1)
                g.wait_ge(yb_r, b + 1)
                g.tensor_tensor(hT[:], hT[:], y16b[:], ALU.add).then_inc(hs_r, 1)

            def mx_segments(b, u):
                d, c, _ = unit(u)
                if u == 0:
                    g.wait_ge(dt_v, 5 * b + 5)
                if u >= 2:
                    g.wait_ge(seg_mm, 8 * b + u - 1)
                g.tensor_tensor(seg[:, u % 2, :, :],
                                adt[:, c, d * HEADS:(d + 1) * HEADS].unsqueeze(2).to_broadcast([P, HEADS, P]),
                                cst[:, (UPTO, FROM)[d], :].unsqueeze(1).to_broadcast([P, HEADS, P]),
                                ALU.mult).then_inc(seg_r, 1)

            def mx_neighbours(b, ct):
                g.wait_ge(cv_r, 8 * b + ct + 1)
                g.wait_ge(nbs_r, 2 * b)
                g.tensor_tensor(nb[:, ct, :], xs[:, ct, 0:S], xs[:, ct, 2:S + 2], ALU.add).then_inc(nb_r, 1)

            def mx_rms(b):
                g.wait_ge(ms_r, b + 1)
                g.tensor_tensor(rms[:], ms[:], half_neg[:], ALU.pow).then_inc(rms_r, 1)

            def mixer(b, nxt):
                def l0(f, *a):
                    if nxt is not None:
                        f(nxt, *a)
                l0(norm_rstd, 0)
                mx_neighbours(b, 0)
                mx_neighbours(b, 1)
                if nxt is None:
                    for one in range(B):
                        scatter(one)
                else:
                    mx_segments(b, 0)
                    mx_segments(b, 1)
                    l0_round(nxt)
                    for u in range(2, STEPS):
                        if u == 3:
                            l0_candidate(nxt)
                        if u == 6:
                            l0_sum(nxt)
                        mx_segments(b, u)
                    norm_rstd(nxt, 1)
                mx_rms(b)

            def scatter(b):
                if b == 0:
                    g.wait_ge(route, ROUTE_ALL)
                    g.wait_ge(slots_zero, 16)
                if b >= 2:
                    g.wait_ge(scattered[b % 2], 16 * NT * TOP * (b // 2))
                g.tensor_copy(stage[:, b % 2, :, :, D:D + 1].bitcast(I32),
                              ids[:, :, b * NT:(b + 1) * NT, :]).then_inc(ids_in, 1)
                g.wait_ge(ids_in, b + 1)
                g.wait_ge(ld_stage[b % 2], 16 * TOP * (b // 2 + 1))
                for k in range(TOP):
                    for j in range(NT):
                        t = b * NT + j
                        g.indirect_dma_start(slots_d, bass.IndirectOffsetOnAxis(ap=slot[:, k, t:t + 1], axis=0),
                                             stage[:, b % 2, k, j, :], None).then_inc(scattered[b % 2], 16)

            def ex_scatter(i, n):
                g.wait_ge(ye_r, i + 1)
                g.wait_ge(carried, i + 1)
                g.tensor_tensor(carrier_p[:], eps[:, 0:1], eps[:, 0:1], ALU.mult).then_inc(carried, 1)
                g.indirect_dma_start(pairs_d, bass.IndirectOffsetOnAxis(ap=to_row[:, n, :], axis=0),
                                     ye[:, n, :], None, bounds_check=B * S * TOP - 1,
                                     oob_is_err=False).then_inc(y_out[n], 16)

            def experts():
                with g.Fori(0, SLOT_TILES // DEEP) as group:
                    for n in range(DEEP):
                        ex_scatter(group * DEEP + n, n)

            g.sem_inc(carried, 1)
            for per, sems in per_batch.items():
                for one in sems:
                    g.sem_inc(one, per)
            g.memset(spare[:], 0.0).then_inc(spare_r, 1)
            g.memset(eps[:], EPS)
            g.memset(half_neg[:], -0.5).then_inc(prep_p, 1)
            g.memset(zero16[:], 0.0).then_inc(prep_p, 1)
            for u in (uT, uT_hi, uT_lo):
                g.memset(u[:, 0:TAPS - 1].bitcast(F32), 0.0)
            g.memset(xs[:, :, 0:1], 0.0)
            g.memset(xs[:, :, S + 1:S + 2], 0.0).then_inc(prep_p, 1)
            norm_rstd(0, 0)
            g.wait_ge(prep_v, 6)
            g.tensor_tensor(xqr[:, 0:P], xqs[:, 0:P], magic[:, 0:P], ALU.add).then_inc(prep_p, 1)
            g.wait_ge(prep_p, 4)
            g.tensor_tensor(kq[:], xqr[:, 0:P], magic[:, 0:P], ALU.subtract).then_inc(prep_p, 1)
            l0_round(0)
            l0_candidate(0)
            l0_sum(0)
            norm_rstd(0, 1)
            with g.Fori(1, B) as b:
                mixer(b, b)
            mixer(B, None)
            experts()



def kernel(L0_attn_x, L0_attn_W_f, L0_attn_b_f, L0_attn_W_i, L0_attn_b_i, L0_attn_W_h, L0_attn_b_h, L0_ffn_kernel,
           L0_ffn_input_scale, L0_ffn_kernel_scale, L0_ffn_bias, L1_attn_in_proj_w, L1_attn_conv_w, L1_attn_conv_b,
           L1_attn_dt_bias, L1_attn_A_log, L1_attn_D, L1_attn_fc_D_w, L1_attn_norm_w, L1_attn_out_proj_w,
           L1_ffn_gate_w, L1_ffn_w1, L1_ffn_w2, L1_ffn_w3):
    import concourse.bacc as bacc
    from concourse.bass_utils import run_bass_kernel_spmd as run

    a = np.asarray

    def columns(w):
        return a(w).reshape(-1, P).T

    def rows(w):
        return a(w).reshape(-1, P, a(w).shape[-1]).transpose(1, 0, 2)

    ins = {
        "x": a(L0_attn_x),
        "w_gates": np.stack([a(L0_attn_W_f).T, a(L0_attn_W_i).T, a(L0_attn_W_h).T], 1),
        "b_gates": np.stack([a(L0_attn_b_f), a(L0_attn_b_i), a(L0_attn_b_h)], 1),
        "w_fp8": a(L0_ffn_kernel), "s_in": a(L0_ffn_input_scale), "s_w": a(L0_ffn_kernel_scale),
        "b_fp8": a(L0_ffn_bias).reshape(P, 1),
        "w_inT": a(L1_attn_in_proj_w).T,
        "conv_w": a(L1_attn_conv_w).reshape(-1, TAPS).T,
        "conv_b": columns(L1_attn_conv_b),
        "dt_bias": a(L1_attn_dt_bias), "a_log": a(L1_attn_A_log),
        "d_skip": columns(np.repeat(a(L1_attn_D), HDIM)),
        "w_fd": rows(np.repeat(a(L1_attn_fc_D_w), HDIM, axis=0).T),
        "norm_w": columns(L1_attn_norm_w),
        "w_outT": rows(a(L1_attn_out_proj_w).T),
        "gate_w": a(L1_ffn_gate_w),
        "w13": np.concatenate([a(L1_ffn_w1), a(L1_ffn_w3)], 2).transpose(1, 0, 2),
        "w2": a(L1_ffn_w2).reshape(E, CT, P, D).transpose(2, 0, 1, 3),
        "consts": shape_constants(),
        "row_ids": ((np.arange(TILES)[None, None, :] * P + np.arange(P)[:, None, None]) * TOP
                    + np.arange(TOP)[None, :, None]).astype(np.int32),
        "spare_ids": (B * S * TOP + np.arange(P, dtype=np.int32)).reshape(P, 1),
        "iotas": np.broadcast_to(np.arange(SLOT_TILES, dtype=np.float32), (P, SLOT_TILES)),
    }
    ins = {k: np.ascontiguousarray(v) for k, v in ins.items()}
    nc = bacc.Bacc("TRN2", target_bir_lowering=False, num_devices=1)
    aps = {k: nc.dram_tensor(f"in_{k}", v.shape, mybir.dt.from_np(v.dtype), kind="ExternalInput").ap()
           for k, v in ins.items()}
    out = nc.dram_tensor("out", (B, S, D), F32, kind="ExternalOutput").ap()
    slots_d = nc.dram_tensor("slots", (SLOT_TILES * P, PAY), F32, kind="Internal").ap()
    pairs_d = nc.dram_tensor("pairs", (B * S * TOP + P, D), F32, kind="Internal").ap()
    rows_d = nc.dram_tensor("rows", (TILES, P, D), F32, kind="Internal").ap()
    build(nc, **aps, slots_d=slots_d, pairs_d=pairs_d, rows_d=rows_d, out=out)
    r = run(nc, [{f"in_{k}": v for k, v in ins.items()}], core_ids=[0])
    return r.results[0]["out"]
```

```python
from contextlib import ExitStack

import numpy as np
import concourse.bass as bass
from concourse import mybir

P = 128
B, S, D = 8, 512, 128
NT = S // P
TILES = B * NT
HEADS, HDIM = 4, 64
INNER = HEADS * HDIM
CT = INNER // P
CONV = INNER + 4 * P
TAPS = 4
E, F = 8, 256
TOP = 2
SLOT_TILES = (B * S * TOP + E * (P - 1)) // P + 1
REGION = B * S // P + 1
IDLE = E * REGION
EPS = 1e-5
CLAMP = 40.0
FP8_MIN = 2.0 ** -6
FP8_MAGIC = 1.5 * 2.0 ** 20
SMALL = 2 * HEADS + E
STEPS = 2 * NT
PAY = D + 4
POOL_SUMS = [3, 7]
DEEP = 8

F32, F32R = mybir.dt.float32, mybir.dt.float32r
BF16, U32, I32 = mybir.dt.bfloat16, mybir.dt.uint32, mybir.dt.int32
ALU, ACT, AX = mybir.AluOpType, mybir.ActivationFunctionType, mybir.AxisListType

XA, XB, BF_, CF_, BB_, CB_ = range(6)
CONV_ORDER = [XA, XB, BF_, BB_, CF_, CB_]
IDENT, AFTER, BEFORE, UPTO, FROM, ONES = range(6)


def shape_constants():
    k = np.arange(P)[:, None]
    j = np.arange(P)[None, :]
    return np.stack([k == j, k > j, k < j, k <= j, k >= j, k + j >= 0], 1).astype(np.float32)


PICKED, RANKED, ROUTED = 14, 16, 23
SCALED = 15
PLAN_PADS, PLAN_EXPERTS, PLAN_BASES, PLANNED = 9, 13, 15, 21
EX_LAST = (SLOT_TILES - 1) // DEEP * DEEP


def unit(u):
    d, k = u % 2, u // 2
    return d, (k if d == 0 else NT - 1 - k), k


def build(nc, x, w_gates, b_gates, w_fp8, s_in, s_w, b_fp8, w_inT, conv_w, conv_b, dt_bias, a_log, d_skip,
          w_fd, norm_w, w_outT, gate_w, w13, w2, consts, iotas, token_ids, spare_ids, slots_d, pairs_d, out):
    with ExitStack() as ctx:
        def sb(name, shape, dt=F32):
            return ctx.enter_context(nc.sbuf_tensor(name, shape, dt))

        def sem(name):
            return ctx.enter_context(nc.semaphore(name))

        bank = [ctx.enter_context(nc.psum_tensor(f"bank{i}", [P, 512], F32)) for i in range(8)]
        conv_ps = bank[0:2]
        seg_ps = bank[2]
        y_ps = bank[3:5]
        state_ps = bank[5]
        tm_ps = [bank[5], bank[2], bank[3], bank[4]]
        l0a_ps, l0b_ps = bank[6], bank[7]

        x_all = sb("x_all", [P, TILES, D])
        logits = sb("logits", [P, TILES, E])
        cst = sb("cst", [P, 6, P])
        ident, ones = cst[:, IDENT, :], cst[:, ONES, :]
        wg = sb("wg", [P, 3, P])
        bg = sb("bg", [P, 3])
        kq = sb("kq", [P, P], BF16)
        ident16 = sb("ident16", [P, P], BF16)
        b8 = sb("b8", [P, 1], BF16)
        scales = sb("scales", [P, 2])
        inv_hi, inv_lo, scale_hi, scale_lo, rest = (
            sb(n, [P, 2]) for n in ("inv_hi", "inv_lo", "scale_hi", "scale_lo", "rest"))
        sprod = sb("sprod", [P, 1])
        w_in = sb("w_in", [P, INNER + CONV + 2 * HEADS + E])
        wc_hi = sb("wc_hi", [P, TAPS, CONV], F32R)
        wc_lo = sb("wc_lo", [P, TAPS, CONV], F32R)
        wz_hi = sb("wz_hi", [P, INNER], F32R)
        wz_lo = sb("wz_lo", [P, INNER], F32R)
        cb = sb("cb", [P, 6])
        dtb = sb("dtb", [P, 2 * HEADS])
        a_neg = sb("a_neg", [P, 2 * HEADS])
        dcol = sb("dcol", [P, CT])
        wfd = sb("wfd", [P, CT, INNER])
        nw = sb("nw", [P, CT])
        wout = sb("wout", [P, CT, D])
        zero16 = sb("zero16", [P, 512], BF16)
        half_neg = sb("half_neg", [P, NT])
        eps = sb("eps", [P, NT])
        carrier = sb("carrier", [P, 1])
        carrier_p = sb("carrier_p", [P, 1])
        st = sb("st", [P, NT, 6])
        mv = sb("mv", [P, NT, 2])
        vpe = sb("vpe", [P, NT])
        rstd = sb("rstd", [P, NT])
        xn = sb("xn", [P, NT, D])
        xnT = sb("xnT", [P, S])
        work = sb("work", [P, 12 * S])
        pre, cl, ex, lgt = (work[:, n * 3 * S:(n + 1) * 3 * S].rearrange("p (g s) -> p g s", g=3) for n in range(4))
        diff = sb("diff", [P, S])
        cld = sb("cld", [P, S])
        val = diff
        hT = sb("hT", [P, S])
        xq16 = sb("xq16", [P, S], BF16)
        xqs = sb("xqs", [P, S])
        magic = sb("magic", [P, S])
        xqr = sb("xqr", [P, S])
        xq = sb("xq", [P, S], BF16)
        kraw = xq[:, 0:P]
        y16 = sb("y16", [P, S], BF16)
        y16b = sb("y16b", [P, S], BF16)
        uT = sb("uT", [P, TAPS - 1 + S])
        uT_hi = sb("uT_hi", [P, TAPS - 1 + S + 1], F32R)
        uT_lo = sb("uT_lo", [P, TAPS - 1 + S + 1], F32R)
        xs = sb("xs", [P, CT, S + 2])
        bc = sb("bc", [P, 4, S])
        zs = sb("zs", [P, CT, S])
        xtm = sb("xtm", [P, NT, INNER])
        btm = sb("btm", [P, 2, NT, P])
        dtr = sb("dtr", [P, NT, 2 * HEADS])
        dtc = sb("dtc", [P, NT, 2 * HEADS])
        dt = sb("dt", [P, NT, 2 * HEADS])
        adt = sb("adt", [P, NT, 2 * HEADS])
        ea = sb("ea", [P, 6, NT, HEADS])
        xdt = sb("xdt", [P, 2, NT, INNER])
        gm = sb("gm", [P, 2, NT, P])
        seg = sb("seg", [P, 2, 2, HEADS, P], F32R)
        masks = sb("masks", [P, 2, P], F32R)
        adt_hi = sb("adt_hi", [P, NT, 2 * HEADS], F32R)
        adt_lo = sb("adt_lo", [P, NT, 2 * HEADS])
        dec = sb("dec", [P, 2, HEADS, P])
        mm_ = sb("mm_", [P, 2, HEADS, P])
        state = sb("state", [P, 2, INNER])
        stt_ = sb("stt_", [P, 2, INNER])
        yo = sb("yo", [P, INNER])
        yt = sb("yt", [P, 2, INNER])
        nbx = sb("nbx", [P, 2 * (NT - 1) * INNER])
        nb = nbx[:, 0:CT * S].rearrange("p (c s) -> p c s", c=CT)
        xdd = nbx[:].rearrange("p (d c n) -> p d c n", d=2, c=NT - 1)
        skip = w_in[:, 0:CT * S].rearrange("p (c s) -> p c s", c=CT)
        yg = sb("yg", [P, CT, S])
        ms = sb("ms", [P, NT])
        rms = sb("rms", [P, NT])

        ws1 = sb("ws1", [P, E, 2 * F])
        ws2 = sb("ws2", [P, E, CT, D])
        taps = ws1[:].rearrange("p e f -> p (e f)")[:, 0:TAPS * CONV].rearrange("p (k n) -> p k n", k=TAPS)
        iota = sb("iota", [P, SLOT_TILES])
        xr = sb("xr", [P, NT, PAY])
        rev = sb("rev", [P, E])
        region = sb("region", [P, E])
        oh, score, both, pos = (sb(n, [P, NT, E]) for n in ("oh", "score", "both", "pos"))
        picks = [sb(f"picks{k}", [P, NT, E]) for k in range(TOP)]
        low = sb("low", [P, TOP, NT])
        picked = sb("picked", [P, E])
        cum = sb("cum", [P, E])
        posf = sb("posf", [P, TOP, NT])
        slot = sb("slot", [P, TOP, NT], U32)
        best = sb("best", [P, TOP, TILES])
        weight = sb("weight", [P, TOP, TILES])
        denom = sb("denom", [P, TILES])
        count = sb("count", [P, E])
        count_i = sb("count_i", [P, E], I32)
        need = sb("need", [P, E])
        upto_e = sb("upto_e", [P, E])
        base = sb("base", [P, E])
        pad_at = sb("pad_at", [P, E])
        pad_slot = sb("pad_slot", [P, E], U32)
        begun, begun_base = (work[:, n * SLOT_TILES * E:(n + 1) * SLOT_TILES * E].rearrange("p (t e) -> p t e", e=E)
                             for n in range(2))
        tile_sum, tile_base, tile_at, tile_idle = (
            work[:, (2 * E + n) * SLOT_TILES:(2 * E + n + 1) * SLOT_TILES] for n in range(4))
        tile_rev = sb("tile_rev", [P, SLOT_TILES])
        tile_e = sb("tile_e", [P, SLOT_TILES], I32)
        tile_d = sb("tile_d", [P, SLOT_TILES], I32)
        spare = sb("spare", [P, PAY])
        xe = bc[:].rearrange("p g s -> p (g s)")[:, 0:DEEP * PAY].rearrange("p (n w) -> p n w", n=DEEP)
        xeT = xnT[:, 0:2 * P].rearrange("p (q t) -> p q t", q=2)
        to_row = sb("to_row", [P, DEEP, 1], U32)
        sg = skip[:, 0, :].rearrange("p (q f) -> p q f", q=2)
        hid = dec[:].rearrange("p a h l -> p (a h l)")[:, 0:2 * F].rearrange("p (q f) -> p q f", q=2)
        hidT = mm_[:].rearrange("p a h l -> p (a h l)")[:, 0:2 * F].rearrange("p (q f) -> p q f", q=2)
        ye = zs[:].rearrange("p a (c d) -> p (a c) d", d=D)
        pair = [x.rearrange("p (t k w) -> p t k w", t=NT, k=TOP) for x in
                [work[:, q * NT * TOP * D:(q + 1) * NT * TOP * D] for q in range(6)]
                + [xdt[:, d, :, :].rearrange("p c n -> p (c n)") for d in range(2)]]

        ld_x0, ld_x, ld_a, ld_b, out_st = sem("ld_x0"), sem("ld_x"), sem("ld_a"), sem("ld_b"), sem("out_st")
        prep_v, prep_p, prep_s, prep_m, taps_r, taps_hi, uh_r, ul_r = (
            sem(n) for n in ("prep_v", "prep_p", "prep_s", "prep_m", "taps_r", "taps_hi", "uh_r", "ul_r"))
        bst, bag, var_e, rs = sem("bst"), sem("bag"), sem("var_e"), sem("rs")
        xn_r, tr1, xnT_r, pre_mm, pre_r = sem("xn_r"), sem("tr1"), sem("xnT_r"), sem("pre_mm"), sem("pre_r")
        cl_r, ex_r, ln_r, sp_r, df_r = sem("cl_r"), sem("ex_r"), sem("ln_r"), sem("sp_r"), sem("df_r")
        lh_r, cd_r, ed_r, ld_r, spd_r, li_r, gt_r = (sem(n) for n in ("lh_r", "cd_r", "ed_r", "ld_r", "spd_r", "li_r", "gt_r"))
        g_r, v_r, h_r = sem("g_r"), sem("v_r"), sem("h_r")
        q_v, q_p, ffn_mm, y_r, yb_r = (sem(n) for n in ("q_v", "q_p", "ffn_mm", "y_r", "yb_r"))
        trh, x1_r, xn2_r, tr2, uT_r, lg_mm, lg_r = (sem(n) for n in ("trh", "x1_r", "xn2_r", "tr2", "uT_r", "lg_mm", "lg_r"))
        dt_v, dt_s, ea_mm, ea_r = (sem(n) for n in ("dt_v", "dt_s", "ea_mm", "ea_r"))
        cv_mm, cv_r, tm_mm, tm_r, g_mm, gm_r, fd_mm, sk_r, nb_r, xdt_r = (
            sem(n) for n in ("cv_mm", "cv_r", "tm_mm", "tm_r", "g_mm", "gm_r", "fd_mm", "sk_r", "nb_r", "xdt_r"))
        seg_r, seg_mm, dec_r, m_r, xdd_r, yd_mm, st_mm, stp_r, st_r, yo_r, yt_r, sh_mm = (
            sem(n) for n in ("seg_r", "seg_mm", "dec_r", "m_r", "xdd_r", "yd_mm", "st_mm", "stp_r", "st_r", "yo_r",
                             "yt_r", "sh_mm"))
        nbs_r, ya_r, yg_r, sq_r, ms_mm, ms_r, rms_r, pj_mm, acc_r = (
            sem(n) for n in ("nbs_r", "ya_r", "yg_r", "sq_r", "ms_mm", "ms_r", "rms_r", "pj_mm", "acc_r"))

        ld_w, ld_t, idle_st, scattered, padded = (sem(n) for n in ("ld_w", "ld_t", "idle_st", "scattered", "padded"))
        pair_in = [sem(f"pair_in{q}") for q in range(B)]
        xe_in, y_out = ([sem(f"{n}{q}") for q in range(DEEP)] for n in ("xe_in", "y_out"))
        route, plan, gap_exp, rank_mm, total_mm, const_r = (
            sem(n) for n in ("route", "plan", "gap_exp", "rank_mm", "total_mm", "const_r"))
        xeT_mm, xeT_r, row_r, h_mm, sg_r, hid_r, hidT_mm, hidT_r, y_mm, ye_r = (
            sem(n) for n in ("xeT_mm", "xeT_r", "row_r", "h_mm", "sg_r", "hid_r", "hidT_mm", "hidT_r", "y_mm",
                             "ye_r"))
        carried = sem("carried")
        sum1, sum2, sum_p, spare_r = (sem(n) for n in ("sum1", "sum2", "sum_p", "spare_r"))

        per_batch = {1: [pj_mm, ea_mm, ea_r, ms_mm, ms_r, rms_r],
                     2: [xdd_r, dt_s, g_mm, gm_r, fd_mm, sk_r, nb_r, xdt_r, nbs_r, ya_r, yg_r, sq_r],
                     4: [tm_mm, tm_r, stp_r, acc_r],
                     7: [dt_v],
                     6: [st_mm, st_r, yo_r],
                     8: [cv_mm, cv_r, seg_mm, dec_r, m_r, yd_mm, yt_r, sh_mm],
                     16: [seg_r]}

        block = ctx.enter_context(nc.Block())

        loads_a = [(cst[:], consts), (wg[:], w_gates), (bg[:], b_gates), (kraw, w_fp8), (b8[:], b_fp8),
                   (scales[:, 0:1], s_in.partition_broadcast(P)), (scales[:, 1:2], s_w.partition_broadcast(P))]
        loads_b = [(w_in[:, 0:INNER + CONV + 2 * HEADS], w_inT), (taps, conv_w.partition_broadcast(P)), (cb[:], conv_b),
                   (dtb[:, 0:HEADS], dt_bias.partition_broadcast(P)), (dtb[:, HEADS:], dt_bias.partition_broadcast(P)),
                   (a_neg[:, 0:HEADS], a_log.partition_broadcast(P)), (a_neg[:, HEADS:], a_log.partition_broadcast(P)),
                   (dcol[:], d_skip), (wfd[:], w_fd), (nw[:], norm_w), (wout[:], w_outT),
                   (w_in[:, INNER + CONV + 2 * HEADS:], gate_w)]

        @block.sync
        def _(sp):
            def store(b):
                if b in POOL_SUMS:
                    sp.wait_ge(sum_p, 4 * (POOL_SUMS.index(b) + 1))
                else:
                    sp.wait_ge(sum2, NT * (sum(q not in POOL_SUMS for q in range(b)) + 1))
                sp.dma_start(out[b].rearrange("(t p) d -> p t d", p=P),
                             x_all[:, NT * b:NT * b + NT, :]).then_inc(out_st, 16)

            def load_x(b, done):
                sp.dma_start(x_all[:, NT * b:NT * b + NT, :], x[b].rearrange("(t p) d -> p t d", p=P)).then_inc(done, 16)

            load_x(0, ld_x0)
            for dst, src in loads_a:
                sp.dma_start(dst, src).then_inc(ld_a, 16)
            for dst, src in loads_b:
                sp.dma_start(dst, src).then_inc(ld_b, 16)
            for b in range(1, B):
                load_x(b, ld_x)
            sp.wait_ge(taps_r, 3)
            sp.dma_start(ws1[:], w13).then_inc(ld_w, 16)
            sp.dma_start(ws2[:], w2).then_inc(ld_w, 16)
            sp.wait_ge(spare_r, 1)
            sp.dma_start(spare[:, D:D + 1], spare_ids).then_inc(ld_t, 16)
            sp.dma_start(xr[:, :, D:], token_ids).then_inc(ld_t, 16)
            sp.dma_start(iota[:], iotas).then_inc(ld_t, 16)
            sp.wait_ge(ld_t, 48)
            slot_tiles = slots_d.rearrange("(t p) w -> t p w", p=P)
            sp.dma_start(slot_tiles[IDLE], spare[:]).then_inc(idle_st, 16)
            sp.wait_ge(idle_st, 16)
            sp.wait_ge(plan, PLANNED)
            sp.wait_ge(scattered, 16 * NT * TOP * B)
            sp.wait_ge(padded, 16 * E)
            sp.wait_ge(yd_mm, 8 * (B + 1))

            def load_group(first, free):
                at = nc.values_load_multi_w_load_instructions(
                    tile_d[0:1, bass.ds(first, DEEP)], engines=[mybir.EngineType.SP], min_val=0, max_val=IDLE,
                    skip_runtime_bounds_check_because="it is cut off at IDLE, and no expert has more than its region")[1]
                for n in range(DEEP):
                    if free:
                        sp.wait_ge(xeT_mm, first + n - DEEP + 1)
                        sp.wait_ge(row_r, first + n - DEEP + 1)
                    sp.dma_start(xe[:, n, :],
                                 slot_tiles[bass.ds(at[n], 1)].rearrange("a p w -> p (a w)")).then_inc(xe_in[n], 16)

            load_group(0, False)
            with sp.Fori(1, SLOT_TILES // DEEP) as group:
                load_group(group * DEEP, True)
            for one in y_out:
                sp.wait_ge(one, 16 * (SLOT_TILES // DEEP))
            by_token = pairs_d[0:B * S * TOP].rearrange("(g t p k) d -> g p t k d", p=P, k=TOP, t=NT)
            for b in range(B):
                sp.dma_start(pair[b], by_token[b]).then_inc(pair_in[b], 16)
            for b in range(B):
                store(b)
            sp.wait_ge(out_st, 16 * B)

        @block.tensor
        def _(pe):
            def l0_transpose(b):
                pe.wait_ge(xn_r, 4 * b + 4)
                if not (isinstance(b, int) and b == 0):
                    pe.wait_ge(uh_r, b)
                for j in range(NT):
                    mm = nc.tensor.transpose(l0a_ps[:, j * P:(j + 1) * P], xn[:, j, :], ident)
                mm.then_inc(tr1, 1)

            def l0_gates(b, g):
                pe.wait_ge(xnT_r, b + 1)
                ps = (l0b_ps, l0a_ps, l0b_ps)[g]
                if g == 0 and not (isinstance(b, int) and b == 0):
                    pe.wait_ge(route, ROUTED * (b - 1) + RANKED)
                if g == 2:
                    pe.wait_ge(pre_r, 3 * b + 1)
                nc.tensor.matmul(ps[:], wg[:, g, :], xnT[:], start=True, stop=True).then_inc(pre_mm, 1)

            def l0_ffn(b):
                pe.wait_ge(pre_r, 3 * b + 2)
                pe.wait_ge(q_p, 2 * b + 2)
                if isinstance(b, int) and b == 0:
                    pe.wait_ge(prep_p, 5)
                nc.tensor.matmul(l0a_ps[:], kq[:], xq[:], start=True, stop=True).then_inc(ffn_mm, 1)

            def l0_back(b):
                pe.wait_ge(pre_r, 3 * b + 3)
                pe.wait_ge(h_r, b + 1)
                pe.wait_ge(yb_r, b + 1)
                if isinstance(b, int) and b == 0:
                    pe.wait_ge(prep_m, 1)
                for j in range(NT):
                    cols = slice(j * P, (j + 1) * P)
                    nc.tensor.matmul(l0b_ps[:, cols], hT[:, cols], ident, start=True, stop=False)
                    mm = nc.tensor.matmul(l0b_ps[:, cols], y16b[:, cols], ident16[:], start=False, stop=True)
                mm.then_inc(trh, 1)

            def l0_u(b):
                pe.wait_ge(y_r, b + 1)
                pe.wait_ge(xn2_r, 4 * b + 4)
                for j in range(NT):
                    mm = nc.tensor.transpose(l0a_ps[:, j * P:(j + 1) * P], xr[:, j, 0:D], ident)
                mm.then_inc(tr2, 1)

            def l0_logits(b):
                if isinstance(b, int) and b == 0:
                    pe.wait_ge(ld_b, 16 * len(loads_b))
                pe.wait_ge(uT_r, b + 1)
                pe.wait_ge(x1_r, b + 1)
                for j in range(NT):
                    mm = nc.tensor.matmul(l0b_ps[:, j * SMALL:(j + 1) * SMALL], uT[:, 3 + j * P:3 + (j + 1) * P],
                                          w_in[:, INNER + CONV:], start=True, stop=True)
                mm.then_inc(lg_mm, 1)

            def mx_conv(b, n):
                if n >= 2:
                    pe.wait_ge(cv_r, 8 * b + n - 1)
                else:
                    pe.wait_ge(ya_r, 2 * b - 1 + n)
                ps = conv_ps[n % 2]
                if n == 0:
                    pe.wait_ge(uh_r, b)
                if n < 6:
                    cols = slice(CONV_ORDER[n] * P, (CONV_ORDER[n] + 1) * P)
                    hi, lo = ([w[:, k, cols] for k in range(TAPS)] for w in (wc_hi, wc_lo))
                    first = 0
                else:
                    cols = slice((n - 6) * P, (n - 5) * P)
                    hi, lo = [wz_hi[:, cols]], [wz_lo[:, cols]]
                    first = TAPS - 1
                for part, (w, u) in enumerate(((hi, uT_hi), (lo, uT_hi), (hi, uT_lo))):
                    if part == 2 and n == 0:
                        pe.wait_ge(ul_r, b)
                    for k, one in enumerate(w):
                        mm = nc.tensor.matmul(ps[:], one, u[:, first + k:first + k + S],
                                              start=(part == 0 and k == 0), stop=(part == 2 and k == len(w) - 1))
                mm.then_inc(cv_mm, 1)

            def mx_timemajor(b, n):
                pe.wait_ge(cv_r, 8 * b + 4)
                pe.wait_ge(*((ms_r, b), (acc_r, 4 * b), (sk_r, 2 * b + 1), (sk_r, 2 * b + 2))[n])
                for q in range(4):
                    if n < 2:
                        c = 2 * n + q // 2
                        src = xs[:, q % 2, 1 + c * P:1 + (c + 1) * P]
                    else:
                        src = bc[:, 2 * (n - 2), q * P:(q + 1) * P]
                    mm = nc.tensor.transpose(tm_ps[n][:, q * P:(q + 1) * P], src, ident)
                mm.then_inc(tm_mm, 1)

            def mx_gram(b, d):
                pe.wait_ge(cv_r, 8 * b + 6)
                pe.wait_ge(tm_r, 4 * b + 3 + d)
                ps = (bank[3], bank[4])[d]
                for c in range(NT):
                    mm = nc.tensor.matmul(ps[:, c * P:(c + 1) * P], bc[:, 2 * d, c * P:(c + 1) * P],
                                          bc[:, 2 * d + 1, c * P:(c + 1) * P], start=True, stop=True)
                mm.then_inc(g_mm, 1)

            def mx_sums(b):
                pe.wait_ge(dt_v, 7 * b + 5)
                pe.wait_ge(st_r, 6 * b)
                for n, mask in enumerate((UPTO, FROM, ONES, ONES, AFTER, BEFORE)):
                    d = n % 2
                    mm = nc.tensor.matmul(state_ps[:, n * 16:(n + 1) * 16], cst[:, mask, :],
                                          adt[:, :, d * HEADS:(d + 1) * HEADS], start=True, stop=True)
                mm.then_inc(ea_mm, 1)

            def mx_skip(b, ct):
                pe.wait_ge(yt_r, 8 * b - 1 + ct)
                if ct == 0:
                    pe.wait_ge(cv_r, 8 * b + 2)
                for k in range(CT):
                    mm = nc.tensor.matmul((bank[3], bank[4])[ct][:], wfd[:, k, ct * P:(ct + 1) * P], xs[:, k, 1:S + 1],
                                          start=(k == 0), stop=(k == CT - 1))
                mm.then_inc(fd_mm, 1)

            def mx_clear(b, ct):
                pe.wait_ge(cv_r, 8 * b + 7 + ct)
                nc.tensor.matmul(conv_ps[ct][:], zero16[:, 0:P], zero16[:], start=True, stop=False, skip_group_check=True)

            def mx_segments(b, u):
                d = unit(u)[0]
                pe.wait_ge(seg_r, 16 * b + 2 * u + 2)
                if u == 0:
                    pe.wait_ge(tm_r, 4 * b + 2)
                else:
                    pe.wait_ge(dec_r, 8 * b + u)
                for part in range(2):
                    mm = nc.tensor.matmul(seg_ps[:], masks[:, d, :], seg[:, u % 2, part, :, :],
                                          start=(part == 0), stop=(part == 1))
                mm.then_inc(seg_mm, 1)

            def mx_output(b, u):
                d, c, k = unit(u)
                ps = y_ps[u % 2]
                if u == 0:
                    pe.wait_ge(gm_r, 2 * b + 2)
                    pe.wait_ge(ea_r, b + 1)
                if u >= 2:
                    pe.wait_ge(yt_r, 8 * b + u - 1)
                if k > 0:
                    pe.wait_ge(st_r, 6 * b + 2 * (k - 1) + d + 1)
                    nc.tensor.matmul(ps[:, 0:INNER], bc[:, 2 * d + 1, c * P:(c + 1) * P], state[:, d, :],
                                     start=True, stop=True)
                pe.wait_ge(m_r, 8 * b + u + 1)
                for h in range(HEADS):
                    mm = nc.tensor.matmul(ps[:, INNER + h * HDIM:INNER + (h + 1) * HDIM], mm_[:, u % 2, h, :],
                                          xdt[:, d, c, h * HDIM:(h + 1) * HDIM], start=True, stop=True)
                mm.then_inc(yd_mm, 1)

            def mx_state(b, u):
                d, c, k = unit(u)
                pe.wait_ge(xdd_r, 2 * b + d + 1)
                if u >= 1:
                    pe.wait_ge(st_r, 6 * b + u)
                nc.tensor.matmul(state_ps[:, (u % 2) * INNER:(u % 2 + 1) * INNER],
                                 btm[:, d, c, :], xdd[:, d, c - d, :],
                                 start=True, stop=True).then_inc(st_mm, 1)

            def mx_shift(b, u):
                d, c, _ = unit(u)
                pe.wait_ge(yt_r, 8 * b + u + 1)
                lo = c * P + (1 if d == 0 else -1)
                first, last = max(lo, 0), min(lo + P, S)
                for ct in range(CT):
                    mm = nc.tensor.matmul(conv_ps[ct][:, first:last], yt[:, u % 2, ct * P:(ct + 1) * P],
                                          cst[:, IDENT, first - lo:last - lo], start=False, stop=(u == STEPS - 1),
                                          skip_group_check=True)
                mm.then_inc(sh_mm, 1)

            def mx_project(b, nxt):
                if nxt is not None:
                    pe.wait_ge(ea_r, b + 2)
                pe.wait_ge(sq_r, 2 * b + 2)
                pe.wait_ge(st_r, 6 * b + 6)
                for j in range(NT):
                    for ct in range(CT):
                        mm = nc.tensor.matmul(state_ps[:, j:j + 1], skip[:, ct, j * P:(j + 1) * P], cst[:, ONES, 0:1],
                                              start=(ct == 0), stop=(ct == CT - 1))
                mm.then_inc(ms_mm, 1)
                pe.wait_ge(dec_r, 8 * b + 8)
                for j in range(NT):
                    for ct in range(CT):
                        mm = nc.tensor.matmul(seg_ps[:, j * P:(j + 1) * P], yg[:, ct, j * P:(j + 1) * P], wout[:, ct, :],
                                              start=(ct == 0), stop=(ct == CT - 1))
                mm.then_inc(pj_mm, 1)

            def mixer(b, nxt):
                def l0(f, *a):
                    if nxt is not None:
                        f(nxt, *a)
                for n in range(2, 8):
                    mx_conv(b, n)
                    if n == 2:
                        mx_skip(b, 0)
                    if n == 3:
                        l0(l0_transpose)
                        mx_skip(b, 1)
                        route_ranks(b)
                    if n in (4, 5, 6):
                        l0(l0_gates, n - 4)
                    if n == 4:
                        mx_timemajor(b, 0)
                        mx_timemajor(b, 1)
                        if nxt is None:
                            route_totals()
                    if n == 6:
                        mx_timemajor(b, 2)
                        mx_timemajor(b, 3)
                mx_segments(b, 0)
                mx_gram(b, 0)
                mx_gram(b, 1)
                mx_clear(b, 0)
                mx_clear(b, 1)
                for u in range(STEPS):
                    if u + 1 < STEPS:
                        mx_segments(b, u + 1)
                    if u == 7:
                        l0(l0_u)
                    mx_output(b, u)
                    if u < STEPS - 2:
                        mx_state(b, u)
                    if u == 4:
                        l0(l0_back)
                    if u >= 1:
                        mx_shift(b, u - 1)
                    if u == 0:
                        l0(l0_ffn)
                mx_shift(b, STEPS - 1)
                if nxt is not None:
                    l0_logits(nxt)
                    mx_head(b + 1)
                mx_project(b, nxt)

            def mx_head(b):
                mx_conv(b, 0)
                mx_sums(b)
                mx_conv(b, 1)

            def layer0(b):
                l0_transpose(b)
                for g in range(3):
                    l0_gates(b, g)
                l0_ffn(b)
                l0_back(b)
                l0_u(b)
                l0_logits(b)

            def route_ranks(b):
                pe.wait_ge(route, ROUTED * (b - 1) + PICKED)
                pe.wait_ge(lg_r, b)
                pe.wait_ge(dt_v, 7 * b + 1)
                nc.tensor.matmul(l0b_ps[:, 0:NT * E], cst[:, BEFORE, :], both[:].rearrange("p t e -> p (t e)"),
                                 start=True, stop=False, skip_group_check=True)
                for q in range(1, NT):
                    nc.tensor.matmul(l0b_ps[:, q * E:NT * E], ones, both[:, 0:NT - q, :].rearrange("p t e -> p (t e)"),
                                     start=False, stop=False, skip_group_check=True)
                nc.tensor.matmul(l0b_ps[:, 0:NT * E], ones, cum[:].unsqueeze(1).to_broadcast([P, NT, E]),
                                 start=False, stop=True, skip_group_check=True).then_inc(rank_mm, 1)

            def route_totals():
                pe.wait_ge(route, ROUTED * B)
                nc.tensor.matmul(l0b_ps[:, 0:E], ones, cum[:], start=True, stop=True).then_inc(total_mm, 1)

            def ex_transpose(i, n, first):
                pe.wait_ge(xe_in[n], (i - n) // DEEP * 16 + 16)
                if not first:
                    pe.wait_ge(xeT_r, i - 1)
                nc.tensor.transpose(bank[n % 2][:, 0:P], xe[:, n, 0:D], ident).then_inc(xeT_mm, 1)

            def tile_experts(first, count=DEEP + 8):
                return nc.values_load_multi_w_load_instructions(
                    tile_e[0:1, bass.ds(first, count)], engines=[mybir.EngineType.PE], min_val=0, max_val=E - 1,
                    skip_runtime_bounds_check_because="it counts the experts that have begun, of E, less one; 0 has")[1]

            def ex_hidden(i, n, first, e):
                pe.wait_ge(xeT_r, i + 1)
                if not first:
                    pe.wait_ge(hid_r, i - 1)
                nc.tensor.matmul(bank[2 + n % 2][:], xeT[:, n % 2, :],
                                 ws1[:, bass.ds(e, 1), :].rearrange("p a f -> p (a f)"),
                                 start=True, stop=True).then_inc(h_mm, 1)

            def ex_hiddenT(i, n, first):
                pe.wait_ge(hid_r, i + 1)
                if not first:
                    pe.wait_ge(hidT_r, i - 1)
                for f in range(CT):
                    mm = nc.tensor.transpose(bank[4 + n % 2][:, f * P:(f + 1) * P], hid[:, n % 2, f * P:(f + 1) * P], ident)
                mm.then_inc(hidT_mm, 1)

            def ex_out(i, n, first, e):
                pe.wait_ge(hidT_r, i + 1)
                if not first:
                    pe.wait_ge(ye_r, i - 1)
                for f in range(CT):
                    mm = nc.tensor.matmul(bank[6 + n % 2][:, 0:D], hidT[:, n % 2, f * P:(f + 1) * P],
                                          ws2[:, bass.ds(e, 1), f, :].rearrange("p a d -> p (a d)"),
                                          start=(f == 0), stop=(f == CT - 1))
                mm.then_inc(y_mm, 1)

            def ex_step(i, n, e_hidden, e_out):
                known = isinstance(i, int)
                if not known or i + 1 < SLOT_TILES:
                    ex_transpose(i + 1, (n + 1) % DEEP, known and i < 1)
                if not known or 0 <= i - 2 < SLOT_TILES:
                    ex_hiddenT(i - 2, (n - 2) % DEEP, known and i - 2 < 2)
                if not known or i - 3 >= 0:
                    ex_out(i - 3, (n - 3) % DEEP, known and i - 3 < 2, e_out)
                if not known or i < SLOT_TILES:
                    ex_hidden(i, n, known and i < 2, e_hidden)

            def experts():
                pe.wait_ge(yg_r, 2 * (B + 1))
                pe.wait_ge(plan, PLANNED)
                e = tile_experts(0)
                ex_transpose(0, 0, True)
                pe.wait_ge(acc_r, NT * (B + 1))
                pe.wait_ge(ms_r, B + 1)
                pe.wait_ge(ld_w, 32)
                for i in range(DEEP + 1):
                    ex_step(i, i % DEEP, e[i], e[i - 3] if i >= 3 else None)
                with pe.Fori(1, EX_LAST // DEEP) as group:
                    e = tile_experts(group * DEEP - 4)
                    for n in range(1, DEEP + 1):
                        ex_step(group * DEEP + n, n % DEEP, e[4 + n], e[4 + n - 3])
                e = tile_experts(EX_LAST - 4, SLOT_TILES - EX_LAST + 4)
                for i in range(EX_LAST + 1, SLOT_TILES + 3):
                    at = i - EX_LAST + 4
                    ex_step(i, i % DEEP, e[at] if i < SLOT_TILES else None, e[at - 3])

            pe.wait_ge(ld_a, 16 * len(loads_a))
            layer0(0)
            pe.wait_ge(prep_m, 7)
            pe.wait_ge(taps_r, 3)
            mx_head(1)
            with pe.Fori(1, B) as b:
                mixer(b, b)
            mixer(B, None)
            experts()

        @block.vector
        def _(v):
            def norm_stats(b, half):
                if half == 1:
                    v.wait_ge(x1_r, b + 1)
                    v.memset(carrier[:], 0.0)
                for j in range(NT):
                    v.bn_stats(st[:, j, :], x_all[:, bass.ds(b * NT + j, 1), :]).then_inc(bst, 1)
                if half == 1 or not (isinstance(b, int) and b == 0):
                    v.wait_ge(rs, 2 * b + half)
                v.wait_ge(bst, 8 * b + 4 * half + 4)
                v.memset(carrier[:], 0.0)
                for j in range(NT):
                    v.bn_aggr(mv[:, j, :], st[:, j, :]).then_inc(bag, 1)

            def norm_apply(b, half):
                v.wait_ge(rs, 2 * b + half + 1)
                if not (isinstance(b, int) and b == 0):
                    if half == 1:
                        v.wait_ge(tr2, b)
                        v.wait_ge(scattered, 16 * NT * TOP * b)
                    else:
                        v.wait_ge(tr1, b)
                for j in range(NT):
                    row = x_all[:, bass.ds(b * NT + j, 1), :].rearrange("p a d -> p (a d)")
                    v.tensor_scalar(xn[:, j, :] if half == 0 else xr[:, j, 0:D], row, mv[:, j, 0:1], rstd[:, j:j + 1],
                                    ALU.subtract, ALU.mult).then_inc((xn_r, xn2_r)[half], 1)

            def l0_clamps(b):
                v.wait_ge(pre_r, 3 * b + 2)
                v.tensor_scalar(cl[:, 0:2, :], pre[:, 0:2, :], CLAMP, None, ALU.min).then_inc(cl_r, 1)
                v.wait_ge(pre_r, 3 * b + 3)
                v.tensor_scalar(cl[:, 2, :], pre[:, 2, :], 0.0, None, ALU.min).then_inc(cl_r, 1)

            def l0_quantise(b):
                v.wait_ge(xnT_r, b + 1)
                if not (isinstance(b, int) and b == 0):
                    v.wait_ge(q_p, 2 * b)
                v.tensor_copy(xq16[:], xnT[:]).then_inc(q_v, 1)
                v.wait_ge(q_v, 5 * b + 1)
                v.tensor_scalar(xqs[:], xq16[:], inv_hi[:, 0:1], None, ALU.mult).then_inc(q_v, 1)
                v.wait_ge(q_v, 5 * b + 2)
                v.scalar_tensor_tensor(xqs[:], xq16[:], inv_lo[:, 0:1], xqs[:], ALU.mult, ALU.add).then_inc(q_v, 1)
                v.wait_ge(q_v, 5 * b + 3)
                v.tensor_scalar(magic[:].bitcast(U32), xqs[:].bitcast(U32), 0x7F800000, None,
                                ALU.bitwise_and).then_inc(q_v, 1)
                v.wait_ge(q_v, 5 * b + 4)
                v.tensor_scalar(magic[:], magic[:], FP8_MIN, FP8_MAGIC, ALU.max, ALU.mult).then_inc(q_v, 1)

            def l0_softplus(b):
                v.wait_ge(ln_r, b + 1)
                v.tensor_tensor(ex[:, 0:2, :], pre[:, 0:2, :], ex[:, 0:2, :], ALU.max).then_inc(sp_r, 1)
                v.wait_ge(sp_r, b + 1)
                v.tensor_tensor(diff[:], ex[:, 0, :], ex[:, 1, :], ALU.subtract).then_inc(df_r, 1)
                v.wait_ge(df_r, b + 1)
                v.tensor_scalar(cld[:], diff[:], CLAMP, None, ALU.min).then_inc(cd_r, 1)

            def l0_gatelogs(b):
                v.wait_ge(ld_r, b + 1)
                v.tensor_tensor(lgt[:, 0, :], diff[:], cld[:], ALU.max).then_inc(spd_r, 1)
                v.wait_ge(spd_r, b + 1)
                v.tensor_tensor(lgt[:, 1, :], lgt[:, 0, :], diff[:], ALU.subtract).then_inc(li_r, 1)

            def l0_recur(b):
                v.wait_ge(gt_r, b + 1)
                v.scalar_tensor_tensor(val[:], pre[:, 2, :], 0.0, lgt[:, 2, :], ALU.max, ALU.add).then_inc(g_r, 1)
                v.wait_ge(g_r, b + 1)
                v.tensor_tensor(val[:], val[:], lgt[:, 1, :], ALU.mult).then_inc(v_r, 1)
                v.wait_ge(v_r, b + 1)
                v.tensor_tensor_scan(hT[:], lgt[:, 0, :], val[:], 1.0, ALU.mult, ALU.add).then_inc(h_r, 1)
                v.wait_ge(y_r, b + 1)
                v.tensor_scalar(y16b[:], y16[:], b8[:, 0:1], None, ALU.add).then_inc(yb_r, 1)

            def l0_residual(b):
                v.wait_ge(trh, b + 1)
                rows = x_all[:, bass.ds(b * NT, NT), :]
                v.tensor_tensor(rows, rows, l0b_ps[:].rearrange("p (t d) -> p t d", t=NT), ALU.add).then_inc(x1_r, 1)

            def l0_rest(b):
                v.wait_ge(uT_r, b + 1)
                v.wait_ge(uh_r, b + 1)
                if not (isinstance(b, int) and b == 0):
                    v.wait_ge(cv_mm, 8 * b + 8)
                v.tensor_tensor(uT_lo[:, TAPS - 1:TAPS - 1 + S], uT[:, TAPS - 1:],
                                uT_hi[:, TAPS - 1:TAPS - 1 + S].bitcast(F32), ALU.subtract).then_inc(ul_r, 1)

            def l0_logits(b):
                v.wait_ge(lg_mm, b + 1)
                v.tensor_copy(logits[:, bass.ds(b * NT, NT), :],
                              l0b_ps[:, 0:NT * SMALL].rearrange("p (t e) -> p t e", t=NT)[:, :, 2 * HEADS:]
                              ).then_inc(lg_r, 1)

            def mx_dt(b):
                v.wait_ge(lg_mm, b)
                v.tensor_tensor(dtr[:], l0b_ps[:, 0:NT * SMALL].rearrange("p (t e) -> p t e", t=NT)[:, :, 0:2 * HEADS],
                                dtb[:].unsqueeze(1).to_broadcast([P, NT, 8]), ALU.add).then_inc(dt_v, 1)
                v.wait_ge(dt_v, 7 * b + 1)
                v.tensor_scalar(dtc[:], dtr[:], CLAMP, None, ALU.min).then_inc(dt_v, 1)
                v.wait_ge(dt_s, 2 * b + 2)
                v.tensor_tensor(dt[:], dtr[:], dtc[:], ALU.max).then_inc(dt_v, 2)
                v.wait_ge(dt_v, 7 * b + 4)
                v.tensor_tensor(adt[:], dt[:], a_neg[:].unsqueeze(1).to_broadcast([P, NT, 8]), ALU.mult).then_inc(dt_v, 1)
                v.wait_ge(dt_v, 7 * b + 5)
                v.tensor_copy(adt_hi[:], adt[:]).then_inc(dt_v, 1)
                v.wait_ge(dt_v, 7 * b + 6)
                v.tensor_tensor(adt_lo[:], adt[:], adt_hi[:].bitcast(F32), ALU.subtract).then_inc(dt_v, 1)

            def mx_inputs(b, d):
                v.wait_ge(tm_r, 4 * b + 2)
                v.wait_ge(dt_v, 7 * b + 5)
                v.tensor_tensor(xdt[:, d, :, :].rearrange("p c (h q) -> p c h q", h=HEADS),
                                xtm[:].rearrange("p c (h q) -> p c h q", h=HEADS),
                                dt[:, :, d * HEADS:(d + 1) * HEADS].unsqueeze(3).to_broadcast([P, NT, HEADS, HDIM]),
                                ALU.mult).then_inc(xdt_r, 1)

            def mx_mask(b, d):
                v.wait_ge(g_mm, 2 * b + d + 1)
                v.tensor_tensor(gm[:, d, :, :], (bank[3], bank[4])[d][:].rearrange("p (c l) -> p c l", c=NT),
                                cst[:, (UPTO, FROM)[d], :].unsqueeze(1).to_broadcast([P, NT, P]),
                                ALU.mult).then_inc(gm_r, 1)

            def mx_skip(b, ct):
                v.wait_ge(fd_mm, 2 * b + ct + 1)
                v.scalar_tensor_tensor(skip[:, ct, :], (bank[3], bank[4])[ct][:], dcol[:, ct:ct + 1],
                                       xs[:, ct, 1:S + 1], ALU.add, ALU.mult).then_inc(sk_r, 1)

            def mx_decay(b, u):
                d, c, k = unit(u)
                v.wait_ge(dec_r, 8 * b + u + 1)
                v.wait_ge(gm_r, 2 * b + 2)
                v.tensor_tensor(mm_[:, u % 2, :, :], dec[:, u % 2, :, :],
                                gm[:, d, c, :].unsqueeze(1).to_broadcast([P, HEADS, P]), ALU.mult).then_inc(m_r, 1)

            def mx_decayed(b, d):
                v.wait_ge(ea_r, b + 1)
                v.wait_ge(xdt_r, 2 * b + d + 1)
                v.wait_ge(nbs_r, 2 * b + 2)
                v.tensor_tensor(xdd[:, d, :, :].rearrange("p c (h q) -> p c h q", h=HEADS),
                                xdt[:, d, d:d + NT - 1, :].rearrange("p c (h q) -> p c h q", h=HEADS),
                                ea[:, 4 + d, d:d + NT - 1, :].unsqueeze(3).to_broadcast([P, NT - 1, HEADS, HDIM]),
                                ALU.mult).then_inc(xdd_r, 1)

            def mx_output(b, u):
                d, c, k = unit(u)
                ps = y_ps[u % 2]
                v.wait_ge(yd_mm, 8 * b + u + 1)
                if u >= 2:
                    v.wait_ge(sh_mm, 8 * b + u - 1)
                if k == 0:
                    v.tensor_copy(yt[:, u % 2, :], ps[:, INNER:]).then_inc(yt_r, 1)
                    return
                v.wait_ge(yt_r, 8 * b + u)
                v.tensor_tensor(yo[:].rearrange("p (h q) -> p h q", h=HEADS),
                                ps[:, 0:INNER].rearrange("p (h q) -> p h q", h=HEADS),
                                ea[:, d, c, :].unsqueeze(2).to_broadcast([P, HEADS, HDIM]), ALU.mult).then_inc(yo_r, 1)
                v.wait_ge(yo_r, 6 * b + u - 1)
                v.tensor_tensor(yt[:, u % 2, :], yo[:], ps[:, INNER:], ALU.add).then_inc(yt_r, 1)

            def mx_state(b, u):
                d, c, k = unit(u)
                half = state_ps[:, (u % 2) * INNER:(u % 2 + 1) * INNER]
                if k == 0:
                    v.wait_ge(st_mm, 6 * b + u + 1)
                    v.tensor_copy(state[:, d, :], half).then_inc(st_r, 1)
                    return
                v.wait_ge(st_mm, 6 * b + u + 1)
                v.wait_ge(stp_r, 4 * b + u - 1)
                v.tensor_tensor(state[:, d, :], stt_[:, d, :], half, ALU.add).then_inc(st_r, 1)

            def mx_neighbours(b, ct):
                v.wait_ge(nb_r, 2 * b + ct + 1)
                v.wait_ge(sk_r, 2 * b + ct + 1)
                v.scalar_tensor_tensor(skip[:, ct, :], nb[:, ct, :], dcol[:, ct:ct + 1], skip[:, ct, :],
                                       ALU.mult, ALU.add).then_inc(nbs_r, 1)

            def mx_gate(b):
                v.wait_ge(nbs_r, 2 * b + 2)
                v.wait_ge(sh_mm, 8 * b + 8)
                for ct in range(CT):
                    v.tensor_tensor(skip[:, ct, :], skip[:, ct, :], conv_ps[ct][:], ALU.add).then_inc(ya_r, 1)
                for ct in range(CT):
                    v.wait_ge(ya_r, 2 * b + ct + 1)
                    v.tensor_tensor(yg[:, ct, :], skip[:, ct, :], zs[:, ct, :], ALU.mult).then_inc(yg_r, 1)

            def mx_finish(b):
                v.wait_ge(ms_mm, b + 1)
                v.tensor_scalar(ms[:], state_ps[:, 0:NT], 1.0 / INNER, EPS, ALU.mult, ALU.add).then_inc(ms_r, 1)
                v.wait_ge(rms_r, b + 1)
                v.wait_ge(pj_mm, b + 1)
                for j in range(NT):
                    row = x_all[:, bass.ds((b - 1) * NT + j, 1), :].rearrange("p a d -> p (a d)")
                    v.scalar_tensor_tensor(row, seg_ps[:, j * P:(j + 1) * P], rms[:, j:j + 1], row,
                                           ALU.mult, ALU.add).then_inc(acc_r, 1)

            def mixer(b, nxt):
                def l0(f, *a):
                    if nxt is not None:
                        f(nxt, *a)
                l0(norm_stats, 0)
                l0(norm_apply, 0)
                route_picks(b)
                mx_skip(b, 0)
                mx_skip(b, 1)
                route_slots(b)
                l0(l0_quantise)
                if nxt is None:
                    plan_padding()
                mx_inputs(b, 0)
                mx_inputs(b, 1)
                mx_neighbours(b, 0)
                mx_neighbours(b, 1)
                mx_decayed(b, 0)
                mx_decayed(b, 1)
                l0(l0_clamps)
                mx_mask(b, 0)
                mx_mask(b, 1)
                for u in range(STEPS):
                    if u == 0:
                        mx_decay(b, 0)
                    if u + 1 < STEPS:
                        mx_decay(b, u + 1)
                    mx_output(b, u)
                    if u < STEPS - 2:
                        mx_state(b, u)
                    if u == 0:
                        l0(l0_softplus)
                    if u == 1:
                        l0(l0_gatelogs)
                    if u == 2:
                        l0(l0_recur)
                    if nxt is None and u in (1, 2, 3):
                        (plan_experts, plan_bases, plan_tiles)[u - 1]()
                    if u == 4:
                        l0(l0_residual)
                        l0(norm_stats, 1)
                    if u == 5:
                        l0(norm_apply, 1)
                l0(l0_rest)
                mx_gate(b)
                if nxt is not None:
                    mx_dt(b + 1)
                    l0_logits(nxt)
                mx_finish(b)

            def over_e(x):
                return x.unsqueeze(2).to_broadcast([P, x.shape[1], E])

            def over_t(x, n):
                return x.unsqueeze(1).to_broadcast([P, n, E])

            def then(done, before, ins):
                before[0] = before[0] + 1
                ins.then_inc(done, 1)
                v.wait_ge(done, before[0])

            def route_picks(b):
                at = [ROUTED * (b - 1)]
                r0 = (b - 1) * NT
                v.wait_ge(lg_r, b)
                for k in range(TOP):
                    src = logits[:, bass.ds(r0, NT), :] if k == 0 else pos[:]
                    top = best[:, k, bass.ds(r0, NT)]
                    then(route, at, v.tensor_reduce(top, src, AX.X, ALU.max))
                    then(route, at, v.tensor_tensor(oh[:], src, over_e(top), ALU.is_equal))
                    then(route, at, v.tensor_tensor(score[:], oh[:], over_t(rev[:], NT), ALU.mult))
                    then(route, at, v.tensor_reduce(low[:, k, :], score[:], AX.X, ALU.max))
                    then(route, at, v.tensor_tensor(picks[k][:], over_t(rev[:], NT), over_e(low[:, k, :]), ALU.is_equal))
                    if k == 0:
                        then(route, at, v.tensor_scalar(score[:], picks[0][:], -3.0e38, None, ALU.mult))
                        then(route, at, v.tensor_tensor(pos[:], score[:], logits[:, bass.ds(r0, NT), :], ALU.add))
                then(route, at, v.tensor_tensor(both[:], picks[0][:], picks[1][:], ALU.add))
                then(route, at, v.tensor_reduce(picked[:], both[:].rearrange("p t e -> p e t"), AX.X, ALU.add))

            def route_slots(b):
                at = [ROUTED * (b - 1) + PICKED]
                v.wait_ge(rank_mm, b)
                then(route, at, v.tensor_tensor(cum[:], cum[:], picked[:], ALU.add))
                then(route, at, v.tensor_tensor(pos[:], l0b_ps[:, 0:NT * E].rearrange("p (t e) -> p t e", e=E),
                                                over_t(region[:], NT), ALU.add))
                for k in range(TOP):
                    then(route, at, v.tensor_tensor(score[:], picks[k][:], pos[:], ALU.mult))
                    then(route, at, v.tensor_reduce(posf[:, k, :], score[:], AX.X, ALU.add))
                then(route, at, v.tensor_copy(slot[:], posf[:]))
                then(route, at, v.tensor_scalar(xr[:, :, D], xr[:, :, D], float(TOP * S), None, ALU.add))
                then(route, at, v.tensor_copy(xr[:, :, D + 1], low[:, 0, :]))

            def plan_padding():
                at = [0]
                v.wait_ge(total_mm, 1)
                then(plan, at, v.tensor_tensor(weight[:, 1, :], best[:, 1, :], best[:, 0, :], ALU.subtract))
                then(plan, at, v.tensor_copy(count[:], l0b_ps[:, 0:E]))
                then(plan, at, v.tensor_scalar(count_i[:], count[:], float(P - 1), None, ALU.add))
                then(plan, at, v.tensor_scalar(count_i[:], count_i[:], 7, None, ALU.arith_shift_right))
                then(plan, at, v.tensor_copy(need[:], count_i[:]))
                then(plan, at, v.tensor_tensor_scan(upto_e[:], cst[:, ONES, 0:E], need[:], 0.0, ALU.mult, ALU.add))
                then(plan, at, v.tensor_tensor(base[:], upto_e[:], need[:], ALU.subtract))
                then(plan, at, v.tensor_tensor(pad_at[:], count[:], region[:], ALU.add))
                then(plan, at, v.tensor_scalar(pad_slot[:], pad_at[:], spare[:, D:D + 1], -float(B * S * TOP),
                                               ALU.add, ALU.add))
                assert at[0] == PLAN_PADS

            def plan_experts():
                at, tiles = [PLAN_PADS], iota[:]
                then(plan, at, v.tensor_tensor(begun, over_t(base[:], SLOT_TILES), over_e(tiles), ALU.is_le))
                then(plan, at, v.tensor_reduce(tile_sum, begun, AX.X, ALU.add))
                then(plan, at, v.tensor_scalar(tile_e[:], tile_sum, -1.0, None, ALU.add))
                then(plan, at, v.tensor_scalar(tile_rev[:], tile_sum, -1.0, float(E + 1), ALU.mult, ALU.add))
                assert at[0] == PLAN_EXPERTS

            def plan_bases():
                at = [PLAN_EXPERTS]
                then(plan, at, v.tensor_tensor(begun_base, begun, over_t(base[:], SLOT_TILES), ALU.mult))
                then(plan, at, v.tensor_reduce(tile_base, begun_base, AX.X, ALU.max))
                assert at[0] == PLAN_BASES

            def plan_tiles():
                at, tiles = [PLAN_BASES], iota[:]
                then(plan, at, v.tensor_tensor(tile_at, tiles, tile_base, ALU.subtract))
                then(plan, at, v.scalar_tensor_tensor(tile_at, tile_sum, float(REGION), tile_at, ALU.mult, ALU.add))
                then(plan, at, v.tensor_scalar(tile_at, tile_at, -float(REGION), None, ALU.add))
                then(plan, at, v.tensor_scalar(tile_idle, tiles, upto_e[:, E - 1:E], float(IDLE), ALU.is_ge, ALU.mult))
                then(plan, at, v.tensor_tensor(tile_at, tile_at, tile_idle, ALU.add))
                then(plan, at, v.tensor_scalar(tile_d[:], tile_at, float(IDLE), None, ALU.min))
                assert at[0] == PLANNED

            def pick_weights():
                at = [PLANNED]
                v.wait_ge(gap_exp, 1)
                then(plan, at, v.tensor_scalar(denom[:], weight[:, 1, :], 1.0, None, ALU.add))
                then(plan, at, v.reciprocal(weight[:, 0, :], denom[:]))
                then(plan, at, v.tensor_tensor(weight[:, 1, :], weight[:, 1, :], weight[:, 0, :], ALU.mult))

            def ex_product(i, n, first):
                v.wait_ge(sg_r, i + 1)
                if not first:
                    v.wait_ge(hidT_mm, i - 1)
                v.tensor_tensor(hid[:, n % 2, :], sg[:, n % 2, :], bank[2 + n % 2][:, F:], ALU.mult).then_inc(hid_r, 1)

            def ex_rows(i, n, first):
                v.wait_ge(xe_in[n], (i - n) // DEEP * 16 + 16)
                if not first:
                    v.wait_ge(y_out[n], (i - n) // DEEP * 16)
                v.scalar_tensor_tensor(to_row[:, n, :], xe[:, n, D + 1:D + 2], tile_rev[:, bass.ds(i, 1)],
                                       xe[:, n, D:D + 1], ALU.not_equal, ALU.add).then_inc(row_r, 1)

            def ex_result(i, n, first):
                v.wait_ge(y_mm, i + 1)
                if not first:
                    v.wait_ge(y_out[n], (i - n) // DEEP * 16)
                v.tensor_copy(ye[:, n, :], bank[6 + n % 2][:, 0:D]).then_inc(ye_r, 1)

            def ex_step(i, n):
                known = isinstance(i, int)
                if not known or i < SLOT_TILES:
                    ex_rows(i, n, known and i < DEEP)
                if not known or i >= 3:
                    ex_result(i - 3, (n - 3) % DEEP, known and i - 3 < DEEP)
                if not known or i < SLOT_TILES:
                    ex_product(i, n, known and i < 2)

            def experts():
                for i in range(DEEP + 3):
                    ex_step(i, i % DEEP)
                with v.Fori(1, EX_LAST // DEEP) as group:
                    for n in range(3, DEEP + 3):
                        ex_step(group * DEEP + n, n % DEEP)
                for i in range(EX_LAST + 3, SLOT_TILES + 3):
                    ex_step(i, i % DEEP)

            def combine():
                for n, b in enumerate(q for q in range(B) if q not in POOL_SUMS):
                    v.wait_ge(pair_in[b], 16)
                    for k, done in enumerate((sum1, sum2)):
                        if k == 1:
                            v.wait_ge(sum1, NT * (n + 1))
                        for j in range(NT):
                            t = b * NT + j
                            v.scalar_tensor_tensor(x_all[:, t, :], pair[b][:, j, k, :], weight[:, k, t:t + 1],
                                                   x_all[:, t, :], ALU.mult, ALU.add).then_inc(done, 1)

            def prep_fp8():
                v.wait_ge(ld_a, 16 * len(loads_a))
                v.tensor_tensor(sprod[:], scales[:, 0:1], scales[:, 1:2], ALU.mult).then_inc(prep_v, 1)
                v.tensor_scalar(bg[:, 0:2], bg[:, 0:2], -1.0, None, ALU.mult).then_inc(prep_v, 1)
                at = [2]
                v.wait_ge(prep_v, 2)
                then(prep_v, at, v.reciprocal(inv_lo[:], scales[:]))
                then(prep_v, at, v.tensor_scalar(inv_hi[:].bitcast(U32), inv_lo[:].bitcast(U32), 0xFFFFF000, None,
                                                 ALU.bitwise_and))
                then(prep_v, at, v.tensor_scalar(scale_hi[:].bitcast(U32), scales[:].bitcast(U32), 0xFFFFF000, None,
                                                 ALU.bitwise_and))
                then(prep_v, at, v.tensor_tensor(scale_lo[:], scales[:], scale_hi[:], ALU.subtract))
                then(prep_v, at, v.tensor_tensor(scale_hi[:], scale_hi[:], inv_hi[:], ALU.mult))
                then(prep_v, at, v.tensor_tensor(scale_lo[:], scale_lo[:], inv_hi[:], ALU.mult))
                then(prep_v, at, v.tensor_scalar(rest[:], scale_hi[:], -1.0, 1.0, ALU.mult, ALU.add))
                then(prep_v, at, v.tensor_tensor(rest[:], rest[:], scale_lo[:], ALU.subtract))
                then(prep_v, at, v.tensor_tensor(inv_lo[:], rest[:], inv_lo[:], ALU.mult))
                then(prep_v, at, v.tensor_scalar(xqs[:, 0:P], kraw, inv_hi[:, 1:2], None, ALU.mult))
                then(prep_v, at, v.scalar_tensor_tensor(xqs[:, 0:P], kraw, inv_lo[:, 1:2], xqs[:, 0:P], ALU.mult, ALU.add))
                then(prep_v, at, v.tensor_scalar(magic[:, 0:P].bitcast(U32), xqs[:, 0:P].bitcast(U32), 0x7F800000, None,
                                                 ALU.bitwise_and))
                then(prep_v, at, v.tensor_scalar(magic[:, 0:P], magic[:, 0:P], FP8_MIN, FP8_MAGIC, ALU.max, ALU.mult))
                assert at[0] == SCALED

            def prep_mixer():
                v.wait_ge(ld_b, 16 * len(loads_b))
                v.tensor_copy(ident16[:], ident).then_inc(prep_m, 1)
                v.tensor_copy(masks[:], cst[:, AFTER:BEFORE + 1, :]).then_inc(prep_m, 1)
                v.tensor_copy(wz_hi[:], w_in[:, 0:INNER]).then_inc(prep_m, 1)
                for ct in range(CT):
                    v.tensor_scalar(wout[:, ct, :], wout[:, ct, :], nw[:, ct:ct + 1], None, ALU.mult).then_inc(prep_m, 1)
                v.wait_ge(prep_s, 1)
                v.tensor_scalar(a_neg[:], a_neg[:], -1.0, None, ALU.mult).then_inc(prep_m, 1)
                v.wait_ge(prep_m, 6)
                v.tensor_tensor(wz_lo[:], w_in[:, 0:INNER], wz_hi[:].bitcast(F32), ALU.subtract).then_inc(prep_m, 1)

            v.wait_ge(ld_x0, 16)
            v.wait_ge(prep_p, 1)
            norm_stats(0, 0)
            norm_apply(0, 0)
            prep_fp8()
            l0_clamps(0)
            v.wait_ge(prep_p, 5)
            l0_quantise(0)
            l0_softplus(0)
            l0_gatelogs(0)
            prep_mixer()
            l0_recur(0)
            l0_residual(0)
            norm_stats(0, 1)
            norm_apply(0, 1)
            l0_rest(0)
            l0_logits(0)
            v.wait_ge(ld_t, 48)
            v.tensor_scalar(rev[:], iota[:, 0:E], -1.0, float(E), ALU.mult, ALU.add).then_inc(const_r, 1)
            v.tensor_scalar(region[:], iota[:, 0:E], float(REGION * P), None, ALU.mult).then_inc(const_r, 1)
            v.wait_ge(const_r, 2)
            v.wait_ge(ld_x, 16 * (B - 1))
            mx_dt(1)
            with v.Fori(1, B) as b:
                mixer(b, b)
            mixer(B, None)
            pick_weights()
            experts()
            combine()

        @block.scalar
        def _(s):
            act = nc.scalar.activation

            def l0_xnT(b):
                s.wait_ge(tr1, b + 1)
                if not (isinstance(b, int) and b == 0):
                    s.wait_ge(pre_mm, 3 * b)
                    s.wait_ge(q_v, 5 * b)
                act(xnT[:], l0a_ps[:], ACT.Copy).then_inc(xnT_r, 1)

            def l0_pre(b, g):
                s.wait_ge(pre_mm, 3 * b + g + 1)
                if g == 0 and not (isinstance(b, int) and b == 0):
                    s.wait_ge(g_r, b)
                act(pre[:, g, :], (l0b_ps, l0a_ps, l0b_ps)[g][:], ACT.Identity, bias=bg[:, g:g + 1],
                    scale=(1.0 if g == 2 else -1.0)).then_inc(pre_r, 1)

            def l0_exp1(b):
                s.wait_ge(cl_r, 2 * b + 2)
                act(ex, cl, ACT.Exp).then_inc(ex_r, 1)
                s.wait_ge(ex_r, b + 1)
                act(ex, ex, ACT.Ln, bias=1.0).then_inc(ln_r, 1)

            def l0_exp2(b):
                s.wait_ge(cd_r, b + 1)
                act(cld[:], cld[:], ACT.Exp).then_inc(ed_r, 1)
                s.wait_ge(ed_r, b + 1)
                act(cld[:], cld[:], ACT.Ln, bias=1.0).then_inc(ld_r, 1)

            def l0_exp3(b):
                s.wait_ge(li_r, b + 1)
                s.wait_ge(lh_r, b + 1)
                act(lgt, lgt, ACT.Exp, scale=-1.0).then_inc(gt_r, 1)

            def l0_y(b):
                s.wait_ge(ffn_mm, b + 1)
                if not (isinstance(b, int) and b == 0):
                    s.wait_ge(yb_r, b)
                act(y16[:], l0a_ps[:], ACT.Identity, bias=0.0, scale=sprod[:, 0:1]).then_inc(y_r, 1)

            def l0_uT(b):
                s.wait_ge(tr2, b + 1)
                if not (isinstance(b, int) and b == 0):
                    s.wait_ge(cv_mm, 8 * b + 8)
                    s.wait_ge(lg_mm, b)
                act(uT[:, TAPS - 1:], l0a_ps[:], ACT.Copy).then_inc(uT_r, 1)
                if not (isinstance(b, int) and b == 0):
                    s.wait_ge(ul_r, b)
                act(uT_hi[:, TAPS - 1:TAPS - 1 + S], l0a_ps[:], ACT.Copy).then_inc(uh_r, 1)

            def mx_dt(b):
                s.wait_ge(dt_v, 7 * b + 2)
                act(dtc[:], dtc[:], ACT.Exp).then_inc(dt_s, 1)
                s.wait_ge(dt_s, 2 * b + 1)
                act(dtc[:], dtc[:], ACT.Ln, bias=1.0).then_inc(dt_s, 1)

            def mx_conv(b, n):
                s.wait_ge(cv_mm, 8 * b + n + 1)
                if n == 0:
                    s.wait_ge(sk_r, 2 * b)
                    s.wait_ge(nb_r, 2 * b)
                if n == 2:
                    s.wait_ge(yd_mm, 8 * b)
                if n == 6:
                    s.wait_ge(yg_r, 2 * b)
                ps = conv_ps[n % 2]
                if n >= 6:
                    act(zs[:, n - 6, :], ps[:], ACT.Silu).then_inc(cv_r, 1)
                    return
                q = CONV_ORDER[n]
                dst = xs[:, q, 1:S + 1] if q < CT else bc[:, q - CT, :]
                act(dst, ps[:], ACT.Silu, bias=cb[:, q:q + 1]).then_inc(cv_r, 1)

            def mx_timemajor(b, n):
                s.wait_ge(tm_mm, 4 * b + n + 1)
                if n == 0:
                    s.wait_ge(xdt_r, 2 * b)
                dst = xtm[:, 2 * n:2 * n + 2, :] if n < 2 else btm[:, n - 2, :, :]
                act(dst.rearrange("p c n -> p (c n)"), tm_ps[n][:], ACT.Copy).then_inc(tm_r, 1)

            def mx_sums(b):
                s.wait_ge(ea_mm, b + 1)
                s.wait_ge(yo_r, 6 * b)
                s.wait_ge(stp_r, 4 * b)
                act(ea[:].rearrange("p a c h -> p (a c h)"), state_ps[:, 0:96], ACT.Exp).then_inc(ea_r, 1)

            def mx_decay(b, u):
                s.wait_ge(seg_mm, 8 * b + u + 1)
                if u >= 2:
                    s.wait_ge(m_r, 8 * b + u - 1)
                act(dec[:, u % 2, :, :].rearrange("p h l -> p (h l)"), seg_ps[:], ACT.Exp).then_inc(dec_r, 1)

            def mx_squares(b, ct):
                s.wait_ge(yg_r, 2 * b + ct + 1)
                act(skip[:, ct, :], yg[:, ct, :], ACT.Square).then_inc(sq_r, 1)

            def mixer(b, nxt):
                def l0(f, *a):
                    if nxt is not None:
                        f(nxt, *a)
                for n in range(2, 8):
                    mx_conv(b, n)
                    if n == 3:
                        l0(l0_xnT)
                    if n in (4, 5, 6):
                        l0(l0_pre, n - 4)
                    if n == 4:
                        mx_timemajor(b, 0)
                        mx_timemajor(b, 1)
                    if n == 6:
                        mx_timemajor(b, 2)
                        mx_timemajor(b, 3)
                nc.scalar.preload_act_table_set("natural_log_exp_and_others")
                if nxt is None:
                    s.wait_ge(plan, 1)
                    act(weight[:, 1, :], weight[:, 1, :], ACT.Exp).then_inc(gap_exp, 1)
                for u in range(STEPS):
                    mx_decay(b, u)
                    if u == 0:
                        l0(l0_exp1)
                    if u == 2:
                        l0(l0_exp2)
                        l0(l0_y)
                    if u == 3:
                        l0(l0_exp3)
                l0(l0_uT)
                mx_squares(b, 0)
                mx_squares(b, 1)
                if nxt is not None:
                    mx_head(b + 1)

            def mx_head(b):
                mx_dt(b)
                mx_sums(b)
                mx_conv(b, 0)
                mx_conv(b, 1)

            def ex_step(i, n):
                known = isinstance(i, int)
                if not known or i + 1 < SLOT_TILES:
                    ex_xT(i + 1, (n + 1) % DEEP, known and i + 1 < 2)
                if not known or i >= 2:
                    s.wait_ge(hidT_mm, i - 1)
                    if not known or i >= 4:
                        s.wait_ge(y_mm, i - 3)
                    act(hidT[:, n % 2, :], bank[4 + n % 2][:, 0:F], ACT.Copy).then_inc(hidT_r, 1)
                if not known or i < SLOT_TILES:
                    s.wait_ge(h_mm, i + 1)
                    if not known or i >= 2:
                        s.wait_ge(hid_r, i - 1)
                    act(sg[:, n % 2, :], bank[2 + n % 2][:, 0:F], ACT.Silu).then_inc(sg_r, 1)

            def ex_xT(i, n, first):
                s.wait_ge(xeT_mm, i + 1)
                if not first:
                    s.wait_ge(h_mm, i - 1)
                act(xeT[:, n % 2, :], bank[n % 2][:, 0:P], ACT.Copy).then_inc(xeT_r, 1)

            def experts():
                ex_xT(0, 0, True)
                for i in range(DEEP):
                    ex_step(i, i % DEEP)
                with s.Fori(1, EX_LAST // DEEP) as group:
                    for n in range(DEEP):
                        ex_step(group * DEEP + n, n)
                for i in range(EX_LAST, SLOT_TILES + 2):
                    ex_step(i, i % DEEP)

            nc.scalar.preload_act_table_set("natural_log_exp_and_others")
            s.wait_ge(prep_v, 2)
            l0_xnT(0)
            for g in range(3):
                l0_pre(0, g)
            l0_exp1(0)
            s.wait_ge(ld_b, 16 * len(loads_b))
            act(a_neg[:], a_neg[:], ACT.Exp).then_inc(prep_s, 1)
            l0_exp2(0)
            s.wait_ge(taps_r, 1)
            act(wc_hi[:, 0:TAPS // 2, :], taps[:, 0:TAPS // 2, :], ACT.Copy).then_inc(taps_hi, 1)
            l0_exp3(0)
            act(wc_hi[:, TAPS // 2:, :], taps[:, TAPS // 2:, :], ACT.Copy).then_inc(taps_hi, 1)
            l0_y(0)
            l0_uT(0)
            mx_head(1)
            with s.Fori(1, B) as b:
                mixer(b, b)
            mixer(B, None)
            experts()

        @block.gpsimd
        def _(g):
            def norm_rstd(b, half):
                g.wait_ge(bag, 8 * b + 4 * half + 4)
                g.tensor_tensor(vpe[:], mv[:, :, 1], eps[:], ALU.add).then_inc(var_e, 1)
                g.wait_ge(var_e, 2 * b + half + 1)
                g.tensor_tensor(rstd[:], vpe[:], half_neg[:], ALU.pow).then_inc(rs, 1)

            def l0_round(b):
                g.wait_ge(q_v, 5 * b + 5)
                g.tensor_tensor(xqr[:], xqs[:], magic[:], ALU.add).then_inc(q_p, 1)
                g.wait_ge(q_p, 2 * b + 1)
                if not (isinstance(b, int) and b == 0):
                    g.wait_ge(ffn_mm, b)
                g.tensor_tensor(xq[:], xqr[:], magic[:], ALU.subtract).then_inc(q_p, 1)

            def l0_candidate(b):
                g.wait_ge(ln_r, b + 1)
                if not (isinstance(b, int) and b == 0):
                    g.wait_ge(h_r, b)
                g.tensor_tensor(lgt[:, 2, :], ex[:, 2, :], cl[:, 2, :], ALU.subtract).then_inc(lh_r, 1)

            def combine():
                g.wait_ge(plan, PLANNED + 3)
                for n, b in enumerate(POOL_SUMS):
                    g.wait_ge(pair_in[b], 16)
                    rows = x_all[:, b * NT:(b + 1) * NT, :]
                    for k in range(TOP):
                        g.tensor_tensor(pair[b][:, :, k, :], pair[b][:, :, k, :],
                                        weight[:, k, b * NT:(b + 1) * NT].unsqueeze(2).to_broadcast([P, NT, D]),
                                        ALU.mult).then_inc(sum_p, 1)
                    for k in range(TOP):
                        g.wait_ge(sum_p, 4 * n + 2 + k)
                        g.tensor_tensor(rows, rows, pair[b][:, :, k, :], ALU.add).then_inc(sum_p, 1)

            def mx_segments(b, u):
                d, c, _ = unit(u)
                if u == 0:
                    g.wait_ge(dt_v, 7 * b + 7)
                if u >= 2:
                    g.wait_ge(seg_mm, 8 * b + u - 1)
                for part, steps in enumerate((adt_hi[:].bitcast(F32), adt_lo[:])):
                    g.tensor_tensor(seg[:, u % 2, part, :, :],
                                    steps[:, c, d * HEADS:(d + 1) * HEADS].unsqueeze(2).to_broadcast([P, HEADS, P]),
                                    cst[:, (UPTO, FROM)[d], :].unsqueeze(1).to_broadcast([P, HEADS, P]),
                                    ALU.mult).then_inc(seg_r, 1)

            def mx_neighbours(b, ct):
                g.wait_ge(cv_r, 8 * b + ct + 1)
                g.wait_ge(nbs_r, 2 * b)
                g.wait_ge(st_mm, 6 * b)
                g.tensor_tensor(nb[:, ct, :], xs[:, ct, 0:S], xs[:, ct, 2:S + 2], ALU.add).then_inc(nb_r, 1)

            def mx_carried(b, u):
                d, c, k = unit(u)
                g.wait_ge(ea_r, b + 1)
                g.wait_ge(st_r, 6 * b + u - 1)
                g.tensor_tensor(stt_[:, d, :].rearrange("p (h q) -> p h q", h=HEADS),
                                state[:, d, :].rearrange("p (h q) -> p h q", h=HEADS),
                                ea[:, 2 + d, c, :].unsqueeze(2).to_broadcast([P, HEADS, HDIM]), ALU.mult).then_inc(stp_r, 1)

            def mx_rms(b):
                g.wait_ge(ms_r, b + 1)
                g.tensor_tensor(rms[:], ms[:], half_neg[:], ALU.pow).then_inc(rms_r, 1)

            def mixer(b, nxt):
                def l0(f, *a):
                    if nxt is not None:
                        f(nxt, *a)
                l0(norm_rstd, 0)
                mx_neighbours(b, 0)
                mx_neighbours(b, 1)
                mx_segments(b, 0)
                mx_segments(b, 1)
                scatter(b, 0)
                l0(l0_round)
                scatter(b, 1)
                for u in range(2, STEPS):
                    if u == 3:
                        l0(l0_candidate)
                    mx_segments(b, u)
                    if 2 <= u - 1 < STEPS - 2:
                        mx_carried(b, u - 1)
                l0(norm_rstd, 1)
                if nxt is None:
                    scatter_padding()
                mx_rms(b)

            def carry(i):
                g.wait_ge(carried, i)
                g.tensor_tensor(carrier_p[:], eps[:, 0:1], eps[:, 0:1], ALU.mult).then_inc(carried, 1)

            def scatter(b, k):
                if k == 0:
                    g.wait_ge(route, ROUTED * b)
                    g.wait_ge(xn2_r, 4 * b)
                    carry(b)
                for j in range(NT):
                    g.indirect_dma_start(slots_d, bass.IndirectOffsetOnAxis(ap=slot[:, k, j:j + 1], axis=0),
                                         xr[:, j, :], None).then_inc(scattered, 16)

            def scatter_padding():
                g.wait_ge(ld_t, 48)
                g.wait_ge(plan, PLAN_PADS)
                for e in range(E):
                    g.indirect_dma_start(slots_d, bass.IndirectOffsetOnAxis(ap=pad_slot[:, e:e + 1], axis=0),
                                         spare[:], None).then_inc(padded, 16)

            def ex_scatter(i, n):
                g.wait_ge(ye_r, i + 1)
                carry(B + i + 1)
                g.indirect_dma_start(pairs_d, bass.IndirectOffsetOnAxis(ap=to_row[:, n, :], axis=0),
                                     ye[:, n, :], None, bounds_check=B * S * TOP - 1,
                                     oob_is_err=False).then_inc(y_out[n], 16)

            def experts():
                with g.Fori(0, SLOT_TILES // DEEP) as group:
                    for n in range(DEEP):
                        ex_scatter(group * DEEP + n, n)

            g.sem_inc(carried, 1)
            for per, sems in per_batch.items():
                for one in sems:
                    g.sem_inc(one, per)
            g.memset(cum[:], 0.0)
            g.memset(spare[:], 0.0).then_inc(spare_r, 1)
            g.memset(eps[:], EPS)
            g.memset(half_neg[:], -0.5).then_inc(prep_p, 1)
            g.memset(zero16[:], 0.0).then_inc(prep_p, 1)
            for u in (uT, uT_hi, uT_lo):
                g.memset(u[:, 0:TAPS - 1].bitcast(F32), 0.0)
            g.memset(xs[:, :, 0:1], 0.0)
            g.memset(xs[:, :, S + 1:S + 2], 0.0).then_inc(prep_p, 1)
            norm_rstd(0, 0)
            g.wait_ge(prep_v, SCALED)
            g.tensor_tensor(xqr[:, 0:P], xqs[:, 0:P], magic[:, 0:P], ALU.add).then_inc(prep_p, 1)
            g.wait_ge(prep_p, 4)
            g.tensor_tensor(kq[:], xqr[:, 0:P], magic[:, 0:P], ALU.subtract).then_inc(prep_p, 1)
            g.wait_ge(ld_b, 16 * len(loads_b))
            g.tensor_tensor(taps, taps, w_in[:, INNER:INNER + CONV].unsqueeze(1).to_broadcast([P, TAPS, CONV]),
                            ALU.mult).then_inc(taps_r, 1)
            l0_candidate(0)
            l0_round(0)
            for n in range(2):
                g.wait_ge(taps_hi, n + 1)
                two = slice(n * TAPS // 2, (n + 1) * TAPS // 2)
                g.tensor_tensor(wc_lo[:, two, :], taps[:, two, :], wc_hi[:, two, :].bitcast(F32),
                                ALU.subtract).then_inc(taps_r, 1)
            norm_rstd(0, 1)
            with g.Fori(1, B) as b:
                mixer(b, b)
            mixer(B, None)
            experts()
            combine()



def kernel(L0_attn_x, L0_attn_W_f, L0_attn_b_f, L0_attn_W_i, L0_attn_b_i, L0_attn_W_h, L0_attn_b_h, L0_ffn_kernel,
           L0_ffn_input_scale, L0_ffn_kernel_scale, L0_ffn_bias, L1_attn_in_proj_w, L1_attn_conv_w, L1_attn_conv_b,
           L1_attn_dt_bias, L1_attn_A_log, L1_attn_D, L1_attn_fc_D_w, L1_attn_norm_w, L1_attn_out_proj_w,
           L1_ffn_gate_w, L1_ffn_w1, L1_ffn_w2, L1_ffn_w3):
    import concourse.bacc as bacc
    from concourse.bass_utils import run_bass_kernel_spmd as run

    a = np.asarray

    def columns(w):
        return a(w).reshape(-1, P).T

    def rows(w):
        return a(w).reshape(-1, P, a(w).shape[-1]).transpose(1, 0, 2)

    ins = {
        "x": a(L0_attn_x),
        "w_gates": np.stack([a(L0_attn_W_f).T, a(L0_attn_W_i).T, a(L0_attn_W_h).T], 1),
        "b_gates": np.stack([a(L0_attn_b_f), a(L0_attn_b_i), a(L0_attn_b_h)], 1),
        "w_fp8": a(L0_ffn_kernel), "s_in": a(L0_ffn_input_scale), "s_w": a(L0_ffn_kernel_scale),
        "b_fp8": a(L0_ffn_bias).reshape(P, 1),
        "w_inT": a(L1_attn_in_proj_w).T,
        "conv_w": a(L1_attn_conv_w).reshape(-1, TAPS).T,
        "conv_b": columns(L1_attn_conv_b),
        "dt_bias": a(L1_attn_dt_bias), "a_log": a(L1_attn_A_log),
        "d_skip": columns(np.repeat(a(L1_attn_D), HDIM)),
        "w_fd": rows(np.repeat(a(L1_attn_fc_D_w), HDIM, axis=0).T),
        "norm_w": columns(L1_attn_norm_w),
        "w_outT": rows(a(L1_attn_out_proj_w).T),
        "gate_w": a(L1_ffn_gate_w),
        "w13": np.concatenate([a(L1_ffn_w1), a(L1_ffn_w3)], 2).transpose(1, 0, 2),
        "w2": a(L1_ffn_w2).reshape(E, CT, P, D).transpose(2, 0, 1, 3),
        "consts": shape_constants(),
        "token_ids": ((TOP * (np.arange(NT)[None, :] * P + np.arange(P)[:, None] - S))[:, :, None]
                      * (np.arange(PAY - D) == 0)).astype(np.float32),
        "spare_ids": (B * S * TOP + np.arange(P, dtype=np.float32)).reshape(P, 1),
        "iotas": np.broadcast_to(np.arange(SLOT_TILES, dtype=np.float32), (P, SLOT_TILES)),
    }
    ins = {k: np.ascontiguousarray(v) for k, v in ins.items()}
    nc = bacc.Bacc("TRN2", target_bir_lowering=False, num_devices=1)
    aps = {k: nc.dram_tensor(f"in_{k}", v.shape, mybir.dt.from_np(v.dtype), kind="ExternalInput").ap()
           for k, v in ins.items()}
    out = nc.dram_tensor("out", (B, S, D), F32, kind="ExternalOutput").ap()
    slots_d = nc.dram_tensor("slots", ((IDLE + 1) * P, PAY), F32, kind="Internal").ap()
    pairs_d = nc.dram_tensor("pairs", (B * S * TOP + P, D), F32, kind="Internal").ap()
    build(nc, **aps, slots_d=slots_d, pairs_d=pairs_d, out=out)
    r = run(nc, [{f"in_{k}": v for k, v in ins.items()}], core_ids=[0])
    return r.results[0]["out"]
```
